# Optimizing a Trainium2 kernel written in Bass

```python
import numpy as np
import jax
import jax.numpy as jnp

def _softmax(x, axis=-1):
    return jax.nn.softmax(x, axis=axis)
def _gelu(x):
    return jax.nn.gelu(x, approximate=True)
def _silu(x):
    return jax.nn.silu(x)
def _sigmoid(x):
    return jax.nn.sigmoid(x)
def _layernorm(x, axis=-1, eps=1e-5):
    m = jnp.mean(x, axis=axis, keepdims=True)
    v = jnp.var(x, axis=axis, keepdims=True)
    return (x - m) / jnp.sqrt(v + eps)
def _scatter_add(tgt, idx, src, axis=0):
    return tgt.at[idx].add(src)
def _segment_sum(src, seg, n):
    return jax.ops.segment_sum(src, seg, n)

kernel_name = 'mk_metaformer_d2_conv_nchw256_7f2a2e'

def setup_inputs(seed: int = 0):
    np.random.seed(seed)
    _w = jnp.asarray
    def _rec_inputs():
        import jax
        import jax.numpy as jnp
        _gk = jax.random.key(seed)
        x = -0.0009438 + 1 * jax.random.normal(jax.random.fold_in(_gk, 1), (2, 256, 48, 48), jnp.float32)
        return x
    x = _rec_inputs()
    def _L0_conv_setup():
        import jax, jax.numpy as jnp
        import numpy as np
        DIM = 256
        HEAD_DIM = 32
        HEADS = DIM // HEAD_DIM
        SCALE = HEAD_DIM ** (-0.5)
        key = jax.random.key(seed)
        ks = jax.random.split(key, 5)
        B, C, H, W = (2, DIM, 48, 48)
        x = jax.random.normal(ks[0], (B, C, H, W), jnp.float32)
        w_qkv = jax.random.normal(ks[1], (3 * C, C), jnp.float32) * C ** (-0.5)
        w_lepe = jax.random.normal(ks[2], (C, 1, 3, 3), jnp.float32) * (1.0 / 3.0)
        b_lepe = jax.random.normal(ks[3], (C,), jnp.float32) * 0.01
        w_proj = jax.random.normal(ks[4], (C, C), jnp.float32) * C ** (-0.5)
        b_proj = jnp.zeros((C,), jnp.float32)
        return {'x': x, 'w_qkv': w_qkv, 'w_lepe': w_lepe, 'b_lepe': b_lepe, 'w_proj': w_proj, 'b_proj': b_proj}
    _L0_conv_all = _L0_conv_setup()
    _L0_conv_in = {k: v for k, v in _L0_conv_all.items() if k in ('w_qkv', 'w_lepe', 'b_lepe', 'w_proj', 'b_proj', )}
    del _L0_conv_all

    def _L0_ffn_setup():
        import jax, jax.numpy as jnp
        import numpy as np
        TOP_K = 2
        LN_EPS = 1e-05
        key = jax.random.key(seed)
        ks = jax.random.split(key, 8)
        B, S, D, E, H = (16, 1024, 256, 8, 1024)
        x = jax.random.normal(ks[0], (B, S, D), dtype=jnp.float32)
        Wr = jax.random.normal(ks[1], (D, E), dtype=jnp.float32) * 0.1
        br = jnp.zeros((E,), dtype=jnp.float32)
        ln_g = jnp.ones((E, D), dtype=jnp.float32)
        ln_b = jnp.zeros((E, D), dtype=jnp.float32)
        W1 = jax.random.normal(ks[2], (E, D, H), dtype=jnp.float32) * (1.0 / np.sqrt(D))
        b1 = jnp.zeros((E, H), dtype=jnp.float32)
        W2 = jax.random.normal(ks[3], (E, H, D), dtype=jnp.float32) * (1.0 / np.sqrt(H))
        b2 = jnp.zeros((E, D), dtype=jnp.float32)
        return {'x': x, 'Wr': Wr, 'br': br, 'ln_g': ln_g, 'ln_b': ln_b, 'W1': W1, 'b1': b1, 'W2': W2, 'b2': b2}
    _L0_ffn_all = _L0_ffn_setup()
    _L0_ffn_in = {k: v for k, v in _L0_ffn_all.items() if k in ('Wr', 'br', 'ln_g', 'ln_b', 'W1', 'b1', 'W2', 'b2', )}
    del _L0_ffn_all

    def _L1_conv_setup():
        import jax, jax.numpy as jnp
        import numpy as np
        DIM = 256
        HEADS = 8
        WINDOWS = (1, 2, 4)
        B, H, W = (1, 64, 64)

        def _integral(a):
            s = jnp.cumsum(jnp.cumsum(a, axis=-2), axis=-1)
            pad = [(0, 0)] * (a.ndim - 2) + [(1, 0), (1, 0)]
            return jnp.pad(s, pad)

        def _box(P, ws, Ho, Wo):
            tp = ws - 1
            r = tp // 2
            l = tp - r
            pad = [(0, 0)] * (P.ndim - 2) + [(l, r), (l, r)]
            Pp = jnp.pad(P, pad, mode='edge')
            return Pp[..., ws:ws + Ho, ws:ws + Wo] - Pp[..., ws:ws + Ho, :Wo] - Pp[..., :Ho, ws:ws + Wo] + Pp[..., :Ho, :Wo]
        key = jax.random.key(seed)
        ks = jax.random.split(key, 6)
        x = jax.random.normal(ks[0], (B, DIM, H, W), jnp.float32)
        Wq = jax.random.normal(ks[1], (DIM, DIM), jnp.float32) * 0.05
        Wk = jax.random.normal(ks[2], (DIM, DIM), jnp.float32) * 0.05
        Wv = jax.random.normal(ks[3], (DIM, DIM), jnp.float32) * 0.05
        Wout = jax.random.normal(ks[4], (DIM, DIM * len(WINDOWS)), jnp.float32) * 0.05
        bout = jnp.zeros((DIM,), jnp.float32)
        return {'x': x, 'Wq': Wq, 'Wk': Wk, 'Wv': Wv, 'Wout': Wout, 'bout': bout}
    _L1_conv_all = _L1_conv_setup()
    _L1_conv_in = {k: v for k, v in _L1_conv_all.items() if k in ('Wq', 'Wk', 'Wv', 'Wout', 'bout', )}
    del _L1_conv_all

    def _L1_ffn_setup():
        import jax, jax.numpy as jnp
        import numpy as np
        NUM_EXPERTS = 8
        TOP_K = 2
        B, S, D = (8, 8192, 256)

        def _moe(tokens, router_w, w1, b1, w2, b2):
            N = tokens.shape[0]
            E = router_w.shape[0]
            logits = tokens.astype(jnp.float32) @ router_w.astype(jnp.float32).T
            probs = jax.nn.softmax(logits, axis=-1)
            rw, re = jax.lax.top_k(probs, TOP_K)
            if TOP_K > 1:
                rw = rw / jnp.maximum(rw.sum(-1, keepdims=True), 1e-12)
            rw = rw.astype(tokens.dtype)
            combine = jnp.zeros((N, E), tokens.dtype).at[jnp.arange(N)[:, None], re].set(rw)
            out = tokens
            for e in range(E):
                h = jax.nn.gelu(tokens @ w1[e] + b1[e], approximate=False)
                y = h @ w2[e] + b2[e]
                out = out + combine[:, e:e + 1] * y
            return out
        key = jax.random.key(seed)
        ks = jax.random.split(key, 4)
        scale = 1.0 / np.sqrt(D).astype(np.float32)
        return {'input_embeddings': jax.random.normal(ks[0], (B, S, D), jnp.float32), 'router_w': jax.random.normal(ks[1], (NUM_EXPERTS, D), jnp.float32) * scale, 'w1': jax.random.normal(ks[2], (NUM_EXPERTS, D, D), jnp.float32) * scale, 'b1': jnp.zeros((NUM_EXPERTS, D), jnp.float32), 'w2': jax.random.normal(ks[3], (NUM_EXPERTS, D, D), jnp.float32) * scale, 'b2': jnp.zeros((NUM_EXPERTS, D), jnp.float32)}
    _L1_ffn_all = _L1_ffn_setup()
    _L1_ffn_in = {k: v for k, v in _L1_ffn_all.items() if k in ('router_w', 'w1', 'b1', 'w2', 'b2', )}
    del _L1_ffn_all

    return {
        "x": x,
        "L0_conv_w_qkv": _L0_conv_in["w_qkv"],
        "L0_conv_w_lepe": _L0_conv_in["w_lepe"],
        "L0_conv_b_lepe": _L0_conv_in["b_lepe"],
        "L0_conv_w_proj": _L0_conv_in["w_proj"],
        "L0_conv_b_proj": _L0_conv_in["b_proj"],
        "L0_ffn_Wr": _L0_ffn_in["Wr"],
        "L0_ffn_br": _L0_ffn_in["br"],
        "L0_ffn_ln_g": _L0_ffn_in["ln_g"],
        "L0_ffn_ln_b": _L0_ffn_in["ln_b"],
        "L0_ffn_W1": _L0_ffn_in["W1"],
        "L0_ffn_b1": _L0_ffn_in["b1"],
        "L0_ffn_W2": _L0_ffn_in["W2"],
        "L0_ffn_b2": _L0_ffn_in["b2"],
        "L1_conv_Wq": _L1_conv_in["Wq"],
        "L1_conv_Wk": _L1_conv_in["Wk"],
        "L1_conv_Wv": _L1_conv_in["Wv"],
        "L1_conv_Wout": _L1_conv_in["Wout"],
        "L1_conv_bout": _L1_conv_in["bout"],
        "L1_ffn_router_w": _L1_ffn_in["router_w"],
        "L1_ffn_w1": _L1_ffn_in["w1"],
        "L1_ffn_b1": _L1_ffn_in["b1"],
        "L1_ffn_w2": _L1_ffn_in["w2"],
        "L1_ffn_b2": _L1_ffn_in["b2"],
    }

def reference(x, L0_conv_w_qkv, L0_conv_w_lepe, L0_conv_b_lepe, L0_conv_w_proj, L0_conv_b_proj, L0_ffn_Wr, L0_ffn_br, L0_ffn_ln_g, L0_ffn_ln_b, L0_ffn_W1, L0_ffn_b1, L0_ffn_W2, L0_ffn_b2, L1_conv_Wq, L1_conv_Wk, L1_conv_Wv, L1_conv_Wout, L1_conv_bout, L1_ffn_router_w, L1_ffn_w1, L1_ffn_b1, L1_ffn_w2, L1_ffn_b2):
    import jax
    import jax.numpy as jnp
    def _L0_conv_ref(x, w_qkv, w_lepe, b_lepe, w_proj, b_proj):
        import jax, jax.numpy as jnp
        import numpy as np
        DIM = 256
        HEAD_DIM = 32
        HEADS = DIM // HEAD_DIM
        SCALE = HEAD_DIM ** (-0.5)
        B, C, H, W = x.shape
        N = H * W
        h, d = (HEADS, HEAD_DIM)
        qkv = jnp.einsum('oc,bchw->bohw', w_qkv, x).reshape(B, h, 3 * d, N)
        q, k, v = jnp.split(qkv, 3, axis=2)
        v4 = v.reshape(B, C, H, W)
        lepe = jax.lax.conv_general_dilated(v4, w_lepe, window_strides=(1, 1), padding='SAME', dimension_numbers=('NCHW', 'OIHW', 'NCHW'), feature_group_count=C) + b_lepe[None, :, None, None]
        attn = jax.nn.softmax(jnp.einsum('bhdk,bhdq->bhkq', k, q) * SCALE, axis=-2)
        out = jnp.einsum('bhdk,bhkq->bhdq', v, attn).reshape(B, C, H, W)
        out = out + lepe
        out = jnp.einsum('oc,bchw->bohw', w_proj, out) + b_proj[None, :, None, None]
        return out

    def _L0_ffn_ref(x, Wr, br, ln_g, ln_b, W1, b1, W2, b2):
        import jax, jax.numpy as jnp
        import numpy as np
        TOP_K = 2
        LN_EPS = 1e-05
        B, S, D = x.shape
        N = B * S
        xt = x.reshape(N, D)
        logits = xt @ Wr + br
        probs = jax.nn.softmax(logits, axis=-1)
        top_p, top_idx = jax.lax.top_k(probs, TOP_K)
        weights = top_p / top_p.sum(axis=-1, keepdims=True)
        mu = xt.mean(axis=-1, keepdims=True)
        var = ((xt - mu) ** 2).mean(axis=-1, keepdims=True)
        xn = (xt - mu) * jax.lax.rsqrt(var + LN_EPS)
        xe = xn[None, :, :] * ln_g[:, None, :] + ln_b[:, None, :]
        h = jax.nn.gelu(jnp.einsum('end,edh->enh', xe, W1) + b1[:, None, :], approximate=False)
        y = jnp.einsum('enh,ehd->end', h, W2) + b2[:, None, :]
        y_tok = jnp.transpose(y, (1, 0, 2))
        sel = jnp.take_along_axis(y_tok, top_idx[:, :, None], axis=1)
        out = (weights[:, :, None] * sel).sum(axis=1)
        return out.reshape(B, S, D)

    def _L1_conv_ref(x, Wq, Wk, Wv, Wout, bout):
        import jax, jax.numpy as jnp
        import numpy as np
        DIM = 256
        HEADS = 8
        WINDOWS = (1, 2, 4)
        B, H, W = (1, 64, 64)

        def _integral(a):
            s = jnp.cumsum(jnp.cumsum(a, axis=-2), axis=-1)
            pad = [(0, 0)] * (a.ndim - 2) + [(1, 0), (1, 0)]
            return jnp.pad(s, pad)

        def _box(P, ws, Ho, Wo):
            tp = ws - 1
            r = tp // 2
            l = tp - r
            pad = [(0, 0)] * (P.ndim - 2) + [(l, r), (l, r)]
            Pp = jnp.pad(P, pad, mode='edge')
            return Pp[..., ws:ws + Ho, ws:ws + Wo] - Pp[..., ws:ws + Ho, :Wo] - Pp[..., :Ho, ws:ws + Wo] + Pp[..., :Ho, :Wo]
        b, C, Hh, Ww = x.shape
        h = HEADS
        d = C // h
        q = jnp.einsum('bchw,oc->bohw', x, Wq).reshape(b * h, d, Hh, Ww)
        k = jnp.einsum('bchw,oc->bohw', x, Wk).reshape(b * h, d, Hh, Ww)
        v = jnp.einsum('bchw,oc->bohw', x, Wv).reshape(b * h, d, Hh, Ww)
        q = jax.nn.sigmoid(q)
        k = jax.nn.sigmoid(k)
        v = v / jnp.maximum(jnp.linalg.norm(v, axis=1, keepdims=True), 1e-12)
        Ik = _integral(k)
        Ikv = _integral(jnp.einsum('bfhw,bghw->bfghw', k, v))
        outs = []
        for w in WINDOWS:
            ws = Hh // w
            wk = _box(Ik, ws, Hh, Ww)
            wkv = _box(Ikv, ws, Hh, Ww)
            attn = jnp.einsum('bdhw,bdfhw->bfhw', q, wkv)
            norm = jnp.einsum('bdhw,bdhw->bhw', q, wk)
            attn = attn / (norm[:, None] + 1e-06)
            outs.append(attn.reshape(b, C, Hh, Ww))
        o = jnp.concatenate(outs, axis=1)
        return jnp.einsum('bchw,oc->bohw', o, Wout) + bout[None, :, None, None]

    def _L1_ffn_ref(input_embeddings, router_w, w1, b1, w2, b2):
        import jax, jax.numpy as jnp
        import numpy as np
        NUM_EXPERTS = 8
        TOP_K = 2
        B, S, D = (8, 8192, 256)

        def _moe(tokens, router_w, w1, b1, w2, b2):
            N = tokens.shape[0]
            E = router_w.shape[0]
            logits = tokens.astype(jnp.float32) @ router_w.astype(jnp.float32).T
            probs = jax.nn.softmax(logits, axis=-1)
            rw, re = jax.lax.top_k(probs, TOP_K)
            if TOP_K > 1:
                rw = rw / jnp.maximum(rw.sum(-1, keepdims=True), 1e-12)
            rw = rw.astype(tokens.dtype)
            combine = jnp.zeros((N, E), tokens.dtype).at[jnp.arange(N)[:, None], re].set(rw)
            out = tokens
            for e in range(E):
                h = jax.nn.gelu(tokens @ w1[e] + b1[e], approximate=False)
                y = h @ w2[e] + b2[e]
                out = out + combine[:, e:e + 1] * y
            return out
        b, s, d = input_embeddings.shape
        tokens = input_embeddings.reshape(b * s, d)
        return _moe(tokens, router_w, w1, b1, w2, b2).reshape(b, s, d)

    def _gn(v, G=32, eps=1e-5):
        B_, C_, H_, W_ = v.shape
        g = v.reshape(B_, G, C_ // G, H_, W_)
        m = jnp.mean(g, axis=(2, 3, 4), keepdims=True)
        s = jnp.var(g, axis=(2, 3, 4), keepdims=True)
        return ((g - m) / jnp.sqrt(s + eps)).reshape(v.shape)

    def _ln_c(v, eps=1e-6):
        m = jnp.mean(v, axis=1, keepdims=True)
        s = jnp.var(v, axis=1, keepdims=True)
        return (v - m) / jnp.sqrt(s + eps)

    def _ln_t(v, eps=1e-5):
        m = jnp.mean(v, axis=-1, keepdims=True)
        s = jnp.var(v, axis=-1, keepdims=True)
        return (v - m) / jnp.sqrt(s + eps)

    def _to_tokens(v):
        B_, C_, H_, W_ = v.shape
        return v.reshape(B_, C_, H_ * W_).transpose(0, 2, 1)
    def _from_tokens(t, like):
        B_, C_, H_, W_ = like.shape
        return t.transpose(0, 2, 1).reshape(B_, C_, H_, W_)

    x = x + _L0_conv_ref(_ln_c(x), L0_conv_w_qkv, L0_conv_w_lepe, L0_conv_b_lepe, L0_conv_w_proj, L0_conv_b_proj)
    t = _to_tokens(x)
    t = t + _L0_ffn_ref(_ln_t(t), L0_ffn_Wr, L0_ffn_br, L0_ffn_ln_g, L0_ffn_ln_b, L0_ffn_W1, L0_ffn_b1, L0_ffn_W2, L0_ffn_b2)
    x = _from_tokens(t, x)
    x = x + _L1_conv_ref(_ln_c(x), L1_conv_Wq, L1_conv_Wk, L1_conv_Wv, L1_conv_Wout, L1_conv_bout)
    t = _to_tokens(x)
    t = t + _L1_ffn_ref(_ln_t(t), L1_ffn_router_w, L1_ffn_w1, L1_ffn_b1, L1_ffn_w2, L1_ffn_b2)
    x = _from_tokens(t, x)
    return x


_drawn_inputs = setup_inputs


def setup_inputs(seed=0):
    import zlib

    import numpy as np

    out = dict(_drawn_inputs(seed))
    spreads = {'L0_conv_b_proj': (0.0, 0.1),
     'L0_ffn_br': (0.0, 0.1),
     'L0_ffn_ln_g': (1.0, 0.2),
     'L0_ffn_ln_b': (0.0, 0.1),
     'L0_ffn_b1': (0.0, 0.1),
     'L0_ffn_b2': (0.0, 0.1),
     'L1_conv_bout': (0.0, 0.1),
     'L1_ffn_b1': (0.0, 0.391),
     'L1_ffn_b2': (0.0, 0.275)}
    factors = {'L1_conv_Wq': 8.0, 'L1_conv_Wk': 8.0}
    for name, (base, spread) in spreads.items():
        noise = np.random.default_rng([zlib.crc32(name.encode()), seed]).standard_normal(out[name].shape)
        drawn = base * np.exp(spread * noise) if base else spread * noise
        out[name] = jnp.asarray(drawn.astype(out[name].dtype))
    for name, factor in factors.items():
        out[name] = (out[name] * factor).astype(out[name].dtype)
    return out
```

```python
from contextlib import ExitStack

import concourse.bass as bass
from concourse import mybir

F32 = mybir.dt.float32
F16 = mybir.dt.float16
ALU = mybir.AluOpType
ACT = mybir.ActivationFunctionType
AX = mybir.AxisListType
ds = bass.ds

P = 128
B, C, HW = 2, 256, 48
N = HW * HW
T = B * N
CT = C // P
HEADS, HD = 8, 32
CH = 8 * HW
NCH = T // CH
QC = N // CH
KT = N // P
TT = T // P
SUB = CH // P
PAIRS = B * HEADS // 2
SCALE = float(HD) ** -0.5
E = 8
WINDOWS = (48, 24, 12)
PADK = 3 * HD + 1


class Core:

    def __init__(self, nc, keep):
        self.nc, self.keep, self.n, self.phase = nc, keep, 0, []

    def sem(self, name):
        self.n += 1
        self.phase.append(self.nc.alloc_semaphore(name=f"{name}_{self.n}"))
        return self.phase[-1]

    def block(self):
        with self.nc.Block() as block:
            @block.sync
            def _(sp):
                for sem in self.phase:
                    sp.sem_inc(sem, 1)
        return self.nc.Block()

    def end_phase(self):
        with self.nc.Block() as block:
            @block.sync
            def _(sp):
                for sem in self.phase:
                    sp.sem_clear(sem)
        for sem in self.phase:
            self.nc.release_semaphore(sem)
        self.phase.clear()

    def sb(self, ctx, name, shape, dt=F32):
        self.n += 1
        return ctx.enter_context(self.nc.sbuf_tensor(f"{name}_{self.n}", shape, dt))

    def ps(self, ctx, name, shape, dt=F32):
        self.n += 1
        return ctx.enter_context(self.nc.psum_tensor(f"{name}_{self.n}", shape, dt))


def copy(pool, out, src, one):
    return pool.tensor_tensor(out, src, one.unsqueeze(2).broadcast_to(list(src.shape)), ALU.mult)


def split_matmul(pe, out, w_hi, w_lo, x_hi, x_lo, first, last):
    pe.matmul(out, w_hi, x_hi, start=first, stop=False)
    pe.matmul(out, w_hi, x_lo, start=False, stop=False)
    return pe.matmul(out, w_lo, x_hi, start=False, stop=last)


def layer_norm(core, src, hi, lo, ones, eps_tile, keep32=None, add_back=False, one=None):
    nc = core.nc
    with ExitStack() as ctx:
        centred = core.sb(ctx, "centred", [P, 2, CT, CH])
        square = core.sb(ctx, "square", [P, 2, CT, CH])
        std = core.sb(ctx, "std", [P, 2, CH])
        rstd = core.sb(ctx, "rstd", [P, 2, CH])
        mean_ps = core.ps(ctx, "mean_ps", [P, 2, 512])
        var_ps = core.ps(ctx, "var_ps", [P, 2, 512])
        mean_ready, centred_ready, square_ready, var_ready, std_ready, rstd_ready, norm_ready, hi_ready, lo_ready, back_ready = (
            core.sem(n) for n in ("mean_ready", "centred_ready", "square_ready", "var_ready", "std_ready",
                                  "rstd_ready", "norm_ready", "hi_ready", "lo_ready", "back_ready"))
        block = ctx.enter_context(core.block())

        @block.tensor
        def _(pe):
            with pe.Fori(0, NCH // 2) as i:
                for b in range(2):
                    pe.wait_ge(centred_ready, 2 * i + 1)
                    for c in range(CT):
                        mm = pe.matmul(mean_ps[:, b, 0:CH], ones[:], src[:, c, ds((2 * i + b) * CH, CH)],
                                       start=c == 0, stop=c == CT - 1)
                    mm.then_inc(mean_ready, 1)
                for b in range(2):
                    pe.wait_ge(square_ready, 2 * i + b + 2)
                    pe.wait_ge(std_ready, 2 * i + 1)
                    for c in range(CT):
                        mm = pe.matmul(var_ps[:, b, 0:CH], ones[:], square[:, b, c, :],
                                       start=c == 0, stop=c == CT - 1)
                    mm.then_inc(var_ready, 1)

        @block.vector
        def _(dve):
            with dve.Fori(0, NCH // 2) as i:
                for b in range(2):
                    dve.wait_ge(mean_ready, 2 * i + b + 2)
                    dve.wait_ge(lo_ready, 2 * i + 1)
                    dve.wait_ge(hi_ready, 2 * i + 1)
                    if keep32 is not None or add_back:
                        dve.wait_ge(back_ready, 2 * i + 1)
                    dve.tensor_tensor(centred[:, b], src[:, :, ds((2 * i + b) * CH, CH)],
                                      mean_ps[:, b, 0:CH].unsqueeze(1).broadcast_to([P, CT, CH]),
                                      ALU.subtract).then_inc(centred_ready, 1)
                for b in range(2):
                    dve.wait_ge(std_ready, 2 * i + b + 2)
                    dve.reciprocal(rstd[:, b], std[:, b]).then_inc(rstd_ready, 1)
                    dve.wait_ge(rstd_ready, 2 * i + b + 2)
                    dve.wait_ge(square_ready, 2 * i + b + 2)
                    dve.tensor_tensor(centred[:, b], centred[:, b],
                                      rstd[:, b].unsqueeze(1).broadcast_to([P, CT, CH]),
                                      ALU.mult).then_inc(norm_ready, 1)

        @block.scalar
        def _(act):
            with act.Fori(0, NCH // 2) as i:
                for b in range(2):
                    act.wait_ge(centred_ready, 2 * i + b + 2)
                    act.wait_ge(var_ready, 2 * i + 1)
                    act.activation(square[:, b], centred[:, b], ACT.Square).then_inc(square_ready, 1)
                for b in range(2):
                    act.wait_ge(var_ready, 2 * i + b + 2)
                    act.wait_ge(rstd_ready, 2 * i + 1)
                    act.activation(std[:, b], var_ps[:, b, 0:CH], ACT.Sqrt, bias=eps_tile[:, 0:1]).then_inc(std_ready, 1)
                for b in range(2):
                    act.wait_ge(norm_ready, 2 * i + b + 2)
                    act.activation(hi[:, :, ds((2 * i + b) * CH, CH)], centred[:, b], ACT.Copy).then_inc(hi_ready, 1)

        @block.gpsimd
        def _(pool):
            with pool.Fori(0, NCH // 2) as i:
                for b in range(2):
                    chunk = ds((2 * i + b) * CH, CH)
                    if keep32 is not None:
                        pool.wait_ge(norm_ready, 2 * i + b + 2)
                        copy(pool, keep32[:, :, chunk], centred[:, b], one).then_inc(back_ready, 1)
                    if add_back:
                        pool.wait_ge(norm_ready, 2 * i + b + 2)
                        pool.tensor_tensor(src[:, :, chunk], src[:, :, chunk], centred[:, b],
                                           ALU.add).then_inc(back_ready, 1)
                    pool.wait_ge(hi_ready, 2 * i + b + 2)
                    pool.tensor_tensor(lo[:, :, chunk], centred[:, b], hi[:, :, chunk],
                                       ALU.subtract).then_inc(lo_ready, 1)


def split_weights(core, pairs):
    nc = core.nc
    with ExitStack() as ctx:
        stages = [core.sb(ctx, "stage", list(src.shape)) for src, _, _ in pairs]
        loaded = [core.sem("loaded") for _ in pairs]
        hi_ready, lo_ready = core.sem("w_hi_ready"), core.sem("w_lo_ready")
        block = ctx.enter_context(core.block())

        @block.sync
        def _(sp):
            for (src, _, _), stage, ready in zip(pairs, stages, loaded):
                sp.dma_start(stage[:], src).then_inc(ready, 16)

        @block.scalar
        def _(act):
            for (_, hi, _), stage, ready in zip(pairs, stages, loaded):
                act.wait_ge(ready, 16 + 1)
                act.activation(hi, stage[:], ACT.Copy).then_inc(hi_ready, 1)

        @block.vector
        def _(dve):
            for n, ((_, hi, lo), stage) in enumerate(zip(pairs, stages)):
                dve.wait_ge(hi_ready, n + 2)
                dve.tensor_tensor(lo, stage[:], hi, ALU.subtract).then_inc(lo_ready, 1)


def project(core, xh, xl, wqk, wv, qk_dram, v_dram, v_cm, sigmoid):
    nc = core.nc
    wqk_hi, wqk_lo = wqk
    wv_hi, wv_lo = wv
    with ExitStack() as ctx:
        hi = core.sb(ctx, "qk_hi", [P, 2, 4, CH], F16)
        lo = core.sb(ctx, "qk_lo", [P, 2, 4, CH], F16)
        gate = core.sb(ctx, "gate", [P, 2, 4, CH])
        v_tok = core.sb(ctx, "v_tok", [P, 2, SUB, C])
        qk_ps = core.ps(ctx, "qk_ps", [P, 4, 512])
        v_ps = core.ps(ctx, "v_ps", [P, 2, 512])
        vt_ps = core.ps(ctx, "vt_ps", [P, 2, 512])
        qk_made, vcm_made, vt_made = core.sem("qk_made"), core.sem("vcm_made"), core.sem("vt_made")
        gated, hi_ready, lo_ready = core.sem("gated"), core.sem("hi_ready"), core.sem("lo_ready")
        vcm_taken, vt_taken = core.sem("vcm_taken"), core.sem("vt_taken")
        v_squared, v_summed, v_rooted, v_guarded, v_inverted, v_ready = (
            core.sem(n) for n in ("v_squared", "v_summed", "v_rooted", "v_guarded", "v_inverted", "v_ready"))
        hi_stored = [core.sem("hi_stored") for _ in range(2)]
        lo_stored = [core.sem("lo_stored") for _ in range(2)]
        v_stored = [core.sem("v_stored") for _ in range(2)]
        v_sq = core.sb(ctx, "v_sq", [P, SUB, C])
        v_ss = core.sb(ctx, "v_ss", [P, SUB, HEADS])
        v_norm = core.sb(ctx, "v_norm", [P, SUB, HEADS])
        v_guard = core.sb(ctx, "v_guard", [P, SUB, HEADS])
        v_inv = core.sb(ctx, "v_inv", [P, SUB, HEADS])
        block = ctx.enter_context(core.block())

        @block.tensor
        def _(pe):
            with pe.Fori(0, NCH) as c:
                chunk = ds(c * CH, CH)
                for m in range(4):
                    pe.wait_ge(lo_ready, 4 * c + 1)
                    for k in range(CT):
                        w = ds((m * CT + k) * P, P)
                        mm = split_matmul(pe, qk_ps[:, m, 0:CH], wqk_hi[:, w], wqk_lo[:, w],
                                          xh[:, k, chunk], xl[:, k, chunk], k == 0, k == CT - 1)
                    mm.then_inc(qk_made, 1)
                if v_cm is not None:
                    for m in range(CT):
                        pe.wait_ge(vcm_taken, 2 * c + 1)
                        for k in range(CT):
                            mm = split_matmul(pe, v_ps[:, m, 0:CH], wv_hi[:, k, m * P:(m + 1) * P],
                                              wv_lo[:, k, m * P:(m + 1) * P], xh[:, k, chunk], xl[:, k, chunk],
                                              k == 0, k == CT - 1)
                        mm.then_inc(vcm_made, 1)
                for t in range(SUB):
                    pe.wait_ge(vt_taken, 2 * c + 1)
                    out = vt_ps[:, t // 2, (t % 2) * C:(t % 2 + 1) * C]
                    tok = ds(c * CH + t * P, P)
                    for k in range(CT):
                        pe.matmul(out, xh[:, k, tok], wv_hi[:, k, :], start=k == 0, stop=False)
                        pe.matmul(out, xl[:, k, tok], wv_hi[:, k, :], start=False, stop=False)
                        mm = pe.matmul(out, xh[:, k, tok], wv_lo[:, k, :], start=False, stop=k == CT - 1)
                    mm.then_inc(vt_made, 1)

        @block.scalar
        def _(act):
            with act.Fori(0, NCH // 2) as i:
                for b in range(2):
                    c = 2 * i + b
                    act.wait_ge(hi_stored[b], 16 * i + 1)
                    if sigmoid:
                        act.wait_ge(lo_ready, 8 * i + 1)
                    for m in range(4):
                        act.wait_ge(qk_made, 4 * c + m + 2)
                        if sigmoid:
                            act.activation(gate[:, b, m], qk_ps[:, m, 0:CH], ACT.Sigmoid).then_inc(gated, 1)
                            act.wait_ge(gated, 4 * c + m + 2)
                            act.activation(hi[:, b, m], gate[:, b, m], ACT.Copy).then_inc(hi_ready, 1)
                        else:
                            act.activation(hi[:, b, m], qk_ps[:, m, 0:CH], ACT.Copy).then_inc(hi_ready, 1)
                    if v_cm is not None:
                        for m in range(CT):
                            act.wait_ge(vcm_made, 2 * c + m + 2)
                            act.activation(v_cm[:, m, ds(c * CH, CH)], v_ps[:, m, 0:CH],
                                           ACT.Copy).then_inc(vcm_taken, 1)
                    if sigmoid:
                        act.wait_ge(v_summed, c + 2)
                        act.activation(v_norm[:], v_ss[:], ACT.Sqrt).then_inc(v_rooted, 1)

        @block.vector
        def _(dve):
            with dve.Fori(0, NCH // 2) as i:
                for b in range(2):
                    c = 2 * i + b
                    dve.wait_ge(lo_stored[b], 16 * i + 1)
                    for m in range(4):
                        dve.wait_ge(hi_ready, 4 * c + m + 2)
                        whole = gate[:, b, m] if sigmoid else qk_ps[:, m, 0:CH]
                        dve.tensor_tensor(lo[:, b, m], whole, hi[:, b, m], ALU.subtract).then_inc(lo_ready, 1)
                    dve.wait_ge(v_stored[b], 16 * i + 1)
                    dve.wait_ge(vt_made, 3 * c + 3 + 1)
                    dve.tensor_copy(v_tok[:, b, 0:2].rearrange("p t c -> p (t c)"), vt_ps[:, 0, :]).then_inc(vt_taken, 1)
                    dve.tensor_copy(v_tok[:, b, 2], vt_ps[:, 1, 0:C]).then_inc(vt_taken, 1)
                    if sigmoid:
                        dve.wait_ge(vt_taken, 2 * c + 2 + 1)
                        dve.tensor_tensor(v_sq[:], v_tok[:, b], v_tok[:, b], ALU.mult).then_inc(v_squared, 1)
                        dve.wait_ge(v_squared, c + 2)
                        dve.tensor_reduce(v_ss[:], v_sq[:].rearrange("p t (h d) -> p t h d", h=HEADS), AX.X,
                                          ALU.add).then_inc(v_summed, 1)
                        dve.wait_ge(v_rooted, c + 2)
                        dve.tensor_scalar(v_guard[:], v_norm[:], 1e-12, None, ALU.max).then_inc(v_guarded, 1)
                        dve.wait_ge(v_guarded, c + 2)
                        dve.reciprocal(v_inv[:], v_guard[:]).then_inc(v_inverted, 1)
                        dve.wait_ge(v_inverted, c + 2)
                        heads = v_tok[:, b].rearrange("p t (h d) -> p (t h) d", h=HEADS)
                        dve.tensor_tensor(heads, heads,
                                          v_inv[:].rearrange("p t h -> p (t h)").unsqueeze(2).broadcast_to([P, SUB * HEADS, HD]),
                                          ALU.mult).then_inc(v_ready, 1)

        @block.sync
        def _(sp):
            with sp.Fori(0, NCH // 2) as i:
                for b in range(2):
                    c = 2 * i + b
                    chunk = ds(c * CH, CH)
                    sp.wait_ge(hi_ready, 4 * c + 4 + 1)
                    sp.dma_start(qk_dram[0, :, chunk].rearrange("(m p) t -> p m t", p=P), hi[:, b]).then_inc(hi_stored[b], 16)
                    sp.wait_ge(lo_ready, 4 * c + 4 + 1)
                    sp.dma_start(qk_dram[1, :, chunk].rearrange("(m p) t -> p m t", p=P), lo[:, b]).then_inc(lo_stored[b], 16)
                    if sigmoid:
                        sp.wait_ge(v_ready, c + 2)
                    else:
                        sp.wait_ge(vt_taken, 2 * c + 2 + 1)
                    sp.dma_start(v_dram[chunk, :].rearrange("(t p) c -> p t c", p=P), v_tok[:, b]).then_inc(v_stored[b], 16)
            for b in range(2):
                for s in (hi_stored[b], lo_stored[b], v_stored[b]):
                    sp.wait_ge(s, 16 * (NCH // 2) + 1)


def softmax_attention(core, qk_dram, v_dram, v_cm, w_tap, b_tap, out_cm, ones32, ident):
    nc = core.nc
    with ExitStack() as ctx:
        qs = [core.sb(ctx, "qs", [PADK, 2, N], F16) for _ in range(2)]
        ks = [core.sb(ctx, "ks", [PADK, 2, N], F16) for _ in range(2)]
        vs = [core.sb(ctx, "vs", [P, KT, 2 * HD]) for _ in range(2)]
        prob = core.sb(ctx, "prob", [P, 3, 2, CH])
        part_max = core.sb(ctx, "part_max", [P, 2, KT, 3])
        row_max = core.sb(ctx, "row_max", [P, 2, KT])
        neg_max = core.sb(ctx, "neg_max", [2 * KT, P], F16)
        summed = core.sb(ctx, "summed", [P, CH])
        rden = core.sb(ctx, "rden", [P, CH])
        tap_sum = core.sb(ctx, "tap_sum", [P, N])
        tap_one = core.sb(ctx, "tap_one", [P, N])
        s_ps = [core.ps(ctx, "s_ps", [P, 2, 512]) for _ in range(2)]
        m_ps = core.ps(ctx, "m_ps", [P, 2, 512])
        acc_ps = core.ps(ctx, "acc_ps", [P, 512])
        t_ps = core.ps(ctx, "t_ps", [P, 512])
        names = ("ones_set", "scored", "weighed", "valued", "acc_done", "acc_taken", "inverted", "out_done",
                 "m_scored", "m_taken", "row_ready", "turned", "neg_ready", "tap_step", "tap_added")
        (ones_set, scored, weighed, valued, acc_done, acc_taken, inverted, out_done,
         m_scored, m_taken, row_ready, turned, neg_ready, tap_step, tap_added) = (core.sem(n) for n in names)
        loaded = [core.sem("loaded") for _ in range(2)]
        max_placed = [core.sem("max_placed") for _ in range(2)]
        block = ctx.enter_context(core.block())
        UNITS = QC * KT
        GROUPS = PAIRS // 2
        LOADS = 16 * 13

        @block.sync
        def _(sp):
            def load(g, b):
                tok = ds(g % B * N, N)
                for h in range(2):
                    row = (g // B * 4 + 2 * b + h) * HD
                    for dst, first, order in ((qs[b], 0, (0, 0, 1)), (ks[b], C, (0, 1, 0))):
                        for part, half in enumerate(order):
                            sp.dma_start(dst[part * HD:(part + 1) * HD, h, :],
                                         qk_dram[half, ds(first + row, HD), tok]).then_inc(loaded[b], 16)
                sp.dma_start(vs[b][:], v_dram[tok, ds((g // B * 4 + 2 * b) * HD, 2 * HD)].rearrange(
                    "(t p) c -> p t c", p=P)).then_inc(loaded[b], 16)

            def place_max(g, b):
                sp.wait_ge(neg_ready, 2 * g + b + 2)
                for h in range(2):
                    sp.dma_start(qs[b][3 * HD:PADK, h, :], neg_max[h * KT:(h + 1) * KT, :]).then_inc(max_placed[b], 16)

            load(0, 0)
            load(0, 1)
            place_max(0, 0)
            with sp.Fori(0, GROUPS - 1) as g:
                place_max(g, 1)
                sp.wait_ge(valued, (2 * g + 1) * UNITS + 1)
                load(g + 1, 0)
                place_max(g + 1, 0)
                sp.wait_ge(valued, (2 * g + 2) * UNITS + 1)
                load(g + 1, 1)
            place_max(GROUPS - 1, 1)

        @block.tensor
        def _(pe):
            def scores(pair, qc, b, kt, opening=False):
                base = pair * UNITS + qc * KT
                pe.wait_ge(weighed, (base if opening else base + kt - 1) + 1)
                for h in range(2):
                    mm = pe.matmul(s_ps[kt % 2][:, h, 0:CH], ks[b][:, h, kt * P:(kt + 1) * P],
                                   qs[b][:, h, ds(qc * CH, CH)], start=True, stop=True)
                mm.then_inc(scored, 1)

            def max_scores(pair, qc, b, kt):
                h, sub, third = kt // 9, kt % 9 // 3, kt % 3
                pe.wait_ge(m_taken, pair * UNITS + qc * KT + kt + 1)
                for j in range(2):
                    mm = pe.matmul(m_ps[:, j, 0:CH], qs[b][0:3 * HD, h, ds((qc * SUB + sub) * P, P)],
                                   ks[b][0:3 * HD, h, (2 * third + j) * CH:(2 * third + j + 1) * CH],
                                   start=True, stop=True)
                mm.then_inc(m_scored, 1)

            def values(pair, qc, b, kt):
                if kt == 0:
                    pe.wait_ge(acc_taken, pair * QC + qc + 1)
                pe.wait_ge(weighed, pair * UNITS + qc * KT + kt + 2)
                num, den = (0, 64) if b == 0 else (64, 0)
                for h in range(2):
                    pe.matmul(acc_ps[num + h * HD:num + (h + 1) * HD, 0:CH], vs[b][:, kt, h * HD:(h + 1) * HD],
                              prob[:, kt % 3, h], start=kt == 0, stop=kt == KT - 1)
                for h in range(2):
                    mm = pe.matmul(acc_ps[den + h * HD:den + (h + 1) * HD, 0:CH], ones32[:],
                                   prob[:, kt % 3, h], start=kt == 0, stop=kt == KT - 1)
                mm.then_inc(valued, 1)

            def chunk_steps(pair, qc, b, closing, next_too):
                for kt in range(KT):
                    if kt < KT - 1:
                        scores(pair, qc, b, kt + 1)
                    elif not closing:
                        scores(pair, qc + 1, b, 0)
                    if next_too:
                        max_scores(pair + 1, qc, 1 - b, kt)
                    values(pair, qc, b, kt)

            def turn_max(pair):
                pe.wait_ge(row_ready, pair + 2)
                pe.wait_ge(neg_ready, pair + 1)
                pe.matmul(t_ps[0:2 * KT, 0:P], row_max[:].rearrange("p h t -> p (h t)"), ident[:],
                          start=True, stop=True).then_inc(turned, 1)

            def second_pass(g, b, next_too):
                pair = 2 * g + b
                if next_too:
                    pe.wait_ge(loaded[1 - b], LOADS * (g + b + 1) + 1)
                pe.wait_ge(max_placed[b], 32 * (g + 1) + 1)
                scores(pair, 0, b, 0, opening=True)
                with pe.Fori(0, QC - 1) as qc:
                    chunk_steps(pair, qc, b, False, next_too)
                chunk_steps(pair, QC - 1, b, True, next_too)
                if next_too:
                    turn_max(pair + 1)

            pe.wait_ge(ones_set, 2 + 1)
            pe.wait_ge(loaded[0], LOADS + 1)
            with pe.Fori(0, QC) as qc:
                for kt in range(KT):
                    max_scores(0, qc, 0, kt)
            turn_max(0)
            with pe.Fori(0, GROUPS - 1) as g:
                second_pass(g, 0, True)
                second_pass(g, 1, True)
            second_pass(GROUPS - 1, 0, True)
            second_pass(GROUPS - 1, 1, False)

        @block.scalar
        def _(act):
            def weigh(chunk):
                for kt in range(KT):
                    act.wait_ge(scored, chunk * KT + kt + 2)
                    if not (isinstance(chunk, int) and kt < 3):
                        act.wait_ge(valued, chunk * KT + kt - 2 + 1)
                    act.activation(prob[:, kt % 3], s_ps[kt % 2][:, :, 0:CH], ACT.Exp, scale=SCALE).then_inc(weighed, 1)

            weigh(0)
            with act.Fori(1, PAIRS * QC) as chunk:
                weigh(chunk)

        @block.vector
        def _(dve):
            for b in range(2):
                dve.memset(ks[b][3 * HD:PADK, :, :], 1.0).then_inc(ones_set, 1)

            def max_steps(pair, qc):
                for kt in range(KT):
                    h, sub, third = kt // 9, kt % 9 // 3, kt % 3
                    dve.wait_ge(m_scored, pair * UNITS + qc * KT + kt + 2)
                    dve.tensor_reduce(part_max[:, h, ds(qc * SUB + sub, 1), third:third + 1],
                                      m_ps[:, :, 0:CH], AX.XY, ALU.max).then_inc(m_taken, 1)

            def max_rows(g, b):
                pair = 2 * g + b
                dve.wait_ge(m_taken, (pair + 1) * UNITS + 1)
                dve.wait_ge(turned, pair + 1)
                dve.tensor_reduce(row_max[:], part_max[:], AX.X, ALU.max).then_inc(row_ready, 1)
                dve.wait_ge(turned, pair + 2)
                dve.wait_ge(max_placed[1 - b], 32 * (g + b) + 1)
                dve.tensor_scalar(neg_max[:], t_ps[0:2 * KT, 0:P], -1.0, None, ALU.mult).then_inc(neg_ready, 1)

            def finish_chunk(g, qc, b):
                index = (2 * g + b) * QC + qc
                num, den = (0, 64) if b == 0 else (64, 0)
                dve.wait_ge(valued, index * KT + KT + 1)
                dve.wait_ge(out_done, index + 1)
                dve.tensor_copy(summed[:], acc_ps[:, 0:CH]).then_inc(acc_taken, 1)
                dve.wait_ge(acc_taken, index + 2)
                dve.reciprocal(rden[num:num + 64, :], summed[den:den + 64, :]).then_inc(inverted, 1)
                dve.wait_ge(inverted, index + 2)
                dve.tensor_tensor(out_cm[num:num + 64, ds(g * N + qc * CH, CH)], summed[num:num + 64, :],
                                  rden[num:num + 64, :], ALU.mult).then_inc(out_done, 1)

            def pair_steps(g, b, next_too):
                with dve.Fori(0, QC) as qc:
                    if next_too:
                        max_steps(2 * g + b + 1, qc)
                    finish_chunk(g, qc, b)
                if next_too:
                    max_rows(g + b, 1 - b)

            with dve.Fori(0, QC) as qc:
                max_steps(0, qc)
            max_rows(0, 0)
            with dve.Fori(0, GROUPS - 1) as g:
                pair_steps(g, 0, True)
                pair_steps(g, 1, True)
            pair_steps(GROUPS - 1, 0, True)
            pair_steps(GROUPS - 1, 1, False)

        @block.gpsimd
        def _(pool):
            centre = [(0, 0)] + [(dy, dx) for dy in (-1, 0, 1) for dx in (-1, 0, 1) if (dy, dx) != (0, 0)]
            steps = 2 * len(centre)
            for g in range(GROUPS):
                tile, img = g // B, g % B
                base = g * steps
                image = v_cm[:, tile, img * N:(img + 1) * N].rearrange("p (y x) -> p y x", y=HW)
                total = tap_sum[:].rearrange("p (y x) -> p y x", y=HW)
                single = tap_one[:].rearrange("p (y x) -> p y x", y=HW)
                for n, (dy, dx) in enumerate(centre):
                    y0, y1 = max(0, -dy), HW - max(0, dy)
                    x0, x1 = max(0, -dx), HW - max(0, dx)
                    shifted = image[:, y0 + dy:y1 + dy, x0 + dx:x1 + dx]
                    tap = w_tap[:, tile, 3 * (dy + 1) + dx + 1:3 * (dy + 1) + dx + 2]
                    tap = tap.unsqueeze(2).broadcast_to([P, y1 - y0, x1 - x0])
                    if n == 0:
                        pool.wait_ge(tap_added, g + 1)
                        pool.tensor_tensor(total, shifted, tap, ALU.mult).then_inc(tap_step, 1)
                        pool.wait_ge(tap_step, base + 2)
                        pool.tensor_tensor(total, total, b_tap[:, tile:tile + 1].unsqueeze(2).broadcast_to([P, HW, HW]),
                                           ALU.add).then_inc(tap_step, 1)
                        continue
                    pool.wait_ge(tap_step, base + 2 * n + 1)
                    pool.tensor_tensor(single[:, y0:y1, x0:x1], shifted, tap, ALU.mult).then_inc(tap_step, 1)
                    pool.wait_ge(tap_step, base + 2 * n + 2)
                    pool.tensor_tensor(total[:, y0:y1, x0:x1], total[:, y0:y1, x0:x1],
                                       single[:, y0:y1, x0:x1], ALU.add).then_inc(tap_step, 1)
                pool.wait_ge(tap_step, base + steps + 1)
                pool.wait_ge(out_done, 2 * QC * (g + 1) + 1)
                part = out_cm[:, g * N:(g + 1) * N]
                pool.tensor_tensor(part, part, tap_sum[:], ALU.add).then_inc(tap_added, 1)


def window_parts(w):
    parts = {}
    for delta in range(-(QC - 1), QC):
        for sub in range(SUB):
            first, last = sub * P // HW, (sub * P + P - 1) // HW
            rows = [y for y in range(CH // HW)
                    if any(0 <= k + 8 * delta - y + w // 2 < w for k in range(first, last + 1))]
            if rows:
                parts[delta, sub] = (rows[0], rows[-1] + 1)
    return parts


def window_attention(core, qk_dram, v_dram, mask_dram, o_dram, ones32):
    nc = core.nc
    parts = [window_parts(w) for w in WINDOWS]
    slots = {}
    for w, part in enumerate(parts):
        for key in part:
            slots[w, key] = len(slots)
    with ExitStack() as ctx:
        qs = [core.sb(ctx, "qs", [3 * HD, 2, N], F16) for _ in range(2)]
        ks = [core.sb(ctx, "ks", [3 * HD, 2, N], F16) for _ in range(2)]
        vs = [core.sb(ctx, "vs", [P, KT, 2 * HD]) for _ in range(2)]
        masks = core.sb(ctx, "masks", [P, len(slots), CH], F16)
        kept = core.sb(ctx, "kept", [P, 4, 2, CH])
        summed = core.sb(ctx, "summed", [P, 3, CH])
        rden = core.sb(ctx, "rden", [P, 3, CH])
        quotient = core.sb(ctx, "quotient", [P, 3, CH])
        s_ps = [core.ps(ctx, "s_ps", [P, 2, 512]) for _ in range(2)]
        acc_ps = core.ps(ctx, "acc_ps", [P, 3, 512])
        masks_loaded, scored, masked, valued, acc_taken, guarded, inverted, out_done = (
            core.sem(n) for n in ("masks_loaded", "scored", "masked", "valued", "acc_taken", "guarded",
                                  "inverted", "out_done"))
        stored = [core.sem("stored") for _ in WINDOWS]
        loaded = [core.sem("loaded") for _ in range(2)]
        block = ctx.enter_context(core.block())

        plan = []
        for qc in range(QC):
            for kt in range(KT):
                key = (kt // SUB - qc, kt % SUB)
                hit = [w for w in range(3) if key in parts[w]]
                if hit:
                    plan.append((qc, kt, key, hit))
        last = {(qc, w): max(n for n, (a, _, _, hit) in enumerate(plan) if a == qc and w in hit)
                for qc in range(QC) for w in range(3)}
        items = []
        for n, (qc, kt, key, hit) in enumerate(plan):
            for w in hit:
                items.append((n, w))
        S, M = len(plan), len(items)
        begun = set()
        first_of = {}
        for n, w in items:
            qc = plan[n][0]
            first_of[n, w] = (qc, w) not in begun
            begun.add((qc, w))

        def rows_of(n, w):
            return (0, CH // HW) if first_of[n, w] else parts[w][plan[n][2]]

        @block.sync
        def _(sp):
            def load(g, b):
                tok = ds(g % B * N, N)
                for h in range(2):
                    row = (g // B * 4 + 2 * b + h) * HD
                    for dst, first, order in ((qs[b], 0, (0, 0, 1)), (ks[b], C, (0, 1, 0))):
                        for part, half in enumerate(order):
                            sp.dma_start(dst[part * HD:(part + 1) * HD, h, :],
                                         qk_dram[half, ds(first + row, HD), tok]).then_inc(loaded[b], 16)
                sp.dma_start(vs[b][:], v_dram[tok, ds((g // B * 4 + 2 * b) * HD, 2 * HD)].rearrange(
                    "(t p) c -> p t c", p=P)).then_inc(loaded[b], 16)

            sp.dma_start(masks[:], mask_dram).then_inc(masks_loaded, 16)
            load(0, 0)
            load(0, 1)
            with sp.Fori(0, PAIRS // 2 - 1) as g:
                for b in range(2):
                    sp.wait_ge(valued, (2 * g + b + 1) * M + 1)
                    load(g + 1, b)

        @block.tensor
        def _(pe):
            def scores(pair, n, b):
                qc, kt, _, _ = plan[n]
                if n >= 2:
                    pe.wait_ge(masked, pair * M + sum(1 for a, _ in items if a <= n - 2) + 1)
                else:
                    pe.wait_ge(masked, pair * M + 1)
                for h in range(2):
                    mm = pe.matmul(s_ps[n % 2][:, h, 0:CH], ks[b][:, h, kt * P:(kt + 1) * P],
                                   qs[b][:, h, qc * CH:(qc + 1) * CH], start=True, stop=True)
                mm.then_inc(scored, 1)

            def values(pair, b):
                scores(pair, 0, b)
                for m, (n, w) in enumerate(items):
                    qc, kt, _, hit = plan[n]
                    if w == hit[0] and n + 1 < S:
                        scores(pair, n + 1, b)
                    r0, r1 = rows_of(n, w)
                    cols = slice(r0 * HW, r1 * HW)
                    if first_of[n, w]:
                        pe.wait_ge(acc_taken, 3 * (pair * QC + qc) + 1)
                    pe.wait_ge(masked, pair * M + m + 2)
                    for h in range(2):
                        pe.matmul(acc_ps[h * HD:(h + 1) * HD, w, cols], vs[b][:, kt, h * HD:(h + 1) * HD],
                                  kept[:, m % 4, h, cols], start=first_of[n, w], stop=n == last[qc, w])
                    for h in range(2):
                        mm = pe.matmul(acc_ps[64 + h * HD:64 + (h + 1) * HD, w, cols], ones32[:],
                                       kept[:, m % 4, h, cols], start=first_of[n, w], stop=n == last[qc, w])
                    mm.then_inc(valued, 1)

            with pe.Fori(0, PAIRS // 2) as g:
                for b in range(2):
                    pe.wait_ge(loaded[b], 13 * 16 * (g + 1) + 1)
                    values(2 * g + b, b)

        @block.vector
        def _(dve):
            dve.wait_ge(masks_loaded, 16 + 1)
            with dve.Fori(0, PAIRS) as pair:
                def finish(qc):
                    dve.wait_ge(out_done, pair * QC + qc + 1)
                    for w in range(3):
                        lastitem = max(m for m, (n, v) in enumerate(items) if v == w and plan[n][0] == qc)
                        dve.wait_ge(valued, pair * M + lastitem + 2)
                        dve.tensor_copy(summed[:, w], acc_ps[:, w, 0:CH]).then_inc(acc_taken, 1)
                    base = pair * QC + qc
                    for w in range(3):
                        dve.wait_ge(stored[w], 16 * base + 1)
                    dve.wait_ge(acc_taken, 3 * base + 3 + 1)
                    dve.tensor_scalar(rden[0:64], summed[64:128], 1e-6, None, ALU.add).then_inc(guarded, 1)
                    dve.wait_ge(guarded, base + 2)
                    dve.reciprocal(rden[0:64], rden[0:64]).then_inc(inverted, 1)
                    dve.wait_ge(inverted, base + 2)
                    dve.tensor_tensor(quotient[0:64], summed[0:64], rden[0:64], ALU.mult).then_inc(out_done, 1)

                begins = [min(m for m, (n, _) in enumerate(items) if plan[n][0] == qc) for qc in range(QC)]
                for m, (n, w) in enumerate(items):
                    qc, kt, key, hit = plan[n]
                    if m - 2 in begins[1:]:
                        finish(begins.index(m - 2) - 1)
                    if w == hit[0]:
                        dve.wait_ge(scored, pair * S + n + 2)
                    if m >= 4:
                        dve.wait_ge(valued, pair * M + m - 3 + 1)
                    else:
                        dve.wait_ge(valued, pair * M + 1)
                    r0, r1 = rows_of(n, w)
                    cols = slice(r0 * HW, r1 * HW)
                    mask = masks[:, slots[w, key], cols].unsqueeze(1).broadcast_to([P, 2, (r1 - r0) * HW])
                    dve.tensor_tensor(kept[:, m % 4, :, cols], s_ps[n % 2][:, :, cols], mask,
                                      ALU.mult).then_inc(masked, 1)
                finish(QC - 1)

        @block.scalar
        def _(act):
            with act.Fori(0, PAIRS // 2) as g:
                for b in range(2):
                    with act.Fori(0, QC) as qc:
                        act.wait_ge(out_done, (2 * g + b) * QC + qc + 2)
                        for w in range(3):
                            act.dma_start(o_dram[w, ds((g // B * 4 + 2 * b) * HD, 2 * HD), ds(g % B * N + qc * CH, CH)],
                                          quotient[0:64, w]).then_inc(stored[w], 16)
            for w in range(3):
                act.wait_ge(stored[w], 16 * PAIRS * QC + 1)


def project_out(core, x_cm, weight, bias, tiles, o_cm=None, o_dram=None):
    nc = core.nc
    with ExitStack() as ctx:
        stage = core.sb(ctx, "stage", [P, 2, tiles, CH]) if o_dram is not None else None
        y_ps = core.ps(ctx, "y_ps", [P, 4, 512])
        made, added = core.sem("made"), core.sem("added")
        fetched = [core.sem("fetched") for _ in range(2)]
        block = ctx.enter_context(core.block())

        @block.sync
        def _(sp):
            if o_dram is not None:
                with sp.Fori(0, NCH // 2) as i:
                    for b in range(2):
                        sp.wait_ge(made, 4 * i + 1)
                        sp.dma_start(stage[:, b], o_dram[:, ds((2 * i + b) * CH, CH)].rearrange(
                            "(k p) t -> p k t", p=P)).then_inc(fetched[b], 16)

        @block.tensor
        def _(pe):
            with pe.Fori(0, NCH // 2) as i:
                for b in range(2):
                    if o_dram is not None:
                        pe.wait_ge(fetched[b], 16 * (i + 1) + 1)
                    for m in range(CT):
                        pe.wait_ge(added, 4 * i + 1)
                        for k in range(tiles):
                            src = stage[:, b, k] if o_dram is not None else o_cm[:, k, ds((2 * i + b) * CH, CH)]
                            mm = pe.matmul(y_ps[:, 2 * b + m, 0:CH], weight[:, k, m * P:(m + 1) * P], src,
                                           start=k == 0, stop=k == tiles - 1)
                        mm.then_inc(made, 1)

        @block.vector
        def _(dve):
            with dve.Fori(0, NCH // 2) as i:
                for b in range(2):
                    for m in range(CT):
                        dve.wait_ge(made, 4 * i + 2 * b + m + 2)
                        x = x_cm[:, m, ds((2 * i + b) * CH, CH)]
                        dve.scalar_tensor_tensor(out=x, in0=y_ps[:, 2 * b + m, 0:CH], scalar=bias[:, m:m + 1], in1=x,
                                                 op0=ALU.add, op1=ALU.add).then_inc(added, 1)


def route(core, th, tl, wr, br, comb, iota):
    nc = core.nc
    wr_hi, wr_lo = wr
    with ExitStack() as ctx:
        big = [P, TT, E]
        small = [P, TT]
        logits, work, hot1, hot2, prob = (core.sb(ctx, n, big) for n in ("logits", "work", "hot1", "hot2", "prob"))
        top, index, total, rest = (core.sb(ctx, n, small) for n in ("top", "index", "total", "rest"))
        l_ps = core.ps(ctx, "l_ps", [P, 512])
        made, step, exped = core.sem("made"), core.sem("step"), core.sem("exped")
        block = ctx.enter_context(core.block())
        wide = lambda t: t[:].unsqueeze(2).broadcast_to(big)
        experts = iota[:, 0:E].unsqueeze(1).broadcast_to(big)

        @block.tensor
        def _(pe):
            with pe.Fori(0, TT) as t:
                out = l_ps[:, ds(t * E, E)]
                tok = ds(t * P, P)
                for k in range(CT):
                    pe.matmul(out, th[:, k, tok], wr_hi[:, k, :], start=k == 0, stop=False)
                    pe.matmul(out, tl[:, k, tok], wr_hi[:, k, :], start=False, stop=False)
                    mm = pe.matmul(out, th[:, k, tok], wr_lo[:, k, :], start=False, stop=k == CT - 1)
                mm.then_inc(made, 1)

        @block.scalar
        def _(act):
            act.wait_ge(step, 3 + 1)
            act.activation(prob[:], work[:], ACT.Exp).then_inc(exped, 1)

        @block.vector
        def _(dve):
            count = 0

            def then(ins):
                nonlocal count
                count += 1
                ins.then_inc(step, 1)
                dve.wait_ge(step, count + 1)

            dve.wait_ge(made, TT + 1)
            scores = l_ps[:, 0:TT * E].rearrange("p (t e) -> p t e", e=E)
            if br is None:
                then(dve.tensor_copy(logits[:], scores))
            else:
                then(dve.tensor_tensor(logits[:], scores, br.unsqueeze(1).broadcast_to(big), ALU.add))
            then(dve.tensor_reduce(top[:], logits[:], AX.X, ALU.max))
            then(dve.tensor_tensor(work[:], logits[:], wide(top), ALU.subtract))
            dve.wait_ge(exped, 1 + 1)
            then(dve.tensor_reduce(total[:], prob[:], AX.X, ALU.add))
            then(dve.reciprocal(total[:], total[:]))
            then(dve.tensor_tensor(prob[:], prob[:], wide(total), ALU.mult))
            for hot in (hot1, hot2):
                then(dve.tensor_tensor(work[:], logits[:], wide(top), ALU.is_lt))
                then(dve.scalar_tensor_tensor(out=work[:], in0=work[:], scalar=float(E), in1=experts,
                                              op0=ALU.mult, op1=ALU.add))
                then(dve.tensor_reduce(index[:], work[:], AX.X, ALU.min))
                then(dve.tensor_tensor(hot[:], experts, wide(index), ALU.is_equal))
                if hot is hot1:
                    then(dve.scalar_tensor_tensor(out=logits[:], in0=hot[:], scalar=-3.0e38, in1=logits[:],
                                                  op0=ALU.mult, op1=ALU.add))
                    then(dve.tensor_reduce(top[:], logits[:], AX.X, ALU.max))
            then(dve.tensor_tensor(hot1[:], hot1[:], hot2[:], ALU.add))
            then(dve.tensor_tensor(prob[:], prob[:], hot1[:], ALU.mult))
            then(dve.tensor_reduce(total[:], prob[:], AX.X, ALU.add))
            then(dve.tensor_scalar(total[:], total[:], 1e-12, None, ALU.max))
            then(dve.reciprocal(rest[:], total[:]))
            then(dve.tensor_tensor(comb[:], prob[:], wide(rest), ALU.mult))


def experts(core, x_cm, xh, xl, comb, w1, b1, w2, b2, hidden, ident, one, ln_g=None, ln_b=None):
    nc = core.nc
    MT = hidden // P
    HR = 4
    w1_v = w1.rearrange("e (k p) h -> e p k h", p=P)
    w2_v = w2.rearrange("e (k p) c -> e p k c", p=P)
    with ExitStack() as outer:
        acc = core.sb(outer, "acc", [P, TT, C])
        with ExitStack() as ctx:
            w1_in = core.sb(ctx, "w1_in", [P, CT, hidden])
            w2_in = core.sb(ctx, "w2_in", [P, MT, C])
            w1s = [[core.sb(ctx, "w1s", [P, CT, hidden], F16) for _ in range(2)] for _ in range(2)]
            w2s = [[core.sb(ctx, "w2s", [P, MT, C], F16) for _ in range(2)] for _ in range(2)]
            b1_all = core.sb(ctx, "b1_all", [P, E, MT])
            bias1 = core.sb(ctx, "bias1", [P, 2, MT])
            b2_row = core.sb(ctx, "b2_row", [P, 2, C])
            h32 = core.sb(ctx, "h32", [P, 2, CH])
            hh = core.sb(ctx, "hh", [P, 2, MT, CH], F16)
            hl = core.sb(ctx, "hl", [P, 2, MT, CH], F16)
            y_one = core.sb(ctx, "y_one", [P, SUB, C])
            g_all = core.sb(ctx, "g_all", [P, E, CT])
            b_all = core.sb(ctx, "b_all", [P, E, CT])
            h_ps = core.ps(ctx, "h_ps", [P, HR, 512])
            y_ps = core.ps(ctx, "y_ps", [P, 3, 512])
            bias_ps = core.ps(ctx, "bias_ps", [P, 512])
            small_in, w_in, b2_in = core.sem("small_in"), core.sem("w_in"), [core.sem("b2_in") for _ in range(2)]
            zeroed = core.sem("zeroed")
            scaled, split, bias_made, bias_ready = (core.sem(n) for n in ("scaled", "split", "bias_made", "bias_ready"))
            h_made, h_ready, h_hi, h_split, y_made, y_taken, y_added = (
                core.sem(n) for n in ("h_made", "h_ready", "h_hi", "h_split", "y_made", "y_taken", "y_added"))
            block = ctx.enter_context(core.block())
            norm = ln_g is not None

            @block.sync
            def _(sp):
                sp.dma_start(b1_all[:], b1).then_inc(small_in, 16)
                if norm:
                    sp.dma_start(g_all[:], ln_g).then_inc(small_in, 16)
                    sp.dma_start(b_all[:], ln_b).then_inc(small_in, 16)
                for e in range(E):
                    sp.wait_ge(split, 4 * e + 1)
                    sp.wait_ge(bias_ready, e + 1)
                    sp.dma_start(w1_in[:], w1_v[e]).then_inc(w_in, 16)
                    sp.dma_start(w2_in[:], w2_v[e]).then_inc(w_in, 16)
                    if e >= 2:
                        sp.wait_ge(y_added, TT * (e - 1) + 1)
                    sp.dma_start(b2_row[:, e % 2], b2[e:e + 1, :].broadcast_to([P, C])).then_inc(b2_in[e % 2], 16)

            @block.gpsimd
            def _(pool):
                pool.wait_ge(small_in, (48 if norm else 16) + 1)

                def prepare(i, b):
                    e = 2 * i + b
                    pool.wait_ge(w_in, 32 * (e + 1) + 1)
                    if not isinstance(i, int):
                        pool.wait_ge(y_made, TT * (2 * i - 1 + b) + 1)
                    if norm:
                        pool.wait_ge(bias_made, e + 2)
                        for k in range(CT):
                            pool.tensor_tensor(w1_in[:, k], w1_in[:, k], g_all[:, ds(e, 1), k].broadcast_to([P, hidden]),
                                               ALU.mult).then_inc(scaled, 1)
                        pool.wait_ge(scaled, 2 * (e + 1) + 1)
                    copy(pool, w1s[b][0][:], w1_in[:], one).then_inc(split, 1)
                    copy(pool, w2s[b][0][:], w2_in[:], one).then_inc(split, 1)
                    pool.wait_ge(split, 4 * e + 2 + 1)
                    pool.tensor_tensor(w1s[b][1][:], w1_in[:], w1s[b][0][:], ALU.subtract).then_inc(split, 1)
                    pool.tensor_tensor(w2s[b][1][:], w2_in[:], w2s[b][0][:], ALU.subtract).then_inc(split, 1)

                prepare(0, 0)
                prepare(0, 1)
                with pool.Fori(1, E // 2) as i:
                    prepare(i, 0)
                    prepare(i, 1)

            @block.tensor
            def _(pe):
                if norm:
                    pe.wait_ge(small_in, 48 + 1)
                with pe.Fori(0, E // 2) as i:
                    for b in range(2):
                        e = 2 * i + b
                        if norm:
                            pe.wait_ge(w_in, 32 * (e + 1) + 1)
                            pe.wait_ge(bias_ready, e + 1)
                            for m in range(MT):
                                for k in range(CT):
                                    mm = pe.matmul(bias_ps[:, m:m + 1], w1_in[:, k, m * P:(m + 1) * P],
                                                   b_all[:, ds(e, 1), k], start=k == 0, stop=k == CT - 1)
                            mm.then_inc(bias_made, 1)
                        with pe.Fori(0, NCH // 2) as j:
                            pe.wait_ge(split, 4 * (e + 1) + 1)
                            for s in range(2):
                                c = e * NCH + 2 * j + s
                                chunk = ds((2 * j + s) * CH, CH)
                                for m in range(MT):
                                    pe.wait_ge(h_ready, 2 * MT * (e * (NCH // 2) + j) + 1) if s * MT + m < HR else \
                                        pe.wait_ge(h_ready, c * MT + m + 1 - HR + 1)
                                    for k in range(CT):
                                        mm = split_matmul(pe, h_ps[:, m % HR, 0:CH] if MT >= HR else h_ps[:, s * MT + m, 0:CH],
                                                          w1s[b][0][:, k, m * P:(m + 1) * P], w1s[b][1][:, k, m * P:(m + 1) * P],
                                                          xh[:, k, chunk], xl[:, k, chunk], k == 0, k == CT - 1)
                                    mm.then_inc(h_made, 1)
                            for s in range(2):
                                c = e * NCH + 2 * j + s
                                pe.wait_ge(h_split, (c + 1) * MT + 1)
                                for t in range(SUB):
                                    pe.wait_ge(y_taken, c * SUB + 1)
                                    tok = slice(t * P, (t + 1) * P)
                                    for m in range(MT):
                                        pe.matmul(y_ps[:, t, 0:C], hh[:, s, m, tok], w2s[b][0][:, m, :], start=m == 0, stop=False)
                                        pe.matmul(y_ps[:, t, 0:C], hl[:, s, m, tok], w2s[b][0][:, m, :], start=False, stop=False)
                                        mm = pe.matmul(y_ps[:, t, 0:C], hh[:, s, m, tok], w2s[b][1][:, m, :],
                                                       start=False, stop=m == MT - 1)
                                    mm.then_inc(y_made, 1)

            @block.scalar
            def _(act):
                act.wait_ge(small_in, (48 if norm else 16) + 1)
                with act.Fori(0, E // 2) as i:
                    for b in range(2):
                        e = 2 * i + b
                        act.wait_ge(bias_ready, e + 2)
                        with act.Fori(0, NCH // 2) as j:
                            for s in range(2):
                                c = e * NCH + 2 * j + s
                                for m in range(MT):
                                    act.wait_ge(h_made, c * MT + m + 2)
                                    act.wait_ge(h_split, c * MT + m - 1 + 1) if (s or m >= 2) else \
                                        act.wait_ge(h_split, 2 * MT * (e * (NCH // 2) + j) + 1)
                                    bank = h_ps[:, m % HR, 0:CH] if MT >= HR else h_ps[:, s * MT + m, 0:CH]
                                    act.activation(h32[:, m % 2], bank, ACT.Gelu,
                                                   bias=bias1[:, b, m:m + 1]).then_inc(h_ready, 1)

            @block.vector
            def _(dve):
                dve.memset(acc[:], 0.0).then_inc(zeroed, 1)
                dve.wait_ge(zeroed, 1 + 1)
                dve.wait_ge(small_in, (48 if norm else 16) + 1)
                with dve.Fori(0, E // 2) as i:
                    for b in range(2):
                        e = 2 * i + b
                        if norm:
                            dve.wait_ge(bias_made, e + 2)
                            dve.tensor_tensor(bias1[:, b], bias_ps[:, 0:MT], b1_all[:, ds(e, 1), :].rearrange("p e m -> p (e m)"),
                                              ALU.add).then_inc(bias_ready, 1)
                        else:
                            dve.tensor_copy(bias1[:, b], b1_all[:, ds(e, 1), :].rearrange("p e m -> p (e m)")).then_inc(bias_ready, 1)
                        with dve.Fori(0, NCH // 2) as j:
                            dve.wait_ge(b2_in[b], 16 * (i + 1) + 1)
                            for s in range(2):
                                c = e * NCH + 2 * j + s
                                dve.wait_ge(y_made, 2 * SUB * (e * (NCH // 2) + j) + 1)
                                for m in range(MT):
                                    dve.wait_ge(h_ready, c * MT + m + 2)
                                    dve.tensor_copy(hh[:, s, m], h32[:, m % 2]).then_inc(h_hi, 1)
                                    dve.wait_ge(h_hi, c * MT + m + 2)
                                    dve.tensor_tensor(hl[:, s, m], h32[:, m % 2], hh[:, s, m],
                                                      ALU.subtract).then_inc(h_split, 1)
                            for s in range(2):
                                c = e * NCH + 2 * j + s
                                for t in range(SUB):
                                    dve.wait_ge(y_made, c * SUB + t + 2)
                                    dve.tensor_tensor(y_one[:, t], y_ps[:, t, 0:C], b2_row[:, b], ALU.add).then_inc(y_taken, 1)
                                    dve.wait_ge(y_taken, c * SUB + t + 2)
                                    tile = ds((2 * j + s) * SUB + t, 1)
                                    weight = comb[:, tile, ds(e, 1)].rearrange("p t e -> p (t e)")
                                    mine = acc[:, tile, :].rearrange("p t c -> p (t c)")
                                    dve.scalar_tensor_tensor(out=mine, in0=y_one[:, t], scalar=weight, in1=mine,
                                                             op0=ALU.mult, op1=ALU.add).then_inc(y_added, 1)
        core.end_phase()
        add_tokens(core, x_cm, acc, ident)
        core.end_phase()


def add_tokens(core, x_cm, acc, ident):
    nc = core.nc
    with ExitStack() as ctx:
        stage = core.sb(ctx, "stage", [P, 2, SUB, C])
        t_ps = core.ps(ctx, "t_ps", [P, 2, CT, 512])
        staged, turned, added = core.sem("staged"), core.sem("turned"), core.sem("added")
        block = ctx.enter_context(core.block())

        @block.scalar
        def _(act):
            with act.Fori(0, NCH // 2) as i:
                for b in range(2):
                    act.wait_ge(turned, 2 * i + 1)
                    act.activation(stage[:, b], acc[:, ds((2 * i + b) * SUB, SUB), :], ACT.Copy).then_inc(staged, 1)

        @block.tensor
        def _(pe):
            with pe.Fori(0, NCH // 2) as i:
                for b in range(2):
                    pe.wait_ge(staged, 2 * i + b + 2)
                    pe.wait_ge(added, 2 * i + 1)
                    for t in range(SUB):
                        for k in range(CT):
                            mm = pe.transpose(t_ps[:, b, k, t * P:(t + 1) * P], stage[:, b, t, k * P:(k + 1) * P], ident[:])
                    mm.then_inc(turned, 1)

        @block.vector
        def _(dve):
            with dve.Fori(0, NCH // 2) as i:
                for b in range(2):
                    dve.wait_ge(turned, 2 * i + b + 2)
                    x = x_cm[:, :, ds((2 * i + b) * CH, CH)]
                    dve.tensor_tensor(x, t_ps[:, b, :, 0:CH], x, ALU.add).then_inc(added, 1)


def metaformer(nc, ins, out):
    with ExitStack() as keep:
        core = Core(nc, keep)
        qk_dram = nc.dram_tensor("qk_scratch", [2, 2 * C, T], F16, kind="Internal").ap()
        v_dram = nc.dram_tensor("v_scratch", [T, C], F32, kind="Internal").ap()
        o_dram = nc.dram_tensor("o_scratch", [3, C, T], F32, kind="Internal").ap()
        x_cm = core.sb(keep, "x_cm", [P, CT, T])
        ones = core.sb(keep, "ones", [P, P])
        ones32 = core.sb(keep, "ones32", [P, HD])
        ident = core.sb(keep, "ident", [P, P])
        iota = core.sb(keep, "iota", [P, E])
        eps5, eps6 = core.sb(keep, "eps5", [P, 1]), core.sb(keep, "eps6", [P, 1])
        small = {}
        for name, shape in (("b_proj", [P, CT]), ("b_out", [P, CT]), ("b_tap", [P, CT]), ("w_tap", [P, CT, 9]),
                            ("br", [P, E])):
            small[name] = core.sb(keep, name, shape)

        loaded, const_set, ident_zero = core.sem("loaded"), core.sem("const_set"), core.sem("ident_zero")
        with core.block() as block:
            @block.sync
            def _(sp):
                for b in range(B):
                    for k in range(CT):
                        sp.dma_start(x_cm[:, k, b * N:(b + 1) * N], ins["x"][b, k * P:(k + 1) * P, :]).then_inc(loaded, 16)
                for name, src in (("b_proj", "L0_conv_b_proj"), ("b_out", "L1_conv_bout"), ("b_tap", "L0_conv_b_lepe")):
                    sp.dma_start(small[name][:], ins[src]).then_inc(loaded, 16)
                sp.dma_start(small["w_tap"][:], ins["L0_conv_w_lepe"]).then_inc(loaded, 16)
                sp.dma_start(small["br"][:], ins["L0_ffn_br"].broadcast_to([P, E])).then_inc(loaded, 16)
                sp.wait_ge(loaded, 16 * 9 + 1)

            @block.gpsimd
            def _(pool):
                pool.memset(ones[:], 1.0 / C).then_inc(const_set, 1)
                pool.memset(ones32[:], 1.0).then_inc(const_set, 1)
                pool.memset(eps5[:], 1e-5).then_inc(const_set, 1)
                pool.memset(eps6[:], 1e-6).then_inc(const_set, 1)
                pool.memset(ident[:], 0.0).then_inc(ident_zero, 1)
                pool.wait_ge(ident_zero, 1 + 1)
                pool.affine_select(out=ident[:], in_=ident[:], compare_op=ALU.not_equal, fill=1.0, base=0,
                                   pattern=[[-1, P]], channel_multiplier=1).then_inc(const_set, 1)
                pool.iota(iota[:], pattern=[[1, E]], base=0, channel_multiplier=0,
                          allow_small_or_imprecise_dtypes=True).then_inc(const_set, 1)

        core.end_phase()

        with ExitStack() as ctx:
            v_cm = core.sb(ctx, "v_cm", [P, CT, T])
            with ExitStack() as proj:
                xh, xl = core.sb(proj, "xh", [P, CT, T], F16), core.sb(proj, "xl", [P, CT, T], F16)
                wqk = [core.sb(proj, "wqk", [P, 4 * CT * P], F16) for _ in range(2)]
                wv = [core.sb(proj, "wv", [P, CT, C], F16) for _ in range(2)]
                split_weights(core, [(ins["w_qk0"], wqk[0][:], wqk[1][:]), (ins["w_v0"], wv[0][:], wv[1][:])])
                core.end_phase()
                layer_norm(core, x_cm, xh, xl, ones, eps6)
                core.end_phase()
                project(core, xh, xl, wqk, wv, qk_dram, v_dram, v_cm, sigmoid=False)
                core.end_phase()
            out_cm = core.sb(ctx, "out_cm", [P, CT * T])
            softmax_attention(core, qk_dram, v_dram, v_cm, small["w_tap"], small["b_tap"], out_cm, ones32, ident)
            core.end_phase()
            weight = core.sb(ctx, "w_proj", [P, CT, C])
            load_weight(core, weight, ins["w_proj"])
            core.end_phase()
            project_out(core, x_cm, weight, small["b_proj"], CT, o_cm=out_cm[:].rearrange("p (k t) -> p k t", k=CT))
            core.end_phase()

        with ExitStack() as ctx:
            comb = core.sb(ctx, "comb", [P, TT, E])
            xh, xl = core.sb(ctx, "xh", [P, CT, T], F16), core.sb(ctx, "xl", [P, CT, T], F16)
            with ExitStack() as inner:
                t32 = core.sb(inner, "t32", [P, CT, T])
                wr = [core.sb(inner, "wr", [P, CT, E], F16) for _ in range(2)]
                split_weights(core, [(ins["w_r0"], wr[0][:], wr[1][:])])
                core.end_phase()
                layer_norm(core, x_cm, xh, xl, ones, eps5, keep32=t32, one=ones32[:, 0:1])
                core.end_phase()
                route(core, xh, xl, wr, small["br"][:], comb, iota)
                core.end_phase()
                layer_norm(core, t32, xh, xl, ones, eps5)
                core.end_phase()
            experts(core, x_cm, xh, xl, comb, ins["L0_ffn_W1"], ins["L0_ffn_b1"], ins["L0_ffn_W2"], ins["L0_ffn_b2"],
                    1024, ident, ones32[:, 0:1], ins["L0_ffn_ln_g"], ins["L0_ffn_ln_b"])

        with ExitStack() as ctx:
            with ExitStack() as proj:
                xh, xl = core.sb(proj, "xh", [P, CT, T], F16), core.sb(proj, "xl", [P, CT, T], F16)
                wqk = [core.sb(proj, "wqk", [P, 4 * CT * P], F16) for _ in range(2)]
                wv = [core.sb(proj, "wv", [P, CT, C], F16) for _ in range(2)]
                split_weights(core, [(ins["w_qk1"], wqk[0][:], wqk[1][:]), (ins["w_v1"], wv[0][:], wv[1][:])])
                core.end_phase()
                layer_norm(core, x_cm, xh, xl, ones, eps6)
                core.end_phase()
                project(core, xh, xl, wqk, wv, qk_dram, v_dram, None, sigmoid=True)
                core.end_phase()
            window_attention(core, qk_dram, v_dram, ins["masks"], o_dram, ones32)
            core.end_phase()
            weight = core.sb(ctx, "w_out", [P, 3 * CT, C])
            load_weight(core, weight, ins["w_out"])
            core.end_phase()
            project_out(core, x_cm, weight, small["b_out"], 3 * CT, o_dram=o_dram.rearrange("w c t -> (w c) t"))
            core.end_phase()

        with ExitStack() as ctx:
            comb = core.sb(ctx, "comb", [P, TT, E])
            xh, xl = core.sb(ctx, "xh", [P, CT, T], F16), core.sb(ctx, "xl", [P, CT, T], F16)
            with ExitStack() as inner:
                wr = [core.sb(inner, "wr", [P, CT, E], F16) for _ in range(2)]
                split_weights(core, [(ins["w_r1"], wr[0][:], wr[1][:])])
                core.end_phase()
                layer_norm(core, x_cm, xh, xl, ones, eps5, add_back=True)
                core.end_phase()
                route(core, xh, xl, wr, None, comb, iota)
                core.end_phase()
            experts(core, x_cm, xh, xl, comb, ins["L1_ffn_w1"], ins["L1_ffn_b1"], ins["L1_ffn_w2"], ins["L1_ffn_b2"],
                    256, ident, ones32[:, 0:1])

        stored = core.sem("stored")
        with core.block() as block:
            @block.sync
            def _(sp):
                for b in range(B):
                    for k in range(CT):
                        sp.dma_start(out[b, k * P:(k + 1) * P, :], x_cm[:, k, b * N:(b + 1) * N]).then_inc(stored, 16)
                sp.wait_ge(stored, 64 + 1)


def load_weight(core, dst, src):
    loaded = core.sem("weight_loaded")
    with core.block() as block:
        @block.sync
        def _(sp):
            sp.dma_start(dst[:], src).then_inc(loaded, 16)
            sp.wait_ge(loaded, 16 + 1)


def window_masks(np):
    tiles = []
    for w in WINDOWS:
        for delta, sub in window_parts(w):
            key = sub * P + np.arange(P)
            query = np.arange(CH)
            dy = (key // HW)[:, None] + 8 * delta - (query // HW)[None, :]
            dx = (key % HW)[:, None] - (query % HW)[None, :]
            seen = (dy >= -(w // 2)) & (dy < w // 2) & (dx >= -(w // 2)) & (dx < w // 2)
            tiles.append(seen.astype(np.float16))
    return np.ascontiguousarray(np.stack(tiles, 1))


def kernel(**inputs):
    import numpy as np
    import concourse.bacc as bacc
    from concourse.bass_utils import run_bass_kernel_spmd as run

    a = {k: np.asarray(v) for k, v in inputs.items()}

    def tiled(w):
        return np.ascontiguousarray(w.reshape(-1, P, w.shape[1]).transpose(1, 0, 2))

    def by_channel(v):
        return np.ascontiguousarray(np.moveaxis(v.reshape(*v.shape[:-1], -1, P), -1, 0))

    def by_tile(q, k):
        both = np.concatenate([q, k], 1).reshape(CT, P, 4, P)
        return np.ascontiguousarray(both.transpose(1, 2, 0, 3).reshape(P, 4 * CT * P))

    qkv = a["L0_conv_w_qkv"].reshape(HEADS, 3, HD, C)
    q0, k0, v0 = (qkv[:, i].reshape(C, C).T for i in range(3))
    arrays = {
        "x": a["x"].reshape(B, C, N),
        "w_qk0": by_tile(q0, k0), "w_v0": tiled(v0),
        "w_proj": tiled(a["L0_conv_w_proj"].T), "L0_conv_b_proj": by_channel(a["L0_conv_b_proj"]),
        "L0_conv_w_lepe": tiled(a["L0_conv_w_lepe"].reshape(C, 9)), "L0_conv_b_lepe": by_channel(a["L0_conv_b_lepe"]),
        "w_r0": tiled(a["L0_ffn_Wr"]), "L0_ffn_br": a["L0_ffn_br"].reshape(1, E),
        "w_qk1": by_tile(a["L1_conv_Wq"].T, a["L1_conv_Wk"].T), "w_v1": tiled(a["L1_conv_Wv"].T),
        "w_out": tiled(a["L1_conv_Wout"].T), "L1_conv_bout": by_channel(a["L1_conv_bout"]),
        "w_r1": tiled(a["L1_ffn_router_w"].T),
        "masks": window_masks(np),
    }
    for name in ("L0_ffn_ln_g", "L0_ffn_ln_b", "L0_ffn_W1", "L0_ffn_b1", "L0_ffn_W2", "L0_ffn_b2",
                 "L1_ffn_w1", "L1_ffn_b1", "L1_ffn_w2", "L1_ffn_b2"):
        arrays[name] = by_channel(a[name]) if name.endswith(("ln_g", "ln_b", "b1")) else a[name]
    arrays = {k: np.ascontiguousarray(v) for k, v in arrays.items()}

    nc = bacc.Bacc("TRN2", target_bir_lowering=False, num_devices=1)
    ins = {k: nc.dram_tensor(f"in_{k}", v.shape, mybir.dt.from_np(v.dtype), kind="ExternalInput").ap()
           for k, v in arrays.items()}
    out = nc.dram_tensor("out", [B, C, N], F32, kind="ExternalOutput").ap()
    metaformer(nc, ins, out)
    r = run(nc, [{f"in_{k}": v for k, v in arrays.items()}], core_ids=[0])
    return r.results[0]["out"].reshape(B, C, HW, HW)
```

```python
from contextlib import ExitStack

import concourse.bass as bass
from concourse import mybir

F32 = mybir.dt.float32
F16 = mybir.dt.float16
ALU = mybir.AluOpType
ACT = mybir.ActivationFunctionType
AX = mybir.AxisListType
ds = bass.ds

P = 128
B, C, HW = 2, 256, 48
N = HW * HW
T = B * N
CT = C // P
HEADS, HD = 8, 32
CH = 8 * HW
NCH = T // CH
QC = N // CH
KT = N // P
TT = T // P
SUB = CH // P
PAIRS = B * HEADS // 2
SCALE = float(HD) ** -0.5
E = 8
WINDOWS = (48, 24, 12)
PADK = 3 * HD + 1


class Core:

    def __init__(self, nc, keep):
        self.nc, self.keep, self.n, self.phase = nc, keep, 0, []

    def sem(self, name):
        self.n += 1
        self.phase.append(self.nc.alloc_semaphore(name=f"{name}_{self.n}"))
        return self.phase[-1]

    def block(self):
        with self.nc.Block() as block:
            @block.sync
            def _(sp):
                for sem in self.phase:
                    sp.sem_inc(sem, 1)
        return self.nc.Block()

    def end_phase(self):
        with self.nc.Block() as block:
            @block.sync
            def _(sp):
                for sem in self.phase:
                    sp.sem_clear(sem)
        for sem in self.phase:
            self.nc.release_semaphore(sem)
        self.phase.clear()

    def sb(self, ctx, name, shape, dt=F32):
        self.n += 1
        return ctx.enter_context(self.nc.sbuf_tensor(f"{name}_{self.n}", shape, dt))

    def ps(self, ctx, name, shape, dt=F32):
        self.n += 1
        return ctx.enter_context(self.nc.psum_tensor(f"{name}_{self.n}", shape, dt))


def copy(pool, out, src, one):
    return pool.tensor_tensor(out, src, one.unsqueeze(2).broadcast_to(list(src.shape)), ALU.mult)


def split_matmul(pe, out, w_hi, w_lo, x_hi, x_lo, first, last):
    pe.matmul(out, w_hi, x_hi, start=first, stop=False)
    pe.matmul(out, w_hi, x_lo, start=False, stop=False)
    return pe.matmul(out, w_lo, x_hi, start=False, stop=last)


def layer_norm(core, src, hi, lo, ones, eps_tile, keep32=None, add_back=False, one=None):
    nc = core.nc
    with ExitStack() as ctx:
        centred = core.sb(ctx, "centred", [P, 2, CT, CH])
        square = core.sb(ctx, "square", [P, 2, CT, CH])
        std = core.sb(ctx, "std", [P, 2, CH])
        rstd = core.sb(ctx, "rstd", [P, 2, CH])
        mean_ps = core.ps(ctx, "mean_ps", [P, 2, 512])
        var_ps = core.ps(ctx, "var_ps", [P, 2, 512])
        mean_ready, centred_ready, square_ready, var_ready, std_ready, rstd_ready, norm_ready, hi_ready, lo_ready, back_ready = (
            core.sem(n) for n in ("mean_ready", "centred_ready", "square_ready", "var_ready", "std_ready",
                                  "rstd_ready", "norm_ready", "hi_ready", "lo_ready", "back_ready"))
        block = ctx.enter_context(core.block())

        @block.tensor
        def _(pe):
            with pe.Fori(0, NCH // 2) as i:
                for b in range(2):
                    pe.wait_ge(centred_ready, 2 * i + 1)
                    for c in range(CT):
                        mm = pe.matmul(mean_ps[:, b, 0:CH], ones[:], src[:, c, ds((2 * i + b) * CH, CH)],
                                       start=c == 0, stop=c == CT - 1)
                    mm.then_inc(mean_ready, 1)
                for b in range(2):
                    pe.wait_ge(square_ready, 2 * i + b + 2)
                    pe.wait_ge(std_ready, 2 * i + 1)
                    for c in range(CT):
                        mm = pe.matmul(var_ps[:, b, 0:CH], ones[:], square[:, b, c, :],
                                       start=c == 0, stop=c == CT - 1)
                    mm.then_inc(var_ready, 1)

        @block.vector
        def _(dve):
            with dve.Fori(0, NCH // 2) as i:
                for b in range(2):
                    dve.wait_ge(mean_ready, 2 * i + b + 2)
                    dve.wait_ge(lo_ready, 2 * i + 1)
                    dve.wait_ge(hi_ready, 2 * i + 1)
                    if keep32 is not None or add_back:
                        dve.wait_ge(back_ready, 2 * i + 1)
                    dve.tensor_tensor(centred[:, b], src[:, :, ds((2 * i + b) * CH, CH)],
                                      mean_ps[:, b, 0:CH].unsqueeze(1).broadcast_to([P, CT, CH]),
                                      ALU.subtract).then_inc(centred_ready, 1)
                for b in range(2):
                    dve.wait_ge(std_ready, 2 * i + b + 2)
                    dve.reciprocal(rstd[:, b], std[:, b]).then_inc(rstd_ready, 1)
                    dve.wait_ge(rstd_ready, 2 * i + b + 2)
                    dve.wait_ge(square_ready, 2 * i + b + 2)
                    dve.tensor_tensor(centred[:, b], centred[:, b],
                                      rstd[:, b].unsqueeze(1).broadcast_to([P, CT, CH]),
                                      ALU.mult).then_inc(norm_ready, 1)

        @block.scalar
        def _(act):
            with act.Fori(0, NCH // 2) as i:
                for b in range(2):
                    act.wait_ge(centred_ready, 2 * i + b + 2)
                    act.wait_ge(var_ready, 2 * i + 1)
                    act.activation(square[:, b], centred[:, b], ACT.Square).then_inc(square_ready, 1)
                for b in range(2):
                    act.wait_ge(var_ready, 2 * i + b + 2)
                    act.wait_ge(rstd_ready, 2 * i + 1)
                    act.activation(std[:, b], var_ps[:, b, 0:CH], ACT.Sqrt, bias=eps_tile[:, 0:1]).then_inc(std_ready, 1)
                for b in range(2):
                    act.wait_ge(norm_ready, 2 * i + b + 2)
                    act.activation(hi[:, :, ds((2 * i + b) * CH, CH)], centred[:, b], ACT.Copy).then_inc(hi_ready, 1)

        @block.gpsimd
        def _(pool):
            with pool.Fori(0, NCH // 2) as i:
                for b in range(2):
                    chunk = ds((2 * i + b) * CH, CH)
                    if keep32 is not None:
                        pool.wait_ge(norm_ready, 2 * i + b + 2)
                        copy(pool, keep32[:, :, chunk], centred[:, b], one).then_inc(back_ready, 1)
                    if add_back:
                        pool.wait_ge(norm_ready, 2 * i + b + 2)
                        pool.tensor_tensor(src[:, :, chunk], src[:, :, chunk], centred[:, b],
                                           ALU.add).then_inc(back_ready, 1)
                    pool.wait_ge(hi_ready, 2 * i + b + 2)
                    pool.tensor_tensor(lo[:, :, chunk], centred[:, b], hi[:, :, chunk],
                                       ALU.subtract).then_inc(lo_ready, 1)


def split_weights(core, pairs):
    nc = core.nc
    with ExitStack() as ctx:
        stages = [core.sb(ctx, "stage", list(src.shape)) for src, _, _ in pairs]
        loaded = [core.sem("loaded") for _ in pairs]
        hi_ready, lo_ready = core.sem("w_hi_ready"), core.sem("w_lo_ready")
        block = ctx.enter_context(core.block())

        @block.sync
        def _(sp):
            for (src, _, _), stage, ready in zip(pairs, stages, loaded):
                sp.dma_start(stage[:], src).then_inc(ready, 16)

        @block.scalar
        def _(act):
            for (_, hi, _), stage, ready in zip(pairs, stages, loaded):
                act.wait_ge(ready, 16 + 1)
                act.activation(hi, stage[:], ACT.Copy).then_inc(hi_ready, 1)

        @block.vector
        def _(dve):
            for n, ((_, hi, lo), stage) in enumerate(zip(pairs, stages)):
                dve.wait_ge(hi_ready, n + 2)
                dve.tensor_tensor(lo, stage[:], hi, ALU.subtract).then_inc(lo_ready, 1)


def project(core, xh, xl, wqk, wv, qk_dram, v_dram, v_cm, sigmoid, k_tok=None):
    nc = core.nc
    wqk_hi, wqk_lo = wqk
    wv_hi, wv_lo = wv
    with ExitStack() as ctx:
        hi = core.sb(ctx, "qk_hi", [P, 2, 4, CH], F16)
        lo = core.sb(ctx, "qk_lo", [P, 2, 4, CH], F16)
        gate = core.sb(ctx, "gate", [P, 2, 4, CH])
        v_tok = core.sb(ctx, "v_tok", [P, 2, SUB, C])
        qk_ps = core.ps(ctx, "qk_ps", [P, 4, 512])
        v_ps = core.ps(ctx, "v_ps", [P, 2, 512])
        vt_ps = core.ps(ctx, "vt_ps", [P, 2, 512])
        qk_made, vcm_made, vt_made = core.sem("qk_made"), core.sem("vcm_made"), core.sem("vt_made")
        gated, hi_ready, lo_ready = core.sem("gated"), core.sem("hi_ready"), core.sem("lo_ready")
        vcm_taken, vt_taken = core.sem("vcm_taken"), core.sem("vt_taken")
        v_squared, v_summed, v_rooted, v_guarded, v_inverted, v_ready = (
            core.sem(n) for n in ("v_squared", "v_summed", "v_rooted", "v_guarded", "v_inverted", "v_ready"))
        hi_stored = [core.sem("hi_stored") for _ in range(2)]
        lo_stored = [core.sem("lo_stored") for _ in range(2)]
        v_stored = [core.sem("v_stored") for _ in range(2)]
        v_sq = core.sb(ctx, "v_sq", [P, SUB, C])
        v_ss = core.sb(ctx, "v_ss", [P, SUB, HEADS])
        v_norm = core.sb(ctx, "v_norm", [P, SUB, HEADS])
        v_guard = core.sb(ctx, "v_guard", [P, SUB, HEADS])
        v_inv = core.sb(ctx, "v_inv", [P, SUB, HEADS])
        k_gate = core.sb(ctx, "k_gate", [P, 2, SUB, C])
        kt_made, kt_gated, kt_hi, kt_lo = (core.sem(n) for n in ("kt_made", "kt_gated", "kt_hi", "kt_lo"))
        block = ctx.enter_context(core.block())

        @block.tensor
        def _(pe):
            with pe.Fori(0, NCH) as c:
                chunk = ds(c * CH, CH)
                for m in range(4):
                    pe.wait_ge(lo_ready, 4 * c + 1)
                    for k in range(CT):
                        w = ds((m * CT + k) * P, P)
                        mm = split_matmul(pe, qk_ps[:, m, 0:CH], wqk_hi[:, w], wqk_lo[:, w],
                                          xh[:, k, chunk], xl[:, k, chunk], k == 0, k == CT - 1)
                    mm.then_inc(qk_made, 1)
                if v_cm is not None:
                    for m in range(CT):
                        pe.wait_ge(vcm_taken, 2 * c + 1)
                        for k in range(CT):
                            mm = split_matmul(pe, v_ps[:, m, 0:CH], wv_hi[:, k, m * P:(m + 1) * P],
                                              wv_lo[:, k, m * P:(m + 1) * P], xh[:, k, chunk], xl[:, k, chunk],
                                              k == 0, k == CT - 1)
                        mm.then_inc(vcm_made, 1)
                if k_tok is not None:
                    for t in range(SUB):
                        pe.wait_ge(kt_gated, 2 * c + 1)
                        out = v_ps[:, t // 2, (t % 2) * C:(t % 2 + 1) * C].rearrange("p (m c) -> p m c", m=CT)
                        tok = ds(c * CH + t * P, P)
                        for k in range(CT):
                            half = [w[:].rearrange("p (m k c) -> p m k c", k=CT, c=P)[:, CT:2 * CT, k, :] for w in (wqk_hi, wqk_lo)]
                            pe.matmul(out, xh[:, k, tok], half[0], start=k == 0, stop=False)
                            pe.matmul(out, xl[:, k, tok], half[0], start=False, stop=False)
                            mm = pe.matmul(out, xh[:, k, tok], half[1], start=False, stop=k == CT - 1)
                        mm.then_inc(kt_made, 1)
                for t in range(SUB):
                    pe.wait_ge(vt_taken, 2 * c + 1)
                    out = vt_ps[:, t // 2, (t % 2) * C:(t % 2 + 1) * C]
                    tok = ds(c * CH + t * P, P)
                    for k in range(CT):
                        pe.matmul(out, xh[:, k, tok], wv_hi[:, k, :], start=k == 0, stop=False)
                        pe.matmul(out, xl[:, k, tok], wv_hi[:, k, :], start=False, stop=False)
                        mm = pe.matmul(out, xh[:, k, tok], wv_lo[:, k, :], start=False, stop=k == CT - 1)
                    mm.then_inc(vt_made, 1)

        @block.scalar
        def _(act):
            with act.Fori(0, NCH // 2) as i:
                for b in range(2):
                    c = 2 * i + b
                    act.wait_ge(hi_stored[b], 16 * i + 1)
                    if sigmoid:
                        act.wait_ge(lo_ready, 8 * i + 1)
                    for m in range(4):
                        act.wait_ge(qk_made, 4 * c + m + 2)
                        if sigmoid:
                            act.activation(gate[:, b, m], qk_ps[:, m, 0:CH], ACT.Sigmoid).then_inc(gated, 1)
                            act.wait_ge(gated, 4 * c + m + 2)
                            act.activation(hi[:, b, m], gate[:, b, m], ACT.Copy).then_inc(hi_ready, 1)
                        else:
                            act.activation(hi[:, b, m], qk_ps[:, m, 0:CH], ACT.Copy).then_inc(hi_ready, 1)
                    if v_cm is not None:
                        for m in range(CT):
                            act.wait_ge(vcm_made, 2 * c + m + 2)
                            act.activation(v_cm[:, m, ds(c * CH, CH)], v_ps[:, m, 0:CH],
                                           ACT.Copy).then_inc(vcm_taken, 1)
                    if k_tok is not None:
                        act.wait_ge(kt_made, 3 * c + 4)
                        act.wait_ge(kt_lo, 2 * i + 1)
                        act.activation(k_gate[:, b, 0:2].rearrange("p t c -> p (t c)"), v_ps[:, 0, :],
                                       ACT.Sigmoid).then_inc(kt_gated, 1)
                        act.activation(k_gate[:, b, 2], v_ps[:, 1, 0:C], ACT.Sigmoid).then_inc(kt_gated, 1)
                        act.wait_ge(kt_gated, 2 * c + 3)
                        act.activation(k_tok[0][:, ds(c * SUB, SUB), :], k_gate[:, b], ACT.Copy).then_inc(kt_hi, 1)
                    if sigmoid:
                        act.wait_ge(v_summed, c + 2)
                        act.activation(v_norm[:], v_ss[:], ACT.Sqrt).then_inc(v_rooted, 1)

        @block.vector
        def _(dve):
            with dve.Fori(0, NCH // 2) as i:
                for b in range(2):
                    c = 2 * i + b
                    dve.wait_ge(lo_stored[b], 16 * i + 1)
                    for m in range(4):
                        dve.wait_ge(hi_ready, 4 * c + m + 2)
                        whole = gate[:, b, m] if sigmoid else qk_ps[:, m, 0:CH]
                        dve.tensor_tensor(lo[:, b, m], whole, hi[:, b, m], ALU.subtract).then_inc(lo_ready, 1)
                    dve.wait_ge(v_stored[b], 16 * i + 1)
                    dve.wait_ge(vt_made, 3 * c + 3 + 1)
                    dve.tensor_copy(v_tok[:, b, 0:2].rearrange("p t c -> p (t c)"), vt_ps[:, 0, :]).then_inc(vt_taken, 1)
                    dve.tensor_copy(v_tok[:, b, 2], vt_ps[:, 1, 0:C]).then_inc(vt_taken, 1)
                    if sigmoid:
                        dve.wait_ge(vt_taken, 2 * c + 2 + 1)
                        dve.tensor_tensor(v_sq[:], v_tok[:, b], v_tok[:, b], ALU.mult).then_inc(v_squared, 1)
                        dve.wait_ge(v_squared, c + 2)
                        dve.tensor_reduce(v_ss[:], v_sq[:].rearrange("p t (h d) -> p t h d", h=HEADS), AX.X,
                                          ALU.add).then_inc(v_summed, 1)
                        dve.wait_ge(v_rooted, c + 2)
                        dve.tensor_scalar(v_guard[:], v_norm[:], 1e-12, None, ALU.max).then_inc(v_guarded, 1)
                        dve.wait_ge(v_guarded, c + 2)
                        dve.reciprocal(v_inv[:], v_guard[:]).then_inc(v_inverted, 1)
                        dve.wait_ge(v_inverted, c + 2)
                        heads = v_tok[:, b].rearrange("p t (h d) -> p (t h) d", h=HEADS)
                        dve.tensor_tensor(heads, heads,
                                          v_inv[:].rearrange("p t h -> p (t h)").unsqueeze(2).broadcast_to([P, SUB * HEADS, HD]),
                                          ALU.mult).then_inc(v_ready, 1)

        @block.gpsimd
        def _(pool):
            if k_tok is not None:
                with pool.Fori(0, NCH // 2) as i:
                    for b in range(2):
                        c = 2 * i + b
                        pool.wait_ge(kt_hi, c + 2)
                        pool.tensor_tensor(k_tok[1][:, ds(c * SUB, SUB), :], k_gate[:, b],
                                           k_tok[0][:, ds(c * SUB, SUB), :], ALU.subtract).then_inc(kt_lo, 1)

        @block.sync
        def _(sp):
            with sp.Fori(0, NCH // 2) as i:
                for b in range(2):
                    c = 2 * i + b
                    chunk = ds(c * CH, CH)
                    sp.wait_ge(hi_ready, 4 * c + 4 + 1)
                    sp.dma_start(qk_dram[0, :, chunk].rearrange("(m p) t -> p m t", p=P), hi[:, b]).then_inc(hi_stored[b], 16)
                    sp.wait_ge(lo_ready, 4 * c + 4 + 1)
                    sp.dma_start(qk_dram[1, :, chunk].rearrange("(m p) t -> p m t", p=P), lo[:, b]).then_inc(lo_stored[b], 16)
                    if sigmoid:
                        sp.wait_ge(v_ready, c + 2)
                    else:
                        sp.wait_ge(vt_taken, 2 * c + 2 + 1)
                    sp.dma_start(v_dram[chunk, :].rearrange("(t p) c -> p t c", p=P), v_tok[:, b]).then_inc(v_stored[b], 16)
            for b in range(2):
                for s in (hi_stored[b], lo_stored[b], v_stored[b]):
                    sp.wait_ge(s, 16 * (NCH // 2) + 1)


def softmax_attention(core, qk_dram, v_dram, v_cm, w_tap, b_tap, out_cm, ones32, ident):
    nc = core.nc
    with ExitStack() as ctx:
        qs = [core.sb(ctx, "qs", [PADK, 2, N], F16) for _ in range(2)]
        ks = [core.sb(ctx, "ks", [PADK, 2, N], F16) for _ in range(2)]
        vs = [core.sb(ctx, "vs", [P, KT, 2 * HD]) for _ in range(2)]
        prob = core.sb(ctx, "prob", [P, 3, 2, CH])
        part_max = core.sb(ctx, "part_max", [P, 2, KT, 3])
        row_max = core.sb(ctx, "row_max", [P, 2, KT])
        neg_max = core.sb(ctx, "neg_max", [2 * KT, P], F16)
        summed = core.sb(ctx, "summed", [P, CH])
        rden = core.sb(ctx, "rden", [P, CH])
        tap_sum = core.sb(ctx, "tap_sum", [P, N])
        tap_one = core.sb(ctx, "tap_one", [P, N])
        s_ps = [core.ps(ctx, "s_ps", [P, 2, 512]) for _ in range(2)]
        m_ps = core.ps(ctx, "m_ps", [P, 2, 512])
        acc_ps = core.ps(ctx, "acc_ps", [P, 512])
        t_ps = core.ps(ctx, "t_ps", [P, 512])
        names = ("ones_set", "scored", "weighed", "valued", "acc_done", "acc_taken", "inverted", "out_done",
                 "m_scored", "m_taken", "row_ready", "turned", "neg_ready", "tap_step", "tap_added")
        (ones_set, scored, weighed, valued, acc_done, acc_taken, inverted, out_done,
         m_scored, m_taken, row_ready, turned, neg_ready, tap_step, tap_added) = (core.sem(n) for n in names)
        loaded = [core.sem("loaded") for _ in range(2)]
        max_placed = [core.sem("max_placed") for _ in range(2)]
        block = ctx.enter_context(core.block())
        UNITS = QC * KT
        GROUPS = PAIRS // 2
        LOADS = 16 * 13

        @block.sync
        def _(sp):
            def load(g, b):
                tok = ds(g % B * N, N)
                for h in range(2):
                    row = (g // B * 4 + 2 * b + h) * HD
                    for dst, first, order in ((qs[b], 0, (0, 0, 1)), (ks[b], C, (0, 1, 0))):
                        for part, half in enumerate(order):
                            sp.dma_start(dst[part * HD:(part + 1) * HD, h, :],
                                         qk_dram[half, ds(first + row, HD), tok]).then_inc(loaded[b], 16)
                sp.dma_start(vs[b][:], v_dram[tok, ds((g // B * 4 + 2 * b) * HD, 2 * HD)].rearrange(
                    "(t p) c -> p t c", p=P)).then_inc(loaded[b], 16)

            def place_max(g, b):
                sp.wait_ge(neg_ready, 2 * g + b + 2)
                for h in range(2):
                    sp.dma_start(qs[b][3 * HD:PADK, h, :], neg_max[h * KT:(h + 1) * KT, :]).then_inc(max_placed[b], 16)

            load(0, 0)
            load(0, 1)
            place_max(0, 0)
            with sp.Fori(0, GROUPS - 1) as g:
                place_max(g, 1)
                sp.wait_ge(valued, (2 * g + 1) * UNITS + 1)
                load(g + 1, 0)
                place_max(g + 1, 0)
                sp.wait_ge(valued, (2 * g + 2) * UNITS + 1)
                load(g + 1, 1)
            place_max(GROUPS - 1, 1)

        @block.tensor
        def _(pe):
            def scores(pair, qc, b, kt, opening=False):
                base = pair * UNITS + qc * KT
                pe.wait_ge(weighed, (base if opening else base + kt - 1) + 1)
                for h in range(2):
                    mm = pe.matmul(s_ps[kt % 2][:, h, 0:CH], ks[b][:, h, kt * P:(kt + 1) * P],
                                   qs[b][:, h, ds(qc * CH, CH)], start=True, stop=True)
                mm.then_inc(scored, 1)

            def max_scores(pair, qc, b, kt):
                h, sub, third = kt // 9, kt % 9 // 3, kt % 3
                pe.wait_ge(m_taken, pair * UNITS + qc * KT + kt + 1)
                for j in range(2):
                    mm = pe.matmul(m_ps[:, j, 0:CH], qs[b][0:3 * HD, h, ds((qc * SUB + sub) * P, P)],
                                   ks[b][0:3 * HD, h, (2 * third + j) * CH:(2 * third + j + 1) * CH],
                                   start=True, stop=True)
                mm.then_inc(m_scored, 1)

            def values(pair, qc, b, kt):
                if kt == 0:
                    pe.wait_ge(acc_taken, pair * QC + qc + 1)
                pe.wait_ge(weighed, pair * UNITS + qc * KT + kt + 2)
                num, den = (0, 64) if b == 0 else (64, 0)
                for h in range(2):
                    pe.matmul(acc_ps[num + h * HD:num + (h + 1) * HD, 0:CH], vs[b][:, kt, h * HD:(h + 1) * HD],
                              prob[:, kt % 3, h], start=kt == 0, stop=kt == KT - 1)
                for h in range(2):
                    mm = pe.matmul(acc_ps[den + h * HD:den + (h + 1) * HD, 0:CH], ones32[:],
                                   prob[:, kt % 3, h], start=kt == 0, stop=kt == KT - 1)
                mm.then_inc(valued, 1)

            def chunk_steps(pair, qc, b, closing, next_too):
                for kt in range(KT):
                    if kt < KT - 1:
                        scores(pair, qc, b, kt + 1)
                    elif not closing:
                        scores(pair, qc + 1, b, 0)
                    if next_too:
                        max_scores(pair + 1, qc, 1 - b, kt)
                    values(pair, qc, b, kt)

            def turn_max(pair):
                pe.wait_ge(row_ready, pair + 2)
                pe.wait_ge(neg_ready, pair + 1)
                pe.matmul(t_ps[0:2 * KT, 0:P], row_max[:].rearrange("p h t -> p (h t)"), ident[:],
                          start=True, stop=True).then_inc(turned, 1)

            def second_pass(g, b, next_too):
                pair = 2 * g + b
                if next_too:
                    pe.wait_ge(loaded[1 - b], LOADS * (g + b + 1) + 1)
                pe.wait_ge(max_placed[b], 32 * (g + 1) + 1)
                scores(pair, 0, b, 0, opening=True)
                with pe.Fori(0, QC - 1) as qc:
                    chunk_steps(pair, qc, b, False, next_too)
                chunk_steps(pair, QC - 1, b, True, next_too)
                if next_too:
                    turn_max(pair + 1)

            pe.wait_ge(ones_set, 2 + 1)
            pe.wait_ge(loaded[0], LOADS + 1)
            with pe.Fori(0, QC) as qc:
                for kt in range(KT):
                    max_scores(0, qc, 0, kt)
            turn_max(0)
            with pe.Fori(0, GROUPS - 1) as g:
                second_pass(g, 0, True)
                second_pass(g, 1, True)
            second_pass(GROUPS - 1, 0, True)
            second_pass(GROUPS - 1, 1, False)

        @block.scalar
        def _(act):
            def weigh(chunk):
                for kt in range(KT):
                    act.wait_ge(scored, chunk * KT + kt + 2)
                    if not (isinstance(chunk, int) and kt < 3):
                        act.wait_ge(valued, chunk * KT + kt - 2 + 1)
                    act.activation(prob[:, kt % 3], s_ps[kt % 2][:, :, 0:CH], ACT.Exp, scale=SCALE).then_inc(weighed, 1)

            weigh(0)
            with act.Fori(1, PAIRS * QC) as chunk:
                weigh(chunk)

        @block.vector
        def _(dve):
            for b in range(2):
                dve.memset(ks[b][3 * HD:PADK, :, :], 1.0).then_inc(ones_set, 1)

            def max_steps(pair, qc):
                for kt in range(KT):
                    h, sub, third = kt // 9, kt % 9 // 3, kt % 3
                    dve.wait_ge(m_scored, pair * UNITS + qc * KT + kt + 2)
                    dve.tensor_reduce(part_max[:, h, ds(qc * SUB + sub, 1), third:third + 1],
                                      m_ps[:, :, 0:CH], AX.XY, ALU.max).then_inc(m_taken, 1)

            def max_rows(g, b):
                pair = 2 * g + b
                dve.wait_ge(m_taken, (pair + 1) * UNITS + 1)
                dve.wait_ge(turned, pair + 1)
                dve.tensor_reduce(row_max[:], part_max[:], AX.X, ALU.max).then_inc(row_ready, 1)
                dve.wait_ge(turned, pair + 2)
                dve.wait_ge(max_placed[1 - b], 32 * (g + b) + 1)
                dve.tensor_scalar(neg_max[:], t_ps[0:2 * KT, 0:P], -1.0, None, ALU.mult).then_inc(neg_ready, 1)

            def finish_chunk(g, qc, b):
                index = (2 * g + b) * QC + qc
                num, den = (0, 64) if b == 0 else (64, 0)
                dve.wait_ge(valued, index * KT + KT + 1)
                dve.wait_ge(out_done, index + 1)
                dve.tensor_copy(summed[:], acc_ps[:, 0:CH]).then_inc(acc_taken, 1)
                dve.wait_ge(acc_taken, index + 2)
                dve.reciprocal(rden[num:num + 64, :], summed[den:den + 64, :]).then_inc(inverted, 1)
                dve.wait_ge(inverted, index + 2)
                dve.tensor_tensor(out_cm[num:num + 64, ds(g * N + qc * CH, CH)], summed[num:num + 64, :],
                                  rden[num:num + 64, :], ALU.mult).then_inc(out_done, 1)

            def pair_steps(g, b, next_too):
                with dve.Fori(0, QC) as qc:
                    if next_too:
                        max_steps(2 * g + b + 1, qc)
                    finish_chunk(g, qc, b)
                if next_too:
                    max_rows(g + b, 1 - b)

            with dve.Fori(0, QC) as qc:
                max_steps(0, qc)
            max_rows(0, 0)
            with dve.Fori(0, GROUPS - 1) as g:
                pair_steps(g, 0, True)
                pair_steps(g, 1, True)
            pair_steps(GROUPS - 1, 0, True)
            pair_steps(GROUPS - 1, 1, False)

        @block.gpsimd
        def _(pool):
            centre = [(0, 0)] + [(dy, dx) for dy in (-1, 0, 1) for dx in (-1, 0, 1) if (dy, dx) != (0, 0)]
            steps = 2 * len(centre)
            for g in range(GROUPS):
                tile, img = g // B, g % B
                base = g * steps
                image = v_cm[:, tile, img * N:(img + 1) * N].rearrange("p (y x) -> p y x", y=HW)
                total = tap_sum[:].rearrange("p (y x) -> p y x", y=HW)
                single = tap_one[:].rearrange("p (y x) -> p y x", y=HW)
                for n, (dy, dx) in enumerate(centre):
                    y0, y1 = max(0, -dy), HW - max(0, dy)
                    x0, x1 = max(0, -dx), HW - max(0, dx)
                    shifted = image[:, y0 + dy:y1 + dy, x0 + dx:x1 + dx]
                    tap = w_tap[:, tile, 3 * (dy + 1) + dx + 1:3 * (dy + 1) + dx + 2]
                    tap = tap.unsqueeze(2).broadcast_to([P, y1 - y0, x1 - x0])
                    if n == 0:
                        pool.wait_ge(tap_added, g + 1)
                        pool.tensor_tensor(total, shifted, tap, ALU.mult).then_inc(tap_step, 1)
                        pool.wait_ge(tap_step, base + 2)
                        pool.tensor_tensor(total, total, b_tap[:, tile:tile + 1].unsqueeze(2).broadcast_to([P, HW, HW]),
                                           ALU.add).then_inc(tap_step, 1)
                        continue
                    pool.wait_ge(tap_step, base + 2 * n + 1)
                    pool.tensor_tensor(single[:, y0:y1, x0:x1], shifted, tap, ALU.mult).then_inc(tap_step, 1)
                    pool.wait_ge(tap_step, base + 2 * n + 2)
                    pool.tensor_tensor(total[:, y0:y1, x0:x1], total[:, y0:y1, x0:x1],
                                       single[:, y0:y1, x0:x1], ALU.add).then_inc(tap_step, 1)
                pool.wait_ge(tap_step, base + steps + 1)
                pool.wait_ge(out_done, 2 * QC * (g + 1) + 1)
                part = out_cm[:, g * N:(g + 1) * N]
                pool.tensor_tensor(part, part, tap_sum[:], ALU.add).then_inc(tap_added, 1)


def window_parts(w):
    parts = {}
    for delta in range(-(QC - 1), QC):
        for sub in range(SUB):
            first, last = sub * P // HW, (sub * P + P - 1) // HW
            rows = [y for y in range(CH // HW)
                    if any(0 <= k + 8 * delta - y + w // 2 < w for k in range(first, last + 1))]
            if rows:
                parts[delta, sub] = (rows[0], rows[-1] + 1)
    return parts


def window_slots():
    slots = {}
    for w, window in enumerate(WINDOWS):
        for key in window_parts(window):
            slots[w, key] = len(slots)
    return slots


def window_steps(qc):
    parts = [window_parts(w) for w in WINDOWS]
    steps = []
    for kt in range(KT):
        key = (kt // SUB - qc, kt % SUB)
        hit = [w for w in range(len(WINDOWS)) if key in parts[w]]
        if hit:
            steps.append((kt, key, hit))
    return steps


def window_norms(core, qk_dram, k_tok, masks, mask_dram, head_sum_dram, rden):
    nc = core.nc
    slots = window_slots()
    parts = [window_parts(w) for w in WINDOWS]
    ROWS = len(WINDOWS) * HEADS
    W = len(WINDOWS)
    with ExitStack() as ctx:
        head_sum = core.sb(ctx, "head_sum", [P, W * CT, ROWS])
        q_half = core.sb(ctx, "q_half", [P, 2, 2, CH], F16)
        q32 = core.sb(ctx, "q32", [P, CH])
        weighed = core.sb(ctx, "weighed", [P, 3, CH])
        den = core.sb(ctx, "den", [ROWS, CH])
        box_ps = core.ps(ctx, "box_ps", [P, 6, 512])
        den_ps = core.ps(ctx, "den_ps", [P, 2, 512])
        const_in, cleared, boxed, multiplied, summed, guarded, inverted, q_whole = (
            core.sem(n) for n in ("const_in", "cleared", "boxed", "multiplied", "summed", "guarded", "inverted", "q_whole"))
        q_in = [core.sem("q_in") for _ in range(2)]
        block = ctx.enter_context(core.block())

        @block.sync
        def _(sp):
            sp.dma_start(masks[:], mask_dram).then_inc(const_in, 16)
            sp.dma_start(head_sum[:], head_sum_dram).then_inc(const_in, 16)
            with sp.Fori(0, NCH) as c:
                for m in range(CT):
                    sp.wait_ge(q_whole, CT * c + 1)
                    for half in range(2):
                        sp.dma_start(q_half[:, m, half], qk_dram[half, m * P:(m + 1) * P, ds(c * CH, CH)]).then_inc(q_in[m], 16)

        @block.tensor
        def _(pe):
            def head_sums(c, m, w):
                n = CT * W * c + m * W + w
                pe.wait_ge(multiplied, n + 2)
                pe.matmul(den_ps[0:ROWS, 0, 0:CH], head_sum[:, w * CT + m], weighed[:, w],
                          start=m == 0 and w == 0, stop=m == CT - 1 and w == W - 1).then_inc(summed, 1)

            pe.wait_ge(const_in, 32 + 1)
            for image in range(B):
                for qc in range(QC):
                    c = image * QC + qc
                    for m in range(CT):
                        for w in range(W):
                            pe.wait_ge(multiplied, CT * W * c + 1)
                            steps = [s for s in window_steps(qc) if w in s[2]]
                            for n, (kt, key, _) in enumerate(steps):
                                r0, r1 = parts[w][key] if n else (0, CH // HW)
                                cols = slice(r0 * HW, r1 * HW)
                                for half in range(2):
                                    mm = pe.matmul(box_ps[:, m * W + w, cols],
                                                   k_tok[half][:, image * KT + kt, m * P:(m + 1) * P],
                                                   masks[:, slots[w, key], cols], start=n == 0 and half == 0,
                                                   stop=n == len(steps) - 1 and half == 1)
                            mm.then_inc(boxed, 1)
                    pe.wait_ge(guarded, c + 1)
                    for m in range(CT):
                        for w in range(W):
                            head_sums(c, m, w)

        @block.gpsimd
        def _(pool):
            pool.memset(rden[:], 0.0).then_inc(cleared, 1)

        @block.vector
        def _(dve):
            dve.wait_ge(cleared, 1 + 1)
            with dve.Fori(0, NCH) as c:
                for m in range(CT):
                    dve.wait_ge(multiplied, CT * W * c + m * W + 1)
                    dve.wait_ge(q_in[m], 32 * (c + 1) + 1)
                    dve.tensor_tensor(q32[:], q_half[:, m, 0], q_half[:, m, 1], ALU.add).then_inc(q_whole, 1)
                    dve.wait_ge(q_whole, CT * c + m + 2)
                    for w in range(W):
                        n = CT * W * c + m * W + w
                        dve.wait_ge(boxed, n + 2)
                        dve.wait_ge(summed, n + 2 - W) if m else dve.wait_ge(summed, CT * W * c + 1)
                        dve.tensor_tensor(weighed[:, w], box_ps[:, m * W + w, 0:CH], q32[:], ALU.mult).then_inc(multiplied, 1)
                dve.wait_ge(summed, CT * W * (c + 1) + 1)
                dve.tensor_scalar(den[:], den_ps[0:ROWS, 0, 0:CH], 1e-6, None, ALU.add).then_inc(guarded, 1)
                dve.wait_ge(guarded, c + 2)
                dve.reciprocal(rden[0:ROWS, ds(c * CH, CH)], den[:]).then_inc(inverted, 1)


POOL_COST = 1.9


def window_attention(core, qk_dram, v_dram, masks, o_dram):
    nc = core.nc
    W = len(WINDOWS)
    parts = [window_parts(w) for w in WINDOWS]
    slots = window_slots()
    plan = [(qc, *step) for qc in range(QC) for step in window_steps(qc)]
    items = [(n, w) for n, (_, _, _, hit) in enumerate(plan) for w in hit]
    S, M = len(plan), len(items)
    first_of = [all(not (v == w and plan[a][0] == plan[n][0]) for a, v in items[:m]) for m, (n, w) in enumerate(items)]
    last_of = [all(not (v == w and plan[a][0] == plan[n][0]) for a, v in items[m + 1:]) for m, (n, w) in enumerate(items)]
    rows = [(0, CH // HW) if first_of[m] else parts[w][plan[n][2]] for m, (n, w) in enumerate(items)]
    on_pool, load = [], {True: 0.0, False: 0.0}
    for r0, r1 in rows:
        cost = {False: float(r1 - r0) + 0.5, True: POOL_COST * (r1 - r0) + 0.5}
        pick = load[True] + cost[True] < load[False] + cost[False]
        load[pick] += cost[pick]
        on_pool.append(pick)
    RING = 4
    mine = {who: [m for m in range(M) if on_pool[m] == who] for who in (False, True)}
    with ExitStack() as ctx:
        qs = [core.sb(ctx, "qs", [3 * HD, 2, N], F16) for _ in range(2)]
        ks = [core.sb(ctx, "ks", [3 * HD, 2, N], F16) for _ in range(2)]
        vs = [core.sb(ctx, "vs", [P, KT, 2 * HD]) for _ in range(2)]
        whole = core.sb(ctx, "whole", [P, 3, 2, CH])
        kept = {who: core.sb(ctx, "kept", [P, RING, 2, CH]) for who in (False, True)}
        result = core.sb(ctx, "result", [P, W, CH])
        s_ps = [core.ps(ctx, "s_ps", [P, 2, 512]) for _ in range(2)]
        acc_ps = core.ps(ctx, "acc_ps", [P, W, 512])
        scored, copied, masked_dve, masked_pool, valued, taken = (
            core.sem(n) for n in ("scored", "copied", "masked_dve", "masked_pool", "valued", "taken"))
        masked = {False: masked_dve, True: masked_pool}
        stored = [core.sem("stored") for _ in WINDOWS]
        loaded = [core.sem("loaded") for _ in range(2)]
        block = ctx.enter_context(core.block())

        def done_by(who, step):
            return sum(1 for m in mine[who] if items[m][0] <= step)

        def lane(w):
            return 64 * (w % 2)

        @block.sync
        def _(sp):
            def load(g, b):
                tok = ds(g % B * N, N)
                for h in range(2):
                    row = (g // B * 4 + 2 * b + h) * HD
                    for dst, first, order in ((qs[b], 0, (0, 0, 1)), (ks[b], C, (0, 1, 0))):
                        for part, half in enumerate(order):
                            sp.dma_start(dst[part * HD:(part + 1) * HD, h, :],
                                         qk_dram[half, ds(first + row, HD), tok]).then_inc(loaded[b], 16)
                sp.dma_start(vs[b][:], v_dram[tok, ds((g // B * 4 + 2 * b) * HD, 2 * HD)].rearrange(
                    "(t p) c -> p t c", p=P)).then_inc(loaded[b], 16)

            def store(g, b):
                with sp.Fori(0, QC) as qc:
                    for w in range(W):
                        sp.wait_ge(taken, W * ((2 * g + b) * QC + qc) + w + 2)
                        sp.dma_start(o_dram[w, ds((g // B * 4 + 2 * b) * HD, 2 * HD), ds(g % B * N + qc * CH, CH)],
                                     result[lane(w):lane(w) + 2 * HD, w]).then_inc(stored[w], 16)

            load(0, 0)
            load(0, 1)
            with sp.Fori(0, PAIRS // 2 - 1) as g:
                for b in range(2):
                    store(g, b)
                    load(g + 1, b)
            for b in range(2):
                store(PAIRS // 2 - 1, b)
            for w in range(W):
                sp.wait_ge(stored[w], 16 * PAIRS * QC + 1)

        @block.tensor
        def _(pe):
            def scores(pair, n, b):
                qc, kt, _, _ = plan[n]
                pe.wait_ge(copied, pair * S + (n - 1 if n >= 2 else 0) + 1)
                for h in range(2):
                    mm = pe.matmul(s_ps[n % 2][:, h, 0:CH], ks[b][:, h, kt * P:(kt + 1) * P],
                                   qs[b][:, h, qc * CH:(qc + 1) * CH], start=True, stop=True)
                mm.then_inc(scored, 1)

            def values(pair, b):
                scores(pair, 0, b)
                scores(pair, 1, b)
                for m, (n, w) in enumerate(items):
                    qc, kt, _, hit = plan[n]
                    if w == hit[0] and n + 2 < S:
                        scores(pair, n + 2, b)
                    cols = slice(rows[m][0] * HW, rows[m][1] * HW)
                    who, index = on_pool[m], mine[on_pool[m]].index(m)
                    if first_of[m]:
                        pe.wait_ge(taken, W * (pair * QC + qc) + 1)
                    pe.wait_ge(masked[who], pair * len(mine[who]) + index + 2)
                    for h in range(2):
                        mm = pe.matmul(acc_ps[lane(w) + h * HD:lane(w) + (h + 1) * HD, w, cols],
                                       vs[b][:, kt, h * HD:(h + 1) * HD],
                                       kept[who][:, index % RING, h, cols], start=first_of[m], stop=last_of[m])
                    mm.then_inc(valued, 1)

            with pe.Fori(0, PAIRS // 2) as g:
                for b in range(2):
                    pe.wait_ge(loaded[b], 13 * 16 * (g + 1) + 1)
                    values(2 * g + b, b)

        @block.scalar
        def _(act):
            with act.Fori(0, PAIRS) as pair:
                def take(qc):
                    for w in range(W):
                        act.wait_ge(stored[w], 16 * (pair * QC + qc) + 1)
                        final = [m for m, (n, v) in enumerate(items) if v == w and plan[n][0] == qc][-1]
                        act.wait_ge(valued, pair * M + final + 2)
                        lanes = slice(lane(w), lane(w) + 2 * HD)
                        act.activation(result[lanes, w], acc_ps[lanes, w, 0:CH], ACT.Copy).then_inc(taken, 1)

                for n, (qc, _, _, _) in enumerate(plan):
                    if qc and plan[n - 2][0] == qc and plan[n - 3][0] != qc:
                        take(qc - 1)
                    act.wait_ge(scored, pair * S + n + 2)
                    for who, sem in ((False, masked_dve), (True, masked_pool)):
                        act.wait_ge(sem, pair * len(mine[who]) + (done_by(who, n - 3) if n >= 3 else 0) + 1)
                    act.activation(whole[:, n % 3], s_ps[n % 2][:, :, 0:CH], ACT.Copy).then_inc(copied, 1)
                take(QC - 1)

        def mask_items(engine, who, sem):
            with engine.Fori(0, PAIRS) as pair:
                for index, m in enumerate(mine[who]):
                    n, w = items[m]
                    engine.wait_ge(copied, pair * S + n + 2)
                    before = mine[who][index - RING] + 1 if index >= RING else 0
                    engine.wait_ge(valued, pair * M + before + 1)
                    cols = slice(rows[m][0] * HW, rows[m][1] * HW)
                    mask = masks[:, slots[w, plan[n][2]], cols].unsqueeze(1).broadcast_to(
                        [P, 2, (rows[m][1] - rows[m][0]) * HW])
                    engine.tensor_tensor(kept[who][:, index % RING, :, cols], whole[:, n % 3, :, cols], mask,
                                         ALU.mult).then_inc(sem, 1)

        @block.vector
        def _(dve):
            mask_items(dve, False, masked_dve)

        @block.gpsimd
        def _(pool):
            mask_items(pool, True, masked_pool)


def project_out(core, x_cm, weight, bias, tiles, o_cm=None, o_dram=None, rden=None, spread=None):
    nc = core.nc
    scaled_too = o_dram is not None
    with ExitStack() as ctx:
        stage = core.sb(ctx, "stage", [P, 2, tiles, CH]) if scaled_too else None
        y_ps = core.ps(ctx, "y_ps", [P, 4, 512])
        r_ps = core.ps(ctx, "r_ps", [P, 3, 512])
        made, added, spreaded, scaled = (core.sem(n) for n in ("made", "added", "spreaded", "scaled"))
        fetched = [core.sem("fetched") for _ in range(2)]
        block = ctx.enter_context(core.block())

        @block.sync
        def _(sp):
            if scaled_too:
                with sp.Fori(0, NCH // 2) as i:
                    for b in range(2):
                        sp.wait_ge(made, 4 * i + 1)
                        sp.dma_start(stage[:, b], o_dram[:, ds((2 * i + b) * CH, CH)].rearrange(
                            "(k p) t -> p k t", p=P)).then_inc(fetched[b], 16)

        @block.tensor
        def _(pe):
            with pe.Fori(0, NCH // 2) as i:
                for b in range(2):
                    chunk = ds((2 * i + b) * CH, CH)
                    if scaled_too:
                        for k in range(tiles):
                            pe.wait_ge(scaled, (2 * i + b) * tiles + k - 1) if b or k >= 3 else \
                                pe.wait_ge(scaled, 2 * i * tiles + 1)
                            pe.matmul(r_ps[:, k % 3, 0:CH], spread[:, k], rden[:, chunk],
                                      start=True, stop=True).then_inc(spreaded, 1)
                        pe.wait_ge(scaled, (2 * i + b + 1) * tiles + 1)
                    for m in range(CT):
                        pe.wait_ge(added, 4 * i + 1)
                        for k in range(tiles):
                            src = stage[:, b, k] if scaled_too else o_cm[:, k, chunk]
                            mm = pe.matmul(y_ps[:, 2 * b + m, 0:CH], weight[:, k, m * P:(m + 1) * P], src,
                                           start=k == 0, stop=k == tiles - 1)
                        mm.then_inc(made, 1)

        @block.vector
        def _(dve):
            with dve.Fori(0, NCH // 2) as i:
                for b in range(2):
                    if scaled_too:
                        dve.wait_ge(fetched[b], 16 * (i + 1) + 1)
                        for k in range(tiles):
                            dve.wait_ge(spreaded, (2 * i + b) * tiles + k + 2)
                            dve.tensor_tensor(stage[:, b, k], stage[:, b, k], r_ps[:, k % 3, 0:CH],
                                              ALU.mult).then_inc(scaled, 1)
                    for m in range(CT):
                        dve.wait_ge(made, 4 * i + 2 * b + m + 2)
                        x = x_cm[:, m, ds((2 * i + b) * CH, CH)]
                        dve.scalar_tensor_tensor(out=x, in0=y_ps[:, 2 * b + m, 0:CH], scalar=bias[:, m:m + 1], in1=x,
                                                 op0=ALU.add, op1=ALU.add).then_inc(added, 1)


def route(core, th, tl, wr, br, comb, iota):
    nc = core.nc
    wr_hi, wr_lo = wr
    with ExitStack() as ctx:
        big = [P, TT, E]
        small = [P, TT]
        logits, work, hot1, hot2, prob = (core.sb(ctx, n, big) for n in ("logits", "work", "hot1", "hot2", "prob"))
        top, index, total, rest = (core.sb(ctx, n, small) for n in ("top", "index", "total", "rest"))
        l_ps = core.ps(ctx, "l_ps", [P, 512])
        made, step, exped = core.sem("made"), core.sem("step"), core.sem("exped")
        block = ctx.enter_context(core.block())
        wide = lambda t: t[:].unsqueeze(2).broadcast_to(big)
        experts = iota[:, 0:E].unsqueeze(1).broadcast_to(big)

        @block.tensor
        def _(pe):
            with pe.Fori(0, TT) as t:
                out = l_ps[:, ds(t * E, E)]
                tok = ds(t * P, P)
                for k in range(CT):
                    pe.matmul(out, th[:, k, tok], wr_hi[:, k, :], start=k == 0, stop=False)
                    pe.matmul(out, tl[:, k, tok], wr_hi[:, k, :], start=False, stop=False)
                    mm = pe.matmul(out, th[:, k, tok], wr_lo[:, k, :], start=False, stop=k == CT - 1)
                mm.then_inc(made, 1)

        @block.scalar
        def _(act):
            act.wait_ge(step, 3 + 1)
            act.activation(prob[:], work[:], ACT.Exp).then_inc(exped, 1)

        @block.vector
        def _(dve):
            count = 0

            def then(ins):
                nonlocal count
                count += 1
                ins.then_inc(step, 1)
                dve.wait_ge(step, count + 1)

            dve.wait_ge(made, TT + 1)
            scores = l_ps[:, 0:TT * E].rearrange("p (t e) -> p t e", e=E)
            if br is None:
                then(dve.tensor_copy(logits[:], scores))
            else:
                then(dve.tensor_tensor(logits[:], scores, br.unsqueeze(1).broadcast_to(big), ALU.add))
            then(dve.tensor_reduce(top[:], logits[:], AX.X, ALU.max))
            then(dve.tensor_tensor(work[:], logits[:], wide(top), ALU.subtract))
            dve.wait_ge(exped, 1 + 1)
            then(dve.tensor_reduce(total[:], prob[:], AX.X, ALU.add))
            then(dve.reciprocal(total[:], total[:]))
            then(dve.tensor_tensor(prob[:], prob[:], wide(total), ALU.mult))
            for hot in (hot1, hot2):
                then(dve.tensor_tensor(work[:], logits[:], wide(top), ALU.is_lt))
                then(dve.scalar_tensor_tensor(out=work[:], in0=work[:], scalar=float(E), in1=experts,
                                              op0=ALU.mult, op1=ALU.add))
                then(dve.tensor_reduce(index[:], work[:], AX.X, ALU.min))
                then(dve.tensor_tensor(hot[:], experts, wide(index), ALU.is_equal))
                if hot is hot1:
                    then(dve.scalar_tensor_tensor(out=logits[:], in0=hot[:], scalar=-3.0e38, in1=logits[:],
                                                  op0=ALU.mult, op1=ALU.add))
                    then(dve.tensor_reduce(top[:], logits[:], AX.X, ALU.max))
            then(dve.tensor_tensor(hot1[:], hot1[:], hot2[:], ALU.add))
            then(dve.tensor_tensor(prob[:], prob[:], hot1[:], ALU.mult))
            then(dve.tensor_reduce(total[:], prob[:], AX.X, ALU.add))
            then(dve.tensor_scalar(total[:], total[:], 1e-12, None, ALU.max))
            then(dve.reciprocal(rest[:], total[:]))
            then(dve.tensor_tensor(comb[:], prob[:], wide(rest), ALU.mult))


def experts(core, x_cm, xh, xl, comb, w1, b1, w2, b2, hidden, ident, one, ln_g=None, ln_b=None):
    nc = core.nc
    MT = hidden // P
    HR = 4
    w1_v = w1.rearrange("e (k p) h -> e p k h", p=P)
    w2_v = w2.rearrange("e (k p) c -> e p k c", p=P)
    with ExitStack() as outer:
        acc = core.sb(outer, "acc", [P, TT, C])
        with ExitStack() as ctx:
            w1_in = core.sb(ctx, "w1_in", [P, CT, hidden])
            w2_in = core.sb(ctx, "w2_in", [P, MT, C])
            w1s = [[core.sb(ctx, "w1s", [P, CT, hidden], F16) for _ in range(2)] for _ in range(2)]
            w2s = [[core.sb(ctx, "w2s", [P, MT, C], F16) for _ in range(2)] for _ in range(2)]
            b1_all = core.sb(ctx, "b1_all", [P, E, MT])
            bias1 = core.sb(ctx, "bias1", [P, 2, MT])
            b2_row = core.sb(ctx, "b2_row", [P, 2, C])
            h32 = core.sb(ctx, "h32", [P, 2, CH])
            hh = core.sb(ctx, "hh", [P, 2, MT, CH], F16)
            hl = core.sb(ctx, "hl", [P, 2, MT, CH], F16)
            y_one = core.sb(ctx, "y_one", [P, SUB, C])
            g_all = core.sb(ctx, "g_all", [P, E, CT])
            b_all = core.sb(ctx, "b_all", [P, E, CT])
            h_ps = core.ps(ctx, "h_ps", [P, HR, 512])
            y_ps = core.ps(ctx, "y_ps", [P, 3, 512])
            bias_ps = core.ps(ctx, "bias_ps", [P, 512])
            small_in, w_in, b2_in = core.sem("small_in"), core.sem("w_in"), [core.sem("b2_in") for _ in range(2)]
            zeroed = core.sem("zeroed")
            scaled, split, bias_made, bias_ready = (core.sem(n) for n in ("scaled", "split", "bias_made", "bias_ready"))
            h_made, h_ready, h_hi, h_split, y_made, y_taken, y_added = (
                core.sem(n) for n in ("h_made", "h_ready", "h_hi", "h_split", "y_made", "y_taken", "y_added"))
            block = ctx.enter_context(core.block())
            norm = ln_g is not None

            @block.sync
            def _(sp):
                sp.dma_start(b1_all[:], b1).then_inc(small_in, 16)
                if norm:
                    sp.dma_start(g_all[:], ln_g).then_inc(small_in, 16)
                    sp.dma_start(b_all[:], ln_b).then_inc(small_in, 16)
                for e in range(E):
                    sp.wait_ge(split, 4 * e + 1)
                    sp.wait_ge(bias_ready, e + 1)
                    sp.dma_start(w1_in[:], w1_v[e]).then_inc(w_in, 16)
                    sp.dma_start(w2_in[:], w2_v[e]).then_inc(w_in, 16)
                    if e >= 2:
                        sp.wait_ge(y_added, TT * (e - 1) + 1)
                    sp.dma_start(b2_row[:, e % 2], b2[e:e + 1, :].broadcast_to([P, C])).then_inc(b2_in[e % 2], 16)

            @block.gpsimd
            def _(pool):
                pool.wait_ge(small_in, (48 if norm else 16) + 1)

                def prepare(i, b):
                    e = 2 * i + b
                    pool.wait_ge(w_in, 32 * (e + 1) + 1)
                    if not isinstance(i, int):
                        pool.wait_ge(y_made, TT * (2 * i - 1 + b) + 1)
                    if norm:
                        pool.wait_ge(bias_made, e + 2)
                        for k in range(CT):
                            pool.tensor_tensor(w1_in[:, k], w1_in[:, k], g_all[:, ds(e, 1), k].broadcast_to([P, hidden]),
                                               ALU.mult).then_inc(scaled, 1)
                        pool.wait_ge(scaled, 2 * (e + 1) + 1)
                    copy(pool, w1s[b][0][:], w1_in[:], one).then_inc(split, 1)
                    copy(pool, w2s[b][0][:], w2_in[:], one).then_inc(split, 1)
                    pool.wait_ge(split, 4 * e + 2 + 1)
                    pool.tensor_tensor(w1s[b][1][:], w1_in[:], w1s[b][0][:], ALU.subtract).then_inc(split, 1)
                    pool.tensor_tensor(w2s[b][1][:], w2_in[:], w2s[b][0][:], ALU.subtract).then_inc(split, 1)

                prepare(0, 0)
                prepare(0, 1)
                with pool.Fori(1, E // 2) as i:
                    prepare(i, 0)
                    prepare(i, 1)

            @block.tensor
            def _(pe):
                if norm:
                    pe.wait_ge(small_in, 48 + 1)
                with pe.Fori(0, E // 2) as i:
                    for b in range(2):
                        e = 2 * i + b
                        if norm:
                            pe.wait_ge(w_in, 32 * (e + 1) + 1)
                            pe.wait_ge(bias_ready, e + 1)
                            for m in range(MT):
                                for k in range(CT):
                                    mm = pe.matmul(bias_ps[:, m:m + 1], w1_in[:, k, m * P:(m + 1) * P],
                                                   b_all[:, ds(e, 1), k], start=k == 0, stop=k == CT - 1)
                            mm.then_inc(bias_made, 1)
                        with pe.Fori(0, NCH // 2) as j:
                            pe.wait_ge(split, 4 * (e + 1) + 1)
                            for s in range(2):
                                c = e * NCH + 2 * j + s
                                chunk = ds((2 * j + s) * CH, CH)
                                for m in range(MT):
                                    pe.wait_ge(h_ready, 2 * MT * (e * (NCH // 2) + j) + 1) if s * MT + m < HR else \
                                        pe.wait_ge(h_ready, c * MT + m + 1 - HR + 1)
                                    for k in range(CT):
                                        mm = split_matmul(pe, h_ps[:, m % HR, 0:CH] if MT >= HR else h_ps[:, s * MT + m, 0:CH],
                                                          w1s[b][0][:, k, m * P:(m + 1) * P], w1s[b][1][:, k, m * P:(m + 1) * P],
                                                          xh[:, k, chunk], xl[:, k, chunk], k == 0, k == CT - 1)
                                    mm.then_inc(h_made, 1)
                            for s in range(2):
                                c = e * NCH + 2 * j + s
                                pe.wait_ge(h_split, (c + 1) * MT + 1)
                                for t in range(SUB):
                                    pe.wait_ge(y_taken, c * SUB + 1)
                                    tok = slice(t * P, (t + 1) * P)
                                    for m in range(MT):
                                        pe.matmul(y_ps[:, t, 0:C], hh[:, s, m, tok], w2s[b][0][:, m, :], start=m == 0, stop=False)
                                        pe.matmul(y_ps[:, t, 0:C], hl[:, s, m, tok], w2s[b][0][:, m, :], start=False, stop=False)
                                        mm = pe.matmul(y_ps[:, t, 0:C], hh[:, s, m, tok], w2s[b][1][:, m, :],
                                                       start=False, stop=m == MT - 1)
                                    mm.then_inc(y_made, 1)

            @block.scalar
            def _(act):
                act.wait_ge(small_in, (48 if norm else 16) + 1)
                with act.Fori(0, E // 2) as i:
                    for b in range(2):
                        e = 2 * i + b
                        act.wait_ge(bias_ready, e + 2)
                        with act.Fori(0, NCH // 2) as j:
                            for s in range(2):
                                c = e * NCH + 2 * j + s
                                for m in range(MT):
                                    act.wait_ge(h_made, c * MT + m + 2)
                                    act.wait_ge(h_split, c * MT + m - 1 + 1) if (s or m >= 2) else \
                                        act.wait_ge(h_split, 2 * MT * (e * (NCH // 2) + j) + 1)
                                    bank = h_ps[:, m % HR, 0:CH] if MT >= HR else h_ps[:, s * MT + m, 0:CH]
                                    act.activation(h32[:, m % 2], bank, ACT.Gelu,
                                                   bias=bias1[:, b, m:m + 1]).then_inc(h_ready, 1)

            @block.vector
            def _(dve):
                dve.memset(acc[:], 0.0).then_inc(zeroed, 1)
                dve.wait_ge(zeroed, 1 + 1)
                dve.wait_ge(small_in, (48 if norm else 16) + 1)
                with dve.Fori(0, E // 2) as i:
                    for b in range(2):
                        e = 2 * i + b
                        if norm:
                            dve.wait_ge(bias_made, e + 2)
                            dve.tensor_tensor(bias1[:, b], bias_ps[:, 0:MT], b1_all[:, ds(e, 1), :].rearrange("p e m -> p (e m)"),
                                              ALU.add).then_inc(bias_ready, 1)
                        else:
                            dve.tensor_copy(bias1[:, b], b1_all[:, ds(e, 1), :].rearrange("p e m -> p (e m)")).then_inc(bias_ready, 1)
                        with dve.Fori(0, NCH // 2) as j:
                            dve.wait_ge(b2_in[b], 16 * (i + 1) + 1)
                            for s in range(2):
                                c = e * NCH + 2 * j + s
                                dve.wait_ge(y_made, 2 * SUB * (e * (NCH // 2) + j) + 1)
                                for m in range(MT):
                                    dve.wait_ge(h_ready, c * MT + m + 2)
                                    dve.tensor_copy(hh[:, s, m], h32[:, m % 2]).then_inc(h_hi, 1)
                                    dve.wait_ge(h_hi, c * MT + m + 2)
                                    dve.tensor_tensor(hl[:, s, m], h32[:, m % 2], hh[:, s, m],
                                                      ALU.subtract).then_inc(h_split, 1)
                            for s in range(2):
                                c = e * NCH + 2 * j + s
                                for t in range(SUB):
                                    dve.wait_ge(y_made, c * SUB + t + 2)
                                    dve.tensor_tensor(y_one[:, t], y_ps[:, t, 0:C], b2_row[:, b], ALU.add).then_inc(y_taken, 1)
                                    dve.wait_ge(y_taken, c * SUB + t + 2)
                                    tile = ds((2 * j + s) * SUB + t, 1)
                                    weight = comb[:, tile, ds(e, 1)].rearrange("p t e -> p (t e)")
                                    mine = acc[:, tile, :].rearrange("p t c -> p (t c)")
                                    dve.scalar_tensor_tensor(out=mine, in0=y_one[:, t], scalar=weight, in1=mine,
                                                             op0=ALU.mult, op1=ALU.add).then_inc(y_added, 1)
        core.end_phase()
        add_tokens(core, x_cm, acc, ident)
        core.end_phase()


def add_tokens(core, x_cm, acc, ident):
    nc = core.nc
    with ExitStack() as ctx:
        stage = core.sb(ctx, "stage", [P, 2, SUB, C])
        t_ps = core.ps(ctx, "t_ps", [P, 2, CT, 512])
        staged, turned, added = core.sem("staged"), core.sem("turned"), core.sem("added")
        block = ctx.enter_context(core.block())

        @block.scalar
        def _(act):
            with act.Fori(0, NCH // 2) as i:
                for b in range(2):
                    act.wait_ge(turned, 2 * i + 1)
                    act.activation(stage[:, b], acc[:, ds((2 * i + b) * SUB, SUB), :], ACT.Copy).then_inc(staged, 1)

        @block.tensor
        def _(pe):
            with pe.Fori(0, NCH // 2) as i:
                for b in range(2):
                    pe.wait_ge(staged, 2 * i + b + 2)
                    pe.wait_ge(added, 2 * i + 1)
                    for t in range(SUB):
                        for k in range(CT):
                            mm = pe.transpose(t_ps[:, b, k, t * P:(t + 1) * P], stage[:, b, t, k * P:(k + 1) * P], ident[:])
                    mm.then_inc(turned, 1)

        @block.vector
        def _(dve):
            with dve.Fori(0, NCH // 2) as i:
                for b in range(2):
                    dve.wait_ge(turned, 2 * i + b + 2)
                    x = x_cm[:, :, ds((2 * i + b) * CH, CH)]
                    dve.tensor_tensor(x, t_ps[:, b, :, 0:CH], x, ALU.add).then_inc(added, 1)


def metaformer(nc, ins, out):
    with ExitStack() as keep:
        core = Core(nc, keep)
        qk_dram = nc.dram_tensor("qk_scratch", [2, 2 * C, T], F16, kind="Internal").ap()
        v_dram = nc.dram_tensor("v_scratch", [T, C], F32, kind="Internal").ap()
        o_dram = nc.dram_tensor("o_scratch", [3, C, T], F32, kind="Internal").ap()
        x_cm = core.sb(keep, "x_cm", [P, CT, T])
        ones = core.sb(keep, "ones", [P, P])
        ones32 = core.sb(keep, "ones32", [P, HD])
        ident = core.sb(keep, "ident", [P, P])
        iota = core.sb(keep, "iota", [P, E])
        eps5, eps6 = core.sb(keep, "eps5", [P, 1]), core.sb(keep, "eps6", [P, 1])
        small = {}
        for name, shape in (("b_proj", [P, CT]), ("b_out", [P, CT]), ("b_tap", [P, CT]), ("w_tap", [P, CT, 9]),
                            ("br", [P, E])):
            small[name] = core.sb(keep, name, shape)

        loaded, const_set, ident_zero = core.sem("loaded"), core.sem("const_set"), core.sem("ident_zero")
        with core.block() as block:
            @block.sync
            def _(sp):
                for b in range(B):
                    for k in range(CT):
                        sp.dma_start(x_cm[:, k, b * N:(b + 1) * N], ins["x"][b, k * P:(k + 1) * P, :]).then_inc(loaded, 16)
                for name, src in (("b_proj", "L0_conv_b_proj"), ("b_out", "L1_conv_bout"), ("b_tap", "L0_conv_b_lepe")):
                    sp.dma_start(small[name][:], ins[src]).then_inc(loaded, 16)
                sp.dma_start(small["w_tap"][:], ins["L0_conv_w_lepe"]).then_inc(loaded, 16)
                sp.dma_start(small["br"][:], ins["L0_ffn_br"].broadcast_to([P, E])).then_inc(loaded, 16)
                sp.wait_ge(loaded, 16 * 9 + 1)

            @block.gpsimd
            def _(pool):
                pool.memset(ones[:], 1.0 / C).then_inc(const_set, 1)
                pool.memset(ones32[:], 1.0).then_inc(const_set, 1)
                pool.memset(eps5[:], 1e-5).then_inc(const_set, 1)
                pool.memset(eps6[:], 1e-6).then_inc(const_set, 1)
                pool.memset(ident[:], 0.0).then_inc(ident_zero, 1)
                pool.wait_ge(ident_zero, 1 + 1)
                pool.affine_select(out=ident[:], in_=ident[:], compare_op=ALU.not_equal, fill=1.0, base=0,
                                   pattern=[[-1, P]], channel_multiplier=1).then_inc(const_set, 1)
                pool.iota(iota[:], pattern=[[1, E]], base=0, channel_multiplier=0,
                          allow_small_or_imprecise_dtypes=True).then_inc(const_set, 1)

        core.end_phase()

        with ExitStack() as ctx:
            v_cm = core.sb(ctx, "v_cm", [P, CT, T])
            with ExitStack() as proj:
                xh, xl = core.sb(proj, "xh", [P, CT, T], F16), core.sb(proj, "xl", [P, CT, T], F16)
                wqk = [core.sb(proj, "wqk", [P, 4 * CT * P], F16) for _ in range(2)]
                wv = [core.sb(proj, "wv", [P, CT, C], F16) for _ in range(2)]
                split_weights(core, [(ins["w_qk0"], wqk[0][:], wqk[1][:]), (ins["w_v0"], wv[0][:], wv[1][:])])
                core.end_phase()
                layer_norm(core, x_cm, xh, xl, ones, eps6)
                core.end_phase()
                project(core, xh, xl, wqk, wv, qk_dram, v_dram, v_cm, sigmoid=False)
                core.end_phase()
            out_cm = core.sb(ctx, "out_cm", [P, CT * T])
            softmax_attention(core, qk_dram, v_dram, v_cm, small["w_tap"], small["b_tap"], out_cm, ones32, ident)
            core.end_phase()
            weight = core.sb(ctx, "w_proj", [P, CT, C])
            load_weight(core, weight, ins["w_proj"])
            core.end_phase()
            project_out(core, x_cm, weight, small["b_proj"], CT, o_cm=out_cm[:].rearrange("p (k t) -> p k t", k=CT))
            core.end_phase()

        with ExitStack() as ctx:
            comb = core.sb(ctx, "comb", [P, TT, E])
            xh, xl = core.sb(ctx, "xh", [P, CT, T], F16), core.sb(ctx, "xl", [P, CT, T], F16)
            with ExitStack() as inner:
                t32 = core.sb(inner, "t32", [P, CT, T])
                wr = [core.sb(inner, "wr", [P, CT, E], F16) for _ in range(2)]
                split_weights(core, [(ins["w_r0"], wr[0][:], wr[1][:])])
                core.end_phase()
                layer_norm(core, x_cm, xh, xl, ones, eps5, keep32=t32, one=ones32[:, 0:1])
                core.end_phase()
                route(core, xh, xl, wr, small["br"][:], comb, iota)
                core.end_phase()
                layer_norm(core, t32, xh, xl, ones, eps5)
                core.end_phase()
            experts(core, x_cm, xh, xl, comb, ins["L0_ffn_W1"], ins["L0_ffn_b1"], ins["L0_ffn_W2"], ins["L0_ffn_b2"],
                    1024, ident, ones32[:, 0:1], ins["L0_ffn_ln_g"], ins["L0_ffn_ln_b"])

        with ExitStack() as ctx:
            k_tok = [core.sb(ctx, "k_tok", [P, TT, C], F16) for _ in range(2)]
            with ExitStack() as proj:
                xh, xl = core.sb(proj, "xh", [P, CT, T], F16), core.sb(proj, "xl", [P, CT, T], F16)
                wqk = [core.sb(proj, "wqk", [P, 4 * CT * P], F16) for _ in range(2)]
                wv = [core.sb(proj, "wv", [P, CT, C], F16) for _ in range(2)]
                split_weights(core, [(ins["w_qk1"], wqk[0][:], wqk[1][:]), (ins["w_v1"], wv[0][:], wv[1][:])])
                core.end_phase()
                layer_norm(core, x_cm, xh, xl, ones, eps6)
                core.end_phase()
                project(core, xh, xl, wqk, wv, qk_dram, v_dram, None, sigmoid=True, k_tok=k_tok)
                core.end_phase()
            rden = core.sb(ctx, "rden", [P, T])
            with ExitStack() as windows:
                masks = core.sb(windows, "masks", [P, len(window_slots()), CH], F16)
                window_norms(core, qk_dram, k_tok, masks, ins["masks"], ins["head_sum"], rden)
                core.end_phase()
                window_attention(core, qk_dram, v_dram, masks, o_dram)
                core.end_phase()
            weight = core.sb(ctx, "w_out", [P, 3 * CT, C])
            load_weight(core, weight, ins["w_out"])
            core.end_phase()
            spread = core.sb(ctx, "spread", [P, 3 * CT, P])
            load_weight(core, spread, ins["head_spread"])
            core.end_phase()
            project_out(core, x_cm, weight, small["b_out"], 3 * CT, o_dram=o_dram.rearrange("w c t -> (w c) t"),
                        rden=rden, spread=spread)
            core.end_phase()

        with ExitStack() as ctx:
            comb = core.sb(ctx, "comb", [P, TT, E])
            xh, xl = core.sb(ctx, "xh", [P, CT, T], F16), core.sb(ctx, "xl", [P, CT, T], F16)
            with ExitStack() as inner:
                wr = [core.sb(inner, "wr", [P, CT, E], F16) for _ in range(2)]
                split_weights(core, [(ins["w_r1"], wr[0][:], wr[1][:])])
                core.end_phase()
                layer_norm(core, x_cm, xh, xl, ones, eps5, add_back=True)
                core.end_phase()
                route(core, xh, xl, wr, None, comb, iota)
                core.end_phase()
            experts(core, x_cm, xh, xl, comb, ins["L1_ffn_w1"], ins["L1_ffn_b1"], ins["L1_ffn_w2"], ins["L1_ffn_b2"],
                    256, ident, ones32[:, 0:1])

        stored = core.sem("stored")
        with core.block() as block:
            @block.sync
            def _(sp):
                for b in range(B):
                    for k in range(CT):
                        sp.dma_start(out[b, k * P:(k + 1) * P, :], x_cm[:, k, b * N:(b + 1) * N]).then_inc(stored, 16)
                sp.wait_ge(stored, 64 + 1)


def load_weight(core, dst, src):
    loaded = core.sem("weight_loaded")
    with core.block() as block:
        @block.sync
        def _(sp):
            sp.dma_start(dst[:], src).then_inc(loaded, 16)
            sp.wait_ge(loaded, 16 + 1)


def window_masks(np):
    tiles = []
    for w in WINDOWS:
        for delta, sub in window_parts(w):
            key = sub * P + np.arange(P)
            query = np.arange(CH)
            dy = (key // HW)[:, None] + 8 * delta - (query // HW)[None, :]
            dx = (key % HW)[:, None] - (query % HW)[None, :]
            seen = (dy >= -(w // 2)) & (dy < w // 2) & (dx >= -(w // 2)) & (dx < w // 2)
            tiles.append(seen.astype(np.float16))
    return np.ascontiguousarray(np.stack(tiles, 1))


def kernel(**inputs):
    import numpy as np
    import concourse.bacc as bacc
    from concourse.bass_utils import run_bass_kernel_spmd as run

    a = {k: np.asarray(v) for k, v in inputs.items()}

    def tiled(w):
        return np.ascontiguousarray(w.reshape(-1, P, w.shape[1]).transpose(1, 0, 2))

    def by_channel(v):
        return np.ascontiguousarray(np.moveaxis(v.reshape(*v.shape[:-1], -1, P), -1, 0))

    def by_tile(q, k):
        both = np.concatenate([q, k], 1).reshape(CT, P, 4, P)
        return np.ascontiguousarray(both.transpose(1, 2, 0, 3).reshape(P, 4 * CT * P))

    head_sum = np.zeros((P, 3 * CT, 3 * HEADS), np.float32)
    for k in range(3 * CT):
        for p in range(P):
            head_sum[p, k, (k * P + p) // HD] = 1.0
    head_spread = np.zeros((P, 3 * CT, P), np.float32)
    head_spread[:3 * HEADS] = head_sum.transpose(2, 1, 0)
    qkv = a["L0_conv_w_qkv"].reshape(HEADS, 3, HD, C)
    q0, k0, v0 = (qkv[:, i].reshape(C, C).T for i in range(3))
    arrays = {
        "x": a["x"].reshape(B, C, N),
        "w_qk0": by_tile(q0, k0), "w_v0": tiled(v0),
        "w_proj": tiled(a["L0_conv_w_proj"].T), "L0_conv_b_proj": by_channel(a["L0_conv_b_proj"]),
        "L0_conv_w_lepe": tiled(a["L0_conv_w_lepe"].reshape(C, 9)), "L0_conv_b_lepe": by_channel(a["L0_conv_b_lepe"]),
        "w_r0": tiled(a["L0_ffn_Wr"]), "L0_ffn_br": a["L0_ffn_br"].reshape(1, E),
        "w_qk1": by_tile(a["L1_conv_Wq"].T, a["L1_conv_Wk"].T), "w_v1": tiled(a["L1_conv_Wv"].T),
        "w_out": tiled(a["L1_conv_Wout"].T), "L1_conv_bout": by_channel(a["L1_conv_bout"]),
        "w_r1": tiled(a["L1_ffn_router_w"].T),
        "masks": window_masks(np), "head_sum": head_sum, "head_spread": head_spread,
    }
    for name in ("L0_ffn_ln_g", "L0_ffn_ln_b", "L0_ffn_W1", "L0_ffn_b1", "L0_ffn_W2", "L0_ffn_b2",
                 "L1_ffn_w1", "L1_ffn_b1", "L1_ffn_w2", "L1_ffn_b2"):
        arrays[name] = by_channel(a[name]) if name.endswith(("ln_g", "ln_b", "b1")) else a[name]
    arrays = {k: np.ascontiguousarray(v) for k, v in arrays.items()}

    nc = bacc.Bacc("TRN2", target_bir_lowering=False, num_devices=1)
    ins = {k: nc.dram_tensor(f"in_{k}", v.shape, mybir.dt.from_np(v.dtype), kind="ExternalInput").ap()
           for k, v in arrays.items()}
    out = nc.dram_tensor("out", [B, C, N], F32, kind="ExternalOutput").ap()
    metaformer(nc, ins, out)
    r = run(nc, [{f"in_{k}": v for k, v in arrays.items()}], core_ids=[0])
    return r.results[0]["out"].reshape(B, C, HW, HW)
```

```python
from contextlib import ExitStack

import concourse.bass as bass
from concourse import mybir

F32 = mybir.dt.float32
F16 = mybir.dt.float16
ALU = mybir.AluOpType
ACT = mybir.ActivationFunctionType
AX = mybir.AxisListType
ds = bass.ds

P = 128
B, C, HW = 2, 256, 48
N = HW * HW
T = B * N
CT = C // P
HEADS, HD = 8, 32
CH = 8 * HW
NCH = T // CH
QC = N // CH
KT = N // P
TT = T // P
SUB = CH // P
PAIRS = B * HEADS // 2
SCALE = float(HD) ** -0.5
E = 8
WINDOWS = (48, 24, 12)
PADK = 3 * HD + 1


class Core:

    def __init__(self, nc, keep):
        self.nc, self.keep, self.n, self.phase = nc, keep, 0, []

    def sem(self, name):
        self.n += 1
        self.phase.append(self.nc.alloc_semaphore(name=f"{name}_{self.n}"))
        return self.phase[-1]

    def block(self):
        with self.nc.Block() as block:
            @block.sync
            def _(sp):
                for sem in self.phase:
                    sp.sem_inc(sem, 1)
        return self.nc.Block()

    def end_phase(self):
        with self.nc.Block() as block:
            @block.sync
            def _(sp):
                for sem in self.phase:
                    sp.sem_clear(sem)
        for sem in self.phase:
            self.nc.release_semaphore(sem)
        self.phase.clear()

    def sb(self, ctx, name, shape, dt=F32):
        self.n += 1
        return ctx.enter_context(self.nc.sbuf_tensor(f"{name}_{self.n}", shape, dt))

    def ps(self, ctx, name, shape, dt=F32):
        self.n += 1
        return ctx.enter_context(self.nc.psum_tensor(f"{name}_{self.n}", shape, dt))


def copy(pool, out, src, one):
    return pool.tensor_tensor(out, src, one.unsqueeze(2).broadcast_to(list(src.shape)), ALU.mult)


def split_matmul(pe, out, w_hi, w_lo, x_hi, x_lo, first, last):
    pe.matmul(out, w_hi, x_hi, start=first, stop=False)
    pe.matmul(out, w_hi, x_lo, start=False, stop=False)
    return pe.matmul(out, w_lo, x_hi, start=False, stop=last)


def layer_norm(core, src, hi, lo, norm_const, eps_tile, whole=None, add_back=False):
    nc = core.nc
    mean_ones, var_rows, row_spread = norm_const
    with ExitStack() as ctx:
        centred = whole if whole is not None else core.sb(ctx, "centred", [P, CT, T])
        square = core.sb(ctx, "square", [P, 2, CT, CH])
        std = core.sb(ctx, "std", [32, CH])
        rstd = core.sb(ctx, "rstd", [32, CH])
        mean_ps = core.ps(ctx, "mean_ps", [P, 2, 512])
        var_ps = core.ps(ctx, "var_ps", [P, 512])
        rstd_ps = core.ps(ctx, "rstd_ps", [P, 4, 512])
        mean_ready, centred_ready, square_ready, var_ready, std_ready, rstd_ready = (
            core.sem(n) for n in ("mean_ready", "centred_ready", "square_ready", "var_ready", "std_ready", "rstd_ready"))
        spreaded, norm_ready, hi_ready, lo_ready, back_ready = (
            core.sem(n) for n in ("spreaded", "norm_ready", "hi_ready", "lo_ready", "back_ready"))
        block = ctx.enter_context(core.block())
        chunk = [slice(c * CH, (c + 1) * CH) for c in range(NCH)]
        lo_on_pool = [not add_back and c % 3 != 2 for c in range(NCH)]

        @block.tensor
        def _(pe):
            def variance(c):
                pe.wait_ge(square_ready, c + 2)
                for k in range(CT):
                    mm = pe.matmul(var_ps[0:32, 0:CH], var_rows[:, c], square[:, c % 2, k, :],
                                   start=c == 0 and k == 0, stop=c == NCH - 1 and k == CT - 1)
                mm.then_inc(var_ready, 1)

            for c in range(NCH):
                if c >= 2:
                    pe.wait_ge(centred_ready, c - 1 + 1)
                for k in range(CT):
                    mm = pe.matmul(mean_ps[:, c % 2, 0:CH], mean_ones[:], src[:, k, chunk[c]],
                                   start=k == 0, stop=k == CT - 1)
                mm.then_inc(mean_ready, 1)
                if c:
                    variance(c - 1)
            variance(NCH - 1)
            pe.wait_ge(rstd_ready, 1 + 1)
            for c in range(NCH):
                if c >= 4:
                    pe.wait_ge(norm_ready, c - 3 + 1)
                pe.matmul(rstd_ps[:, c % 4, 0:CH], row_spread[:, c], rstd[:], start=True, stop=True).then_inc(spreaded, 1)

        @block.vector
        def _(dve):
            def remainder(c):
                dve.wait_ge(hi_ready, c + 2)
                dve.tensor_tensor(lo[:, :, chunk[c]], centred[:, :, chunk[c]], hi[:, :, chunk[c]],
                                  ALU.subtract).then_inc(lo_ready, 1)

            for c in range(NCH):
                dve.wait_ge(mean_ready, c + 2)
                dve.tensor_tensor(centred[:, :, chunk[c]], src[:, :, chunk[c]],
                                  mean_ps[:, c % 2, 0:CH].unsqueeze(1).broadcast_to([P, CT, CH]),
                                  ALU.subtract).then_inc(centred_ready, 1)
            dve.wait_ge(std_ready, 1 + 1)
            dve.reciprocal(rstd[:], std[:]).then_inc(rstd_ready, 1)
            for c in range(NCH):
                dve.wait_ge(spreaded, c + 2)
                dve.wait_ge(square_ready, c + 2)
                dve.tensor_tensor(centred[:, :, chunk[c]], centred[:, :, chunk[c]],
                                  rstd_ps[:, c % 4, 0:CH].unsqueeze(1).broadcast_to([P, CT, CH]),
                                  ALU.mult).then_inc(norm_ready, 1)
                if c >= 2 and not lo_on_pool[c - 2]:
                    remainder(c - 2)
            for c in (NCH - 2, NCH - 1):
                if not lo_on_pool[c]:
                    remainder(c)

        @block.scalar
        def _(act):
            for c in range(NCH):
                act.wait_ge(centred_ready, c + 2)
                if c >= 2:
                    act.wait_ge(var_ready, c - 1 + 1)
                act.activation(square[:, c % 2], centred[:, :, chunk[c]], ACT.Square).then_inc(square_ready, 1)
            act.wait_ge(var_ready, NCH + 1)
            act.activation(std[:], var_ps[0:32, 0:CH], ACT.Sqrt, bias=eps_tile[0:32, 0:1]).then_inc(std_ready, 1)
            for c in range(NCH):
                act.wait_ge(norm_ready, c + 2)
                act.activation(hi[:, :, chunk[c]], centred[:, :, chunk[c]], ACT.Copy).then_inc(hi_ready, 1)

        @block.gpsimd
        def _(pool):
            for c in range(NCH):
                if add_back:
                    pool.wait_ge(norm_ready, c + 2)
                    pool.tensor_tensor(src[:, :, chunk[c]], src[:, :, chunk[c]], centred[:, :, chunk[c]],
                                       ALU.add).then_inc(back_ready, 1)
                if lo_on_pool[c]:
                    pool.wait_ge(hi_ready, c + 2)
                    pool.tensor_tensor(lo[:, :, chunk[c]], centred[:, :, chunk[c]], hi[:, :, chunk[c]],
                                       ALU.subtract).then_inc(lo_ready, 1)


def split_weights(core, pairs):
    nc = core.nc
    with ExitStack() as ctx:
        stages = [core.sb(ctx, "stage", list(src.shape)) for src, _, _ in pairs]
        loaded = [core.sem("loaded") for _ in pairs]
        hi_ready, lo_ready = core.sem("w_hi_ready"), core.sem("w_lo_ready")
        block = ctx.enter_context(core.block())

        @block.sync
        def _(sp):
            for (src, _, _), stage, ready in zip(pairs, stages, loaded):
                sp.dma_start(stage[:], src).then_inc(ready, 16)

        @block.scalar
        def _(act):
            for (_, hi, _), stage, ready in zip(pairs, stages, loaded):
                act.wait_ge(ready, 16 + 1)
                act.activation(hi, stage[:], ACT.Copy).then_inc(hi_ready, 1)

        @block.vector
        def _(dve):
            for n, ((_, hi, lo), stage) in enumerate(zip(pairs, stages)):
                dve.wait_ge(hi_ready, n + 2)
                dve.tensor_tensor(lo, stage[:], hi, ALU.subtract).then_inc(lo_ready, 1)


def project(core, xh, xl, wqk, wv, qk_dram, v_dram, v_cm, sigmoid, k_tok=None):
    nc = core.nc
    wqk_hi, wqk_lo = wqk
    wv_hi, wv_lo = wv
    with ExitStack() as ctx:
        hi = core.sb(ctx, "qk_hi", [P, 2, 4, CH], F16)
        lo = core.sb(ctx, "qk_lo", [P, 2, 4, CH], F16)
        gate = core.sb(ctx, "gate", [P, 4, CH]) if sigmoid else None
        v_tok = core.sb(ctx, "v_tok", [P, 2, SUB, C])
        qk_ps = core.ps(ctx, "qk_ps", [P, 4, 512])
        v_ps = core.ps(ctx, "v_ps", [P, 2, 512])
        vt_ps = core.ps(ctx, "vt_ps", [P, 2, 512])
        qk_made, vcm_made, vt_made = core.sem("qk_made"), core.sem("vcm_made"), core.sem("vt_made")
        gated, hi_ready, lo_ready = core.sem("gated"), core.sem("hi_ready"), core.sem("lo_ready")
        vcm_taken, vt_taken = core.sem("vcm_taken"), core.sem("vt_taken")
        v_squared, v_summed, v_rooted, v_guarded, v_inverted, v_ready = (
            core.sem(n) for n in ("v_squared", "v_summed", "v_rooted", "v_guarded", "v_inverted", "v_ready"))
        hi_stored = [core.sem("hi_stored") for _ in range(2)]
        lo_stored = [core.sem("lo_stored") for _ in range(2)]
        v_stored = [core.sem("v_stored") for _ in range(2)]
        v_sq = core.sb(ctx, "v_sq", [P, SUB, C])
        v_ss = core.sb(ctx, "v_ss", [P, SUB, HEADS])
        v_norm = core.sb(ctx, "v_norm", [P, SUB, HEADS])
        v_inv = core.sb(ctx, "v_inv", [P, SUB, HEADS])
        k_gate = core.sb(ctx, "k_gate", [P, 2, SUB, C]) if sigmoid else None
        kt_made, kt_gated, kt_hi, kt_lo = (core.sem(n) for n in ("kt_made", "kt_gated", "kt_hi", "kt_lo"))
        block = ctx.enter_context(core.block())

        @block.tensor
        def _(pe):
            with pe.Fori(0, NCH) as c:
                chunk = ds(c * CH, CH)
                for m in range(4):
                    pe.wait_ge(lo_ready, 4 * c + 1)
                    for k in range(CT):
                        w = ds((m * CT + k) * P, P)
                        mm = split_matmul(pe, qk_ps[:, m, 0:CH], wqk_hi[:, w], wqk_lo[:, w],
                                          xh[:, k, chunk], xl[:, k, chunk], k == 0, k == CT - 1)
                    mm.then_inc(qk_made, 1)
                if v_cm is not None:
                    for m in range(CT):
                        pe.wait_ge(vcm_taken, 2 * c + 1)
                        for k in range(CT):
                            mm = split_matmul(pe, v_ps[:, m, 0:CH], wv_hi[:, k, m * P:(m + 1) * P],
                                              wv_lo[:, k, m * P:(m + 1) * P], xh[:, k, chunk], xl[:, k, chunk],
                                              k == 0, k == CT - 1)
                        mm.then_inc(vcm_made, 1)
                if k_tok is not None:
                    for t in range(SUB):
                        pe.wait_ge(kt_gated, 2 * c + 1)
                        out = v_ps[:, t // 2, (t % 2) * C:(t % 2 + 1) * C].rearrange("p (m c) -> p m c", m=CT)
                        tok = ds(c * CH + t * P, P)
                        for k in range(CT):
                            half = [w[:].rearrange("p (m k c) -> p m k c", k=CT, c=P)[:, CT:2 * CT, k, :] for w in (wqk_hi, wqk_lo)]
                            pe.matmul(out, xh[:, k, tok], half[0], start=k == 0, stop=False)
                            pe.matmul(out, xl[:, k, tok], half[0], start=False, stop=False)
                            mm = pe.matmul(out, xh[:, k, tok], half[1], start=False, stop=k == CT - 1)
                        mm.then_inc(kt_made, 1)
                for t in range(SUB):
                    pe.wait_ge(vt_taken, 2 * c + 1)
                    out = vt_ps[:, t // 2, (t % 2) * C:(t % 2 + 1) * C]
                    tok = ds(c * CH + t * P, P)
                    for k in range(CT):
                        pe.matmul(out, xh[:, k, tok], wv_hi[:, k, :], start=k == 0, stop=False)
                        pe.matmul(out, xl[:, k, tok], wv_hi[:, k, :], start=False, stop=False)
                        mm = pe.matmul(out, xh[:, k, tok], wv_lo[:, k, :], start=False, stop=k == CT - 1)
                    mm.then_inc(vt_made, 1)

        @block.scalar
        def _(act):
            with act.Fori(0, NCH // 2) as i:
                for b in range(2):
                    c = 2 * i + b
                    act.wait_ge(hi_stored[b], 16 * i + 1)
                    if sigmoid:
                        act.wait_ge(lo_ready, 4 * c + 1)
                    for m in range(4):
                        act.wait_ge(qk_made, 4 * c + m + 2)
                        if sigmoid:
                            act.activation(gate[:, m], qk_ps[:, m, 0:CH], ACT.Sigmoid).then_inc(gated, 1)
                            act.wait_ge(gated, 4 * c + m + 2)
                            act.activation(hi[:, b, m], gate[:, m], ACT.Copy).then_inc(hi_ready, 1)
                        else:
                            act.activation(hi[:, b, m], qk_ps[:, m, 0:CH], ACT.Copy).then_inc(hi_ready, 1)
                    if v_cm is not None:
                        for m in range(CT):
                            act.wait_ge(vcm_made, 2 * c + m + 2)
                            act.activation(v_cm[:, m, ds(c * CH, CH)], v_ps[:, m, 0:CH],
                                           ACT.Copy).then_inc(vcm_taken, 1)
                    if k_tok is not None:
                        act.wait_ge(kt_made, 3 * c + 4)
                        act.wait_ge(kt_lo, 2 * i + 1)
                        act.activation(k_gate[:, b, 0:2].rearrange("p t c -> p (t c)"), v_ps[:, 0, :],
                                       ACT.Sigmoid).then_inc(kt_gated, 1)
                        act.activation(k_gate[:, b, 2], v_ps[:, 1, 0:C], ACT.Sigmoid).then_inc(kt_gated, 1)
                        act.wait_ge(kt_gated, 2 * c + 3)
                        act.activation(k_tok[0][:, ds(c * SUB, SUB), :], k_gate[:, b], ACT.Copy).then_inc(kt_hi, 1)
                    if sigmoid:
                        act.wait_ge(v_summed, c + 2)
                        act.activation(v_norm[:], v_ss[:], ACT.Sqrt).then_inc(v_rooted, 1)

        @block.vector
        def _(dve):
            with dve.Fori(0, NCH // 2) as i:
                for b in range(2):
                    c = 2 * i + b
                    dve.wait_ge(lo_stored[b], 16 * i + 1)
                    for m in range(4):
                        dve.wait_ge(hi_ready, 4 * c + m + 2)
                        whole = gate[:, m] if sigmoid else qk_ps[:, m, 0:CH]
                        dve.tensor_tensor(lo[:, b, m], whole, hi[:, b, m], ALU.subtract).then_inc(lo_ready, 1)
                    dve.wait_ge(v_stored[b], 16 * i + 1)
                    dve.wait_ge(vt_made, 3 * c + 4)
                    dve.tensor_copy(v_tok[:, b, 0:2].rearrange("p t c -> p (t c)"), vt_ps[:, 0, :]).then_inc(vt_taken, 1)
                    dve.tensor_copy(v_tok[:, b, 2], vt_ps[:, 1, 0:C]).then_inc(vt_taken, 1)
                    if sigmoid:
                        dve.wait_ge(vt_taken, 2 * c + 3)
                        dve.tensor_tensor(v_sq[:], v_tok[:, b], v_tok[:, b], ALU.mult).then_inc(v_squared, 1)
                        dve.wait_ge(v_squared, c + 2)
                        dve.tensor_reduce(v_ss[:], v_sq[:].rearrange("p t (h d) -> p t h d", h=HEADS), AX.X,
                                          ALU.add).then_inc(v_summed, 1)
                        dve.wait_ge(v_rooted, c + 2)
                        dve.tensor_scalar(v_inv[:], v_norm[:], 1e-12, None, ALU.max).then_inc(v_guarded, 1)
                        dve.wait_ge(v_guarded, c + 2)
                        dve.reciprocal(v_inv[:], v_inv[:]).then_inc(v_inverted, 1)
                        dve.wait_ge(v_inverted, c + 2)
                        heads = v_tok[:, b].rearrange("p t (h d) -> p (t h) d", h=HEADS)
                        dve.tensor_tensor(heads, heads,
                                          v_inv[:].rearrange("p t h -> p (t h)").unsqueeze(2).broadcast_to([P, SUB * HEADS, HD]),
                                          ALU.mult).then_inc(v_ready, 1)

        @block.gpsimd
        def _(pool):
            if k_tok is not None:
                with pool.Fori(0, NCH // 2) as i:
                    for b in range(2):
                        c = 2 * i + b
                        pool.wait_ge(kt_hi, c + 2)
                        pool.tensor_tensor(k_tok[1][:, ds(c * SUB, SUB), :], k_gate[:, b],
                                           k_tok[0][:, ds(c * SUB, SUB), :], ALU.subtract).then_inc(kt_lo, 1)

        @block.sync
        def _(sp):
            with sp.Fori(0, NCH // 2) as i:
                for b in range(2):
                    c = 2 * i + b
                    chunk = ds(c * CH, CH)
                    sp.wait_ge(hi_ready, 4 * c + 5)
                    sp.dma_start(qk_dram[0, :, chunk].rearrange("(m p) t -> p m t", p=P), hi[:, b]).then_inc(hi_stored[b], 16)
                    sp.wait_ge(lo_ready, 4 * c + 5)
                    sp.dma_start(qk_dram[1, :, chunk].rearrange("(m p) t -> p m t", p=P), lo[:, b]).then_inc(lo_stored[b], 16)
                    if sigmoid:
                        sp.wait_ge(v_ready, c + 2)
                    else:
                        sp.wait_ge(vt_taken, 2 * c + 3)
                    sp.dma_start(v_dram[chunk, :].rearrange("(t p) c -> p t c", p=P), v_tok[:, b]).then_inc(v_stored[b], 16)
            for b in range(2):
                for s in (hi_stored[b], lo_stored[b], v_stored[b]):
                    sp.wait_ge(s, 16 * (NCH // 2) + 1)


def max_schedule(qc):
    if qc == 0:
        return 0, 0, 0, [0] * 6 + [2] * 12
    if qc == QC - 1:
        return 24 + 42 * (QC - 2), 1, 14, [3] * 8 + [0] * 10
    return 24 + 42 * (qc - 1), (qc - 1) // 2, (4 + 7 * (qc - 1)) % KT, [3 if kt % 3 == 2 else 2 for kt in range(KT)]


def softmax_attention(core, qk_dram, v_dram, v_cm, w_tap, b_tap, out_cm, ident, den_ones_dram, den_spread_dram):
    nc = core.nc
    with ExitStack() as ctx:
        qs = [core.sb(ctx, "qs", [PADK, 2, N], F16) for _ in range(2)]
        ks = [core.sb(ctx, "ks", [PADK, 2, N], F16) for _ in range(2)]
        vs = [core.sb(ctx, "vs", [P, KT, 2 * HD]) for _ in range(2)]
        prob = core.sb(ctx, "prob", [P, 3, 2, CH])
        part_max = core.sb(ctx, "part_max", [P, 2, KT, QC])
        row_max = core.sb(ctx, "row_max", [P, 2, KT])
        neg_max = core.sb(ctx, "neg_max", [2 * KT, P], F16)
        den_ones = core.sb(ctx, "den_ones", [P, QC, HD])
        den_spread = core.sb(ctx, "den_spread", [P, QC, P])
        den = core.sb(ctx, "den", [P, CH])
        rden = core.sb(ctx, "rden", [P, CH])
        tap_sum = core.sb(ctx, "tap_sum", [P, N])
        tap_one = core.sb(ctx, "tap_one", [P, N])
        s_ps = [core.ps(ctx, "s_ps", [P, 2, 512]) for _ in range(2)]
        m_ps = core.ps(ctx, "m_ps", [P, 2, 512])
        acc_ps = core.ps(ctx, "acc_ps", [P, 512])
        t_ps = core.ps(ctx, "t_ps", [P, 512])
        names = ("const_in", "ones_set", "scored", "weighed", "valued", "acc_taken", "den_taken", "inverted", "spreaded",
                 "out_done", "row_ready", "turned", "neg_ready", "tap_step", "tap_added")
        (const_in, ones_set, scored, weighed, valued, acc_taken, den_taken, inverted, spreaded,
         out_done, row_ready, turned, neg_ready, tap_step, tap_added) = (core.sem(n) for n in names)
        head0_in = [core.sem("head0_in") for _ in range(2)]
        rest_in = [core.sem("rest_in") for _ in range(2)]
        max_placed = [core.sem("max_placed") for _ in range(2)]
        m_scored = [[core.sem("m_scored") for _ in range(2)] for _ in range(2)]
        m_taken = [[core.sem("m_taken") for _ in range(2)] for _ in range(2)]
        first_scored, first_taken = core.sem("first_scored"), core.sem("first_taken")
        block = ctx.enter_context(core.block())
        UNITS = QC * KT
        GROUPS = PAIRS // 2
        HEAD0, REST = 16 * 6, 16 * 7

        def upto(g, k, each, more):
            return g * (2 * each) + (k * each + more + 1)

        def halves(b):
            return (0, 64) if b == 0 else (64, 0)

        @block.sync
        def _(sp):
            def load(g, b):
                tok = ds(g % B * N, N)
                for h in range(2):
                    row = (g // B * 4 + 2 * b + h) * HD
                    for dst, first, order in ((qs[b], 0, (0, 0, 1)), (ks[b], C, (0, 1, 0))):
                        for part, half in enumerate(order):
                            sp.dma_start(dst[part * HD:(part + 1) * HD, h, :],
                                         qk_dram[half, ds(first + row, HD), tok]).then_inc((head0_in if h == 0 else rest_in)[b], 16)
                sp.dma_start(vs[b][:], v_dram[tok, ds((g // B * 4 + 2 * b) * HD, 2 * HD)].rearrange(
                    "(t p) c -> p t c", p=P)).then_inc(rest_in[b], 16)

            def place_max(g, b):
                sp.wait_ge(neg_ready, 2 * g + b + 2)
                for h in range(2):
                    sp.dma_start(qs[b][3 * HD:PADK, h, :], neg_max[h * KT:(h + 1) * KT, :]).then_inc(max_placed[b], 16)

            for sem in (*m_scored[0], *m_taken[0]):
                sp.sem_inc(sem, UNITS)
            load(0, 0)
            sp.dma_start(den_ones[:], den_ones_dram).then_inc(const_in, 16)
            sp.dma_start(den_spread[:], den_spread_dram).then_inc(const_in, 16)
            load(0, 1)
            place_max(0, 0)
            with sp.Fori(0, GROUPS - 1) as g:
                place_max(g, 1)
                sp.wait_ge(valued, (2 * g + 1) * UNITS + 1)
                load(g + 1, 0)
                place_max(g + 1, 0)
                sp.wait_ge(valued, (2 * g + 2) * UNITS + 1)
                load(g + 1, 1)
            place_max(GROUPS - 1, 1)

        @block.tensor
        def _(pe):
            def scores(g, k, qc, b, kt):
                if not (isinstance(g, int) and g == k == qc == 0 and kt < 2):
                    pe.wait_ge(weighed, upto(g, k, UNITS, qc * KT + kt - 1))
                for h in range(2):
                    mm = pe.matmul(s_ps[kt % 2][:, h, 0:CH], ks[b][:, h, kt * P:(kt + 1) * P],
                                   qs[b][:, h, qc * CH:(qc + 1) * CH], start=True, stop=True)
                mm.then_inc(scored, 1)

            def max_products(bank, b, h, tile, part):
                return pe.matmul(bank[:, 0:CH], qs[b][0:3 * HD, h, ds(tile * P, P)],
                                 ks[b][0:3 * HD, h, part * CH:(part + 1) * CH], start=True, stop=True)

            def values(g, qc, b, kt):
                if kt == 0:
                    pe.wait_ge(acc_taken, upto(g, b, QC, qc))
                    if qc == 0:
                        pe.wait_ge(den_taken, upto(g, b, 1, 0))
                pe.wait_ge(weighed, upto(g, b, UNITS, qc * KT + kt + 1))
                num, low = halves(b)
                for h in range(2):
                    pe.matmul(acc_ps[num + h * HD:num + (h + 1) * HD, 0:CH], vs[b][:, kt, h * HD:(h + 1) * HD],
                              prob[:, kt % 3, h], start=kt == 0, stop=kt == KT - 1)

            def weight_sums(qc, b, kt):
                num, low = halves(b)
                for h in range(2):
                    mm = pe.matmul(acc_ps[low + h * HD:low + (h + 1) * HD, 0:CH], den_ones[:, qc],
                                   prob[:, kt % 3, h], start=qc == 0 and kt == 0, stop=qc == QC - 1 and kt == KT - 1)
                mm.then_inc(valued, 1)

            def spread(g, k, b, qc):
                pe.wait_ge(inverted, upto(g, k, 1, 1))
                pe.wait_ge(out_done, upto(g, k, QC, qc))
                pe.wait_ge(neg_ready, upto(g, k, 1, 2))
                pe.matmul(t_ps[:, 0:CH], den_spread[:, qc], rden[:], start=True, stop=True).then_inc(spreaded, 1)

            def turn_max(g, k):
                pe.wait_ge(row_ready, upto(g, k, 1, 1))
                pe.wait_ge(neg_ready, upto(g, k, 1, 0))
                pe.matmul(t_ps[0:2 * KT, 0:P], row_max[:].rearrange("p h t -> p (h t)"), ident[:],
                          start=True, stop=True).then_inc(turned, 1)

            def second_pass(g, b, first, last):
                for qc in range(QC):
                    before, h, tile, counts = max_schedule(qc)
                    step = 0
                    for kt in range(KT):
                        if kt < KT - 1:
                            scores(g, b, qc, b, kt + 1)
                        elif qc < QC - 1:
                            scores(g, b, qc + 1, b, 0)
                        elif not last:
                            pe.wait_ge(max_placed[1 - b], 32 * g + (32 * (b + 1) + 1))
                            scores(g, b + 1, 0, 1 - b, 0)
                        for turn in range(3):
                            if turn == 1:
                                values(g, qc, b, kt)
                            if turn == 2:
                                weight_sums(qc, b, kt)
                            if not last and turn < counts[kt]:
                                if step == 0 and qc == 0:
                                    pe.wait_ge(head0_in[1 - b], HEAD0 * (g + 1 + b) + 1)
                                if step == 0 and qc == 3:
                                    pe.wait_ge(rest_in[1 - b], REST * (g + 1 + b) + 1)
                                j, count = step % 2, (before + step) // 2
                                pe.wait_ge(m_taken[1 - b][j], g * UNITS + (b * UNITS + count + 1))
                                max_products(m_ps[:, j], 1 - b, h, tile + step // QC, step % QC).then_inc(
                                    m_scored[1 - b][j], 1)
                                step += 1
                        if kt == (3 if qc == QC - 1 else 9) and not first:
                            spread(g, b - 1, 1 - b, qc)
                        if kt == 9 and qc == QC - 1 and not last:
                            pe.wait_ge(out_done, upto(g, b, QC, 0) if not first else 1)
                            turn_max(g, b + 1)

            pe.wait_ge(const_in, 32 + 1)
            pe.wait_ge(ones_set, 4 + 1)
            pe.wait_ge(head0_in[0], HEAD0 + 1)
            banks = (m_ps, s_ps[0], s_ps[1])
            def first_products(h, tile, third):
                for j in range(2):
                    mm = max_products(banks[third][:, j], 0, h, tile, 2 * third + j)
                mm.then_inc(first_scored, 1)

            for third in range(3):
                first_products(0, 0, third)
            for h in range(2):
                if h == 1:
                    pe.wait_ge(rest_in[0], REST + 1)
                with pe.Fori(1 - h, KT) as tile:
                    for third in range(3):
                        pe.wait_ge(first_taken, 3 * (h * KT + tile) + third - 1)
                        first_products(h, tile, third)
            turn_max(0, 0)
            pe.wait_ge(max_placed[0], 32 + 1)
            scores(0, 0, 0, 0, 0)
            second_pass(0, 0, True, False)
            second_pass(0, 1, False, False)
            with pe.Fori(1, GROUPS - 1) as g:
                second_pass(g, 0, False, False)
                second_pass(g, 1, False, False)
            second_pass(GROUPS - 1, 0, False, False)
            second_pass(GROUPS - 1, 1, False, True)
            for qc in range(QC):
                pe.wait_ge(inverted, PAIRS + 1)
                pe.wait_ge(out_done, (PAIRS - 1) * QC + qc + 1)
                pe.matmul(t_ps[:, 0:CH], den_spread[:, qc], rden[:], start=True, stop=True).then_inc(spreaded, 1)

        @block.scalar
        def _(act):
            def weigh(chunk, kt):
                act.wait_ge(scored, chunk * KT + kt + 2)
                if not (isinstance(chunk, int) and chunk == 0 and kt < 3):
                    act.wait_ge(valued, chunk * KT + kt - 1)
                act.activation(prob[:, kt % 3], s_ps[kt % 2][:, :, 0:CH], ACT.Exp, scale=SCALE).then_inc(weighed, 1)

            def take(g, b, qc):
                num, low = halves(b)
                act.wait_ge(valued, ((2 * g + b) * QC + qc + 1) * KT + 1)
                act.activation(out_cm[num:num + 64, ds(g * N + qc * CH, CH)], acc_ps[num:num + 64, 0:CH],
                               ACT.Copy).then_inc(acc_taken, 1)

            def take_den(g, b):
                num, low = halves(b)
                act.wait_ge(inverted, 2 * g + b + 1)
                act.activation(den[low:low + 64, :], acc_ps[low:low + 64, 0:CH], ACT.Copy).then_inc(den_taken, 1)

            def pair_steps(g, b, last):
                chunk = (2 * g + b) * QC
                with act.Fori(0, QC - 1) as qc:
                    weigh(chunk + qc + 1, 0)
                    take(g, b, qc)
                    for kt in range(1, KT):
                        weigh(chunk + qc + 1, kt)
                if not last:
                    weigh(chunk + QC, 0)
                take(g, b, QC - 1)
                take_den(g, b)
                if not last:
                    for kt in range(1, KT):
                        weigh(chunk + QC, kt)

            for kt in range(KT):
                weigh(0, kt)
            with act.Fori(0, GROUPS - 1) as g:
                pair_steps(g, 0, False)
                pair_steps(g, 1, False)
            pair_steps(GROUPS - 1, 0, False)
            pair_steps(GROUPS - 1, 1, True)

        @block.vector
        def _(dve):
            for b in range(2):
                dve.memset(ks[b][3 * HD:PADK, :, :], 1.0).then_inc(ones_set, 1)
            dve.memset(rden[:], 0.0).then_inc(ones_set, 1)
            dve.memset(den[:], 1.0).then_inc(ones_set, 1)
            dve.wait_ge(ones_set, 4 + 1)

            def maximum(b, j, count, h, tile, part):
                dve.wait_ge(m_scored[b][j], count)
                dve.tensor_reduce(part_max[:, h, tile:tile + 1, part:part + 1], m_ps[:, j, 0:CH], AX.X,
                                  ALU.max).then_inc(m_taken[b][j], 1)

            def max_rows(g, b):
                pair = 2 * g + b
                if isinstance(g, int) and g == b == 0:
                    dve.wait_ge(first_taken, 3 * 2 * KT + 1)
                else:
                    for j in range(2):
                        dve.wait_ge(m_taken[b][j], (g + 1) * UNITS + 1)
                dve.wait_ge(turned, pair + 1)
                dve.tensor_reduce(row_max[:], part_max[:], AX.X, ALU.max).then_inc(row_ready, 1)
                dve.wait_ge(turned, pair + 2)
                dve.wait_ge(max_placed[1 - b], 32 * (g + b) + 1)
                dve.tensor_scalar(neg_max[:], t_ps[0:2 * KT, 0:P], -1.0, None, ALU.mult).then_inc(neg_ready, 1)

            def invert(g, b):
                num, low = halves(b)
                dve.wait_ge(den_taken, 2 * g + b + 2)
                dve.wait_ge(spreaded, (2 * g + b) * QC + 1)
                dve.reciprocal(rden[low:low + 64, :], den[low:low + 64, :]).then_inc(inverted, 1)

            def divide(g, b, qc):
                num, low = halves(b)
                dve.wait_ge(spreaded, upto(g, b, QC, qc + 1))
                dve.wait_ge(acc_taken, upto(g, b, QC, qc + 1))
                part = out_cm[num:num + 64, ds(g * N + qc * CH, CH)]
                dve.tensor_tensor(part, part, t_ps[num:num + 64, 0:CH], ALU.mult).then_inc(out_done, 1)

            def pair_steps(g, b, first, last):
                before_g = g - 1 + b
                if not first:
                    invert(before_g, 1 - b)
                for qc in range(QC):
                    before, h, tile, counts = max_schedule(qc)
                    step = 0
                    for kt in range(KT):
                        for _ in range(0 if last else counts[kt]):
                            maximum(1 - b, step % 2, g * UNITS + (b * UNITS + (before + step) // 2 + 2), h, tile + step // QC, step % QC)
                            step += 1
                        if kt == (3 if qc == QC - 1 else 9) and not first:
                            divide(before_g, 1 - b, qc)
                if not last:
                    max_rows(g + b, 1 - b)

            banks = (m_ps, s_ps[0], s_ps[1])
            for h in range(2):
                with dve.Fori(0, KT) as tile:
                    for third in range(3):
                        dve.wait_ge(first_scored, 3 * (h * KT + tile) + third + 2)
                        dve.tensor_reduce(part_max[:, h, ds(tile, 1), 2 * third:2 * third + 2].rearrange("p t j -> p (t j)"),
                                          banks[third][:, :, 0:CH], AX.X, ALU.max).then_inc(first_taken, 1)
            max_rows(0, 0)
            pair_steps(0, 0, True, False)
            pair_steps(0, 1, False, False)
            with dve.Fori(1, GROUPS - 1) as g:
                pair_steps(g, 0, False, False)
                pair_steps(g, 1, False, False)
            pair_steps(GROUPS - 1, 0, False, False)
            pair_steps(GROUPS - 1, 1, False, True)
            invert(GROUPS - 1, 1)
            for qc in range(QC):
                divide(GROUPS - 1, 1, qc)

        @block.gpsimd
        def _(pool):
            centre = [(0, 0)] + [(dy, dx) for dy in (-1, 0, 1) for dx in (-1, 0, 1) if (dy, dx) != (0, 0)]
            steps = 2 * len(centre)
            for g in range(GROUPS):
                tile, img = g // B, g % B
                base = g * steps
                image = v_cm[:, tile, img * N:(img + 1) * N].rearrange("p (y x) -> p y x", y=HW)
                total = tap_sum[:].rearrange("p (y x) -> p y x", y=HW)
                single = tap_one[:].rearrange("p (y x) -> p y x", y=HW)
                for n, (dy, dx) in enumerate(centre):
                    y0, y1 = max(0, -dy), HW - max(0, dy)
                    x0, x1 = max(0, -dx), HW - max(0, dx)
                    shifted = image[:, y0 + dy:y1 + dy, x0 + dx:x1 + dx]
                    tap = w_tap[:, tile, 3 * (dy + 1) + dx + 1:3 * (dy + 1) + dx + 2]
                    tap = tap.unsqueeze(2).broadcast_to([P, y1 - y0, x1 - x0])
                    if n == 0:
                        pool.wait_ge(tap_added, g + 1)
                        pool.tensor_tensor(total, shifted, tap, ALU.mult).then_inc(tap_step, 1)
                        pool.wait_ge(tap_step, base + 2)
                        pool.tensor_tensor(total, total, b_tap[:, tile:tile + 1].unsqueeze(2).broadcast_to([P, HW, HW]),
                                           ALU.add).then_inc(tap_step, 1)
                        continue
                    pool.wait_ge(tap_step, base + 2 * n + 1)
                    pool.tensor_tensor(single[:, y0:y1, x0:x1], shifted, tap, ALU.mult).then_inc(tap_step, 1)
                    pool.wait_ge(tap_step, base + 2 * n + 2)
                    pool.tensor_tensor(total[:, y0:y1, x0:x1], total[:, y0:y1, x0:x1],
                                       single[:, y0:y1, x0:x1], ALU.add).then_inc(tap_step, 1)
                pool.wait_ge(tap_step, base + steps + 1)
                pool.wait_ge(out_done, 2 * QC * (g + 1) + 1)
                part = out_cm[:, g * N:(g + 1) * N]
                pool.tensor_tensor(part, part, tap_sum[:], ALU.add).then_inc(tap_added, 1)


def window_parts(w):
    parts = {}
    for delta in range(-(QC - 1), QC):
        for sub in range(SUB):
            first, last = sub * P // HW, (sub * P + P - 1) // HW
            rows = [y for y in range(CH // HW)
                    if any(0 <= k + 8 * delta - y + w // 2 < w for k in range(first, last + 1))]
            if rows:
                parts[delta, sub] = (rows[0], rows[-1] + 1)
    return parts


def window_slots():
    slots = {}
    for w, window in enumerate(WINDOWS):
        for key in window_parts(window):
            slots[w, key] = len(slots)
    return slots


def window_steps(qc):
    parts = [window_parts(w) for w in WINDOWS]
    steps = []
    for kt in range(KT):
        key = (kt // SUB - qc, kt % SUB)
        hit = [w for w in range(len(WINDOWS)) if key in parts[w]]
        if hit:
            steps.append((kt, key, hit))
    return steps


def window_norms(core, qk_dram, k_tok, masks, mask_dram, head_sum_dram, rden):
    nc = core.nc
    slots = window_slots()
    parts = [window_parts(w) for w in WINDOWS]
    ROWS = len(WINDOWS) * HEADS
    W = len(WINDOWS)
    with ExitStack() as ctx:
        head_sum = core.sb(ctx, "head_sum", [P, W * CT, ROWS])
        q_half = core.sb(ctx, "q_half", [P, 2, 2, CH], F16)
        q32 = core.sb(ctx, "q32", [P, CH])
        weighed = core.sb(ctx, "weighed", [P, 3, CH])
        den = core.sb(ctx, "den", [ROWS, CH])
        box_ps = core.ps(ctx, "box_ps", [P, 6, 512])
        den_ps = core.ps(ctx, "den_ps", [P, 2, 512])
        const_in, cleared, boxed, multiplied, summed, guarded, inverted, q_whole = (
            core.sem(n) for n in ("const_in", "cleared", "boxed", "multiplied", "summed", "guarded", "inverted", "q_whole"))
        q_in = [core.sem("q_in") for _ in range(2)]
        block = ctx.enter_context(core.block())

        @block.sync
        def _(sp):
            sp.dma_start(masks[:], mask_dram).then_inc(const_in, 16)
            sp.dma_start(head_sum[:], head_sum_dram).then_inc(const_in, 16)
            with sp.Fori(0, NCH) as c:
                for m in range(CT):
                    sp.wait_ge(q_whole, CT * c + 1)
                    for half in range(2):
                        sp.dma_start(q_half[:, m, half], qk_dram[half, m * P:(m + 1) * P, ds(c * CH, CH)]).then_inc(q_in[m], 16)

        @block.tensor
        def _(pe):
            def head_sums(c, m, w):
                n = CT * W * c + m * W + w
                pe.wait_ge(multiplied, n + 2)
                pe.matmul(den_ps[0:ROWS, 0, 0:CH], head_sum[:, w * CT + m], weighed[:, w],
                          start=m == 0 and w == 0, stop=m == CT - 1 and w == W - 1).then_inc(summed, 1)

            pe.wait_ge(const_in, 32 + 1)
            for image in range(B):
                for qc in range(QC):
                    c = image * QC + qc
                    for m in range(CT):
                        for w in range(W):
                            pe.wait_ge(multiplied, CT * W * c + 1)
                            steps = [s for s in window_steps(qc) if w in s[2]]
                            for n, (kt, key, _) in enumerate(steps):
                                r0, r1 = parts[w][key] if n else (0, CH // HW)
                                cols = slice(r0 * HW, r1 * HW)
                                for half in range(2):
                                    mm = pe.matmul(box_ps[:, m * W + w, cols],
                                                   k_tok[half][:, image * KT + kt, m * P:(m + 1) * P],
                                                   masks[:, slots[w, key], cols], start=n == 0 and half == 0,
                                                   stop=n == len(steps) - 1 and half == 1)
                            mm.then_inc(boxed, 1)
                    pe.wait_ge(guarded, c + 1)
                    for m in range(CT):
                        for w in range(W):
                            head_sums(c, m, w)

        @block.gpsimd
        def _(pool):
            pool.memset(rden[:], 0.0).then_inc(cleared, 1)

        @block.vector
        def _(dve):
            dve.wait_ge(cleared, 1 + 1)
            with dve.Fori(0, NCH) as c:
                for m in range(CT):
                    dve.wait_ge(multiplied, CT * W * c + m * W + 1)
                    dve.wait_ge(q_in[m], 32 * (c + 1) + 1)
                    dve.tensor_tensor(q32[:], q_half[:, m, 0], q_half[:, m, 1], ALU.add).then_inc(q_whole, 1)
                    dve.wait_ge(q_whole, CT * c + m + 2)
                    for w in range(W):
                        n = CT * W * c + m * W + w
                        dve.wait_ge(boxed, n + 2)
                        dve.wait_ge(summed, n + 2 - W) if m else dve.wait_ge(summed, CT * W * c + 1)
                        dve.tensor_tensor(weighed[:, w], box_ps[:, m * W + w, 0:CH], q32[:], ALU.mult).then_inc(multiplied, 1)
                dve.wait_ge(summed, CT * W * (c + 1) + 1)
                dve.tensor_scalar(den[:], den_ps[0:ROWS, 0, 0:CH], 1e-6, None, ALU.add).then_inc(guarded, 1)
                dve.wait_ge(guarded, c + 2)
                dve.reciprocal(rden[0:ROWS, ds(c * CH, CH)], den[:]).then_inc(inverted, 1)


POOL_COST = 1.9


def window_attention(core, qk_dram, v_dram, masks, o_dram):
    nc = core.nc
    W = len(WINDOWS)
    parts = [window_parts(w) for w in WINDOWS]
    slots = window_slots()
    plan = [(qc, *step) for qc in range(QC) for step in window_steps(qc)]
    items = [(n, w) for n, (_, _, _, hit) in enumerate(plan) for w in hit]
    S, M = len(plan), len(items)
    first_of = [all(not (v == w and plan[a][0] == plan[n][0]) for a, v in items[:m]) for m, (n, w) in enumerate(items)]
    last_of = [all(not (v == w and plan[a][0] == plan[n][0]) for a, v in items[m + 1:]) for m, (n, w) in enumerate(items)]
    rows = [(0, CH // HW) if first_of[m] else parts[w][plan[n][2]] for m, (n, w) in enumerate(items)]
    on_pool, load = [], {True: 0.0, False: 0.0}
    for r0, r1 in rows:
        cost = {False: float(r1 - r0) + 0.5, True: POOL_COST * (r1 - r0) + 0.5}
        pick = load[True] + cost[True] < load[False] + cost[False]
        load[pick] += cost[pick]
        on_pool.append(pick)
    RING, WHOLE = 6, 5
    mine = {who: [m for m in range(M) if on_pool[m] == who] for who in (False, True)}
    with ExitStack() as ctx:
        qs = [core.sb(ctx, "qs", [3 * HD, 2, N], F16) for _ in range(2)]
        ks = [core.sb(ctx, "ks", [3 * HD, 2, N], F16) for _ in range(2)]
        vs = [core.sb(ctx, "vs", [P, KT, 2 * HD]) for _ in range(2)]
        whole = core.sb(ctx, "whole", [P, WHOLE, 2, CH])
        kept = {who: core.sb(ctx, "kept", [P, RING, 2, CH]) for who in (False, True)}
        result = core.sb(ctx, "result", [P, W, CH])
        s_ps = [core.ps(ctx, "s_ps", [P, 2, 512]) for _ in range(2)]
        acc_ps = core.ps(ctx, "acc_ps", [P, W, 512])
        scored, copied, masked_dve, masked_pool, valued, taken = (
            core.sem(n) for n in ("scored", "copied", "masked_dve", "masked_pool", "valued", "taken"))
        masked = {False: masked_dve, True: masked_pool}
        stored = [core.sem("stored") for _ in WINDOWS]
        loaded = [core.sem("loaded") for _ in range(2)]
        block = ctx.enter_context(core.block())

        def done_by(who, step):
            return sum(1 for m in mine[who] if items[m][0] <= step)

        def lane(qc, w):
            return 64 * ((qc + w) % 2)

        @block.sync
        def _(sp):
            def load(g, b):
                tok = ds(g % B * N, N)
                for h in range(2):
                    row = (g // B * 4 + 2 * b + h) * HD
                    for dst, first, order in ((qs[b], 0, (0, 0, 1)), (ks[b], C, (0, 1, 0))):
                        for part, half in enumerate(order):
                            sp.dma_start(dst[part * HD:(part + 1) * HD, h, :],
                                         qk_dram[half, ds(first + row, HD), tok]).then_inc(loaded[b], 16)
                sp.dma_start(vs[b][:], v_dram[tok, ds((g // B * 4 + 2 * b) * HD, 2 * HD)].rearrange(
                    "(t p) c -> p t c", p=P)).then_inc(loaded[b], 16)

            def store(g, b):
                for qc in range(QC):
                    for w in range(W):
                        sp.wait_ge(taken, W * ((2 * g + b) * QC + qc) + w + 2)
                        sp.dma_start(o_dram[w, ds((g // B * 4 + 2 * b) * HD, 2 * HD), ds(g % B * N + qc * CH, CH)],
                                     result[lane(qc, w):lane(qc, w) + 2 * HD, w]).then_inc(stored[w], 16)

            load(0, 0)
            load(0, 1)
            with sp.Fori(0, PAIRS // 2 - 1) as g:
                for b in range(2):
                    store(g, b)
                    load(g + 1, b)
            for b in range(2):
                store(PAIRS // 2 - 1, b)
            for w in range(W):
                sp.wait_ge(stored[w], 16 * PAIRS * QC + 1)

        @block.tensor
        def _(pe):
            def scores(pair, n, b):
                qc, kt, _, _ = plan[n]
                pe.wait_ge(copied, pair * S + (n - 1 if n >= 2 else 0) + 1)
                for h in range(2):
                    mm = pe.matmul(s_ps[n % 2][:, h, 0:CH], ks[b][:, h, kt * P:(kt + 1) * P],
                                   qs[b][:, h, qc * CH:(qc + 1) * CH], start=True, stop=True)
                mm.then_inc(scored, 1)

            def values(pair, b):
                scores(pair, 0, b)
                scores(pair, 1, b)
                for m, (n, w) in enumerate(items):
                    qc, kt, _, hit = plan[n]
                    if w == hit[0] and n + 2 < S:
                        scores(pair, n + 2, b)
                    cols = slice(rows[m][0] * HW, rows[m][1] * HW)
                    who, index = on_pool[m], mine[on_pool[m]].index(m)
                    if first_of[m]:
                        pe.wait_ge(taken, W * (pair * QC + max(qc - 1, 0)) + 1)
                    pe.wait_ge(masked[who], pair * len(mine[who]) + index + 2)
                    for h in range(2):
                        mm = pe.matmul(acc_ps[lane(qc, w) + h * HD:lane(qc, w) + (h + 1) * HD, w, cols],
                                       vs[b][:, kt, h * HD:(h + 1) * HD],
                                       kept[who][:, index % RING, h, cols], start=first_of[m], stop=last_of[m])
                    mm.then_inc(valued, 1)

            with pe.Fori(0, PAIRS // 2) as g:
                for b in range(2):
                    pe.wait_ge(loaded[b], 13 * 16 * (g + 1) + 1)
                    values(2 * g + b, b)

        @block.scalar
        def _(act):
            with act.Fori(0, PAIRS) as pair:
                def take(qc):
                    for w in range(W):
                        act.wait_ge(stored[w], 16 * (pair * QC + qc) + 1)
                        final = [m for m, (n, v) in enumerate(items) if v == w and plan[n][0] == qc][-1]
                        act.wait_ge(valued, pair * M + final + 2)
                        lanes = slice(lane(qc, w), lane(qc, w) + 2 * HD)
                        act.activation(result[lanes, w], acc_ps[lanes, w, 0:CH], ACT.Copy).then_inc(taken, 1)

                for n, (qc, _, _, _) in enumerate(plan):
                    if qc and plan[n - 2][0] == qc and plan[n - 3][0] != qc:
                        take(qc - 1)
                    act.wait_ge(scored, pair * S + n + 2)
                    for who, sem in ((False, masked_dve), (True, masked_pool)):
                        act.wait_ge(sem, pair * len(mine[who]) + (done_by(who, n - WHOLE) if n >= WHOLE else 0) + 1)
                    act.activation(whole[:, n % WHOLE], s_ps[n % 2][:, :, 0:CH], ACT.Copy).then_inc(copied, 1)
                take(QC - 1)

        def mask_items(engine, who, sem):
            with engine.Fori(0, PAIRS) as pair:
                for index, m in enumerate(mine[who]):
                    n, w = items[m]
                    engine.wait_ge(copied, pair * S + n + 2)
                    before = mine[who][index - RING] + 1 if index >= RING else 0
                    engine.wait_ge(valued, pair * M + before + 1)
                    cols = slice(rows[m][0] * HW, rows[m][1] * HW)
                    mask = masks[:, slots[w, plan[n][2]], cols].unsqueeze(1).broadcast_to(
                        [P, 2, (rows[m][1] - rows[m][0]) * HW])
                    engine.tensor_tensor(kept[who][:, index % RING, :, cols], whole[:, n % WHOLE, :, cols], mask,
                                         ALU.mult).then_inc(sem, 1)

        @block.vector
        def _(dve):
            mask_items(dve, False, masked_dve)

        @block.gpsimd
        def _(pool):
            mask_items(pool, True, masked_pool)


def project_out(core, x_cm, weight, bias, tiles, o_cm=None, o_dram=None, rden=None, spread=None, fetch=()):
    nc = core.nc
    scaled_too = o_dram is not None
    with ExitStack() as ctx:
        stage = core.sb(ctx, "stage", [P, 2, tiles, CH]) if scaled_too else None
        y_ps = core.ps(ctx, "y_ps", [P, 4, 512])
        r_ps = core.ps(ctx, "r_ps", [P, 3, 512])
        made, added, spreaded, scaled, const_in = (
            core.sem(n) for n in ("made", "added", "spreaded", "scaled", "const_in"))
        fetched = [core.sem("fetched") for _ in range(2)]
        block = ctx.enter_context(core.block())

        @block.sync
        def _(sp):
            for dst, src in fetch:
                sp.dma_start(dst[:], src).then_inc(const_in, 16)
            if scaled_too:
                with sp.Fori(0, NCH // 2) as i:
                    for b in range(2):
                        sp.wait_ge(made, 4 * i + 1)
                        sp.dma_start(stage[:, b], o_dram[:, ds((2 * i + b) * CH, CH)].rearrange(
                            "(k p) t -> p k t", p=P)).then_inc(fetched[b], 16)

        @block.tensor
        def _(pe):
            if fetch:
                pe.wait_ge(const_in, 16 * len(fetch) + 1)
            with pe.Fori(0, NCH // 2) as i:
                for b in range(2):
                    chunk = ds((2 * i + b) * CH, CH)
                    if scaled_too:
                        for k in range(tiles):
                            pe.wait_ge(scaled, (2 * i + b) * tiles + k - 1) if b or k >= 3 else \
                                pe.wait_ge(scaled, 2 * i * tiles + 1)
                            pe.matmul(r_ps[:, k % 3, 0:CH], spread[:, k], rden[:, chunk],
                                      start=True, stop=True).then_inc(spreaded, 1)
                        pe.wait_ge(scaled, (2 * i + b + 1) * tiles + 1)
                    for m in range(CT):
                        pe.wait_ge(added, 4 * i + 1)
                        for k in range(tiles):
                            src = stage[:, b, k] if scaled_too else o_cm[:, k, chunk]
                            mm = pe.matmul(y_ps[:, 2 * b + m, 0:CH], weight[:, k, m * P:(m + 1) * P], src,
                                           start=k == 0, stop=k == tiles - 1)
                        mm.then_inc(made, 1)

        @block.vector
        def _(dve):
            with dve.Fori(0, NCH // 2) as i:
                for b in range(2):
                    if scaled_too:
                        dve.wait_ge(fetched[b], 16 * (i + 1) + 1)
                        for k in range(tiles):
                            dve.wait_ge(spreaded, (2 * i + b) * tiles + k + 2)
                            dve.tensor_tensor(stage[:, b, k], stage[:, b, k], r_ps[:, k % 3, 0:CH],
                                              ALU.mult).then_inc(scaled, 1)
                    for m in range(CT):
                        dve.wait_ge(made, 4 * i + 2 * b + m + 2)
                        x = x_cm[:, m, ds((2 * i + b) * CH, CH)]
                        dve.scalar_tensor_tensor(out=x, in0=y_ps[:, 2 * b + m, 0:CH], scalar=bias[:, m:m + 1], in1=x,
                                                 op0=ALU.add, op1=ALU.add).then_inc(added, 1)


def route(core, th, tl, wr, br, comb, iota):
    nc = core.nc
    wr_hi, wr_lo = wr
    with ExitStack() as ctx:
        big = [P, TT, E]
        small = [P, TT]
        logits, work, hot1, hot2, prob = (core.sb(ctx, n, big) for n in ("logits", "work", "hot1", "hot2", "prob"))
        top, index, total, rest = (core.sb(ctx, n, small) for n in ("top", "index", "total", "rest"))
        l_ps = core.ps(ctx, "l_ps", [P, 512])
        made, step, exped = core.sem("made"), core.sem("step"), core.sem("exped")
        block = ctx.enter_context(core.block())
        wide = lambda t: t[:].unsqueeze(2).broadcast_to(big)
        experts = iota[:, 0:E].unsqueeze(1).broadcast_to(big)

        @block.tensor
        def _(pe):
            with pe.Fori(0, TT) as t:
                out = l_ps[:, ds(t * E, E)]
                tok = ds(t * P, P)
                for k in range(CT):
                    pe.matmul(out, th[:, k, tok], wr_hi[:, k, :], start=k == 0, stop=False)
                    pe.matmul(out, tl[:, k, tok], wr_hi[:, k, :], start=False, stop=False)
                    mm = pe.matmul(out, th[:, k, tok], wr_lo[:, k, :], start=False, stop=k == CT - 1)
                mm.then_inc(made, 1)

        @block.scalar
        def _(act):
            act.wait_ge(step, 3 + 1)
            act.activation(prob[:], work[:], ACT.Exp).then_inc(exped, 1)

        @block.vector
        def _(dve):
            count = 0

            def then(ins):
                nonlocal count
                count += 1
                ins.then_inc(step, 1)
                dve.wait_ge(step, count + 1)

            dve.wait_ge(made, TT + 1)
            scores = l_ps[:, 0:TT * E].rearrange("p (t e) -> p t e", e=E)
            if br is None:
                then(dve.tensor_copy(logits[:], scores))
            else:
                then(dve.tensor_tensor(logits[:], scores, br.unsqueeze(1).broadcast_to(big), ALU.add))
            then(dve.tensor_reduce(top[:], logits[:], AX.X, ALU.max))
            then(dve.tensor_tensor(work[:], logits[:], wide(top), ALU.subtract))
            dve.wait_ge(exped, 1 + 1)
            then(dve.tensor_reduce(total[:], prob[:], AX.X, ALU.add))
            then(dve.reciprocal(total[:], total[:]))
            then(dve.tensor_tensor(prob[:], prob[:], wide(total), ALU.mult))
            for hot in (hot1, hot2):
                then(dve.tensor_tensor(work[:], logits[:], wide(top), ALU.is_lt))
                then(dve.scalar_tensor_tensor(out=work[:], in0=work[:], scalar=float(E), in1=experts,
                                              op0=ALU.mult, op1=ALU.add))
                then(dve.tensor_reduce(index[:], work[:], AX.X, ALU.min))
                then(dve.tensor_tensor(hot[:], experts, wide(index), ALU.is_equal))
                if hot is hot1:
                    then(dve.scalar_tensor_tensor(out=logits[:], in0=hot[:], scalar=-3.0e38, in1=logits[:],
                                                  op0=ALU.mult, op1=ALU.add))
                    then(dve.tensor_reduce(top[:], logits[:], AX.X, ALU.max))
            then(dve.tensor_tensor(hot1[:], hot1[:], hot2[:], ALU.add))
            then(dve.tensor_tensor(prob[:], prob[:], hot1[:], ALU.mult))
            then(dve.tensor_reduce(total[:], prob[:], AX.X, ALU.add))
            then(dve.tensor_scalar(total[:], total[:], 1e-12, None, ALU.max))
            then(dve.reciprocal(rest[:], total[:]))
            then(dve.tensor_tensor(comb[:], prob[:], wide(rest), ALU.mult))


def experts(core, x_cm, xh, xl, comb, w1, b1, w2, b2, hidden, ident, one, ln_g=None, ln_b=None):
    nc = core.nc
    MT = hidden // P
    HR = 4
    FIRST = NCH // 4 if ln_g is not None else NCH // 2
    w1_v = w1.rearrange("e (k p) h -> e p k h", p=P)
    w2_v = w2.rearrange("e (k p) c -> e p k c", p=P)
    with ExitStack() as outer:
        acc = core.sb(outer, "acc", [P, TT, C])
        with ExitStack() as ctx:
            w1_in = core.sb(ctx, "w1_in", [P, CT, hidden])
            w2_in = core.sb(ctx, "w2_in", [P, MT, C])
            w1s = [[core.sb(ctx, "w1s", [P, CT, hidden], F16) for _ in range(2)] for _ in range(2)]
            w2s = [[core.sb(ctx, "w2s", [P, MT, C], F16) for _ in range(2)] for _ in range(2)]
            b1_all = core.sb(ctx, "b1_all", [P, E, MT])
            bias1 = core.sb(ctx, "bias1", [P, 2, MT])
            h32 = core.sb(ctx, "h32", [P, 2, CH])
            hh = core.sb(ctx, "hh", [P, 2, MT, CH], F16)
            hl = core.sb(ctx, "hl", [P, 2, MT, CH], F16)
            g_all = core.sb(ctx, "g_all", [P, E, CT])
            b_all = core.sb(ctx, "b_all", [P, E, CT])
            h_ps = core.ps(ctx, "h_ps", [P, HR, 512])
            y_ps = core.ps(ctx, "y_ps", [P, 3, 512])
            bias_ps = core.ps(ctx, "bias_ps", [P, 512])
            small_in, w_in = core.sem("small_in"), core.sem("w_in")
            zeroed = core.sem("zeroed")
            scaled, split, bias_made, bias_ready = (core.sem(n) for n in ("scaled", "split", "bias_made", "bias_ready"))
            h_made, h_ready, h_hi, h_split, y_taken = (
                core.sem(n) for n in ("h_made", "h_ready", "h_hi", "h_split", "y_taken"))
            y_made = [core.sem("y_made") for _ in range(2)]
            block = ctx.enter_context(core.block())
            norm = ln_g is not None

            @block.sync
            def _(sp):
                sp.dma_start(b1_all[:], b1).then_inc(small_in, 16)
                if norm:
                    sp.dma_start(g_all[:], ln_g).then_inc(small_in, 16)
                    sp.dma_start(b_all[:], ln_b).then_inc(small_in, 16)
                for e in range(E):
                    sp.wait_ge(split, 4 * e + 1)
                    sp.wait_ge(bias_ready, e + 1)
                    sp.dma_start(w1_in[:], w1_v[e]).then_inc(w_in, 16)
                    sp.dma_start(w2_in[:], w2_v[e]).then_inc(w_in, 16)

            @block.gpsimd
            def _(pool):
                pool.wait_ge(small_in, (48 if norm else 16) + 1)

                def prepare(i, b):
                    e = 2 * i + b
                    pool.wait_ge(w_in, 32 * (e + 1) + 1)
                    if not isinstance(i, int):
                        for made in y_made:
                            pool.wait_ge(made, TT // 2 * (2 * i - 1 + b) + 1)
                    if norm:
                        pool.wait_ge(bias_made, e + 2)
                        for k in range(CT):
                            pool.tensor_tensor(w1_in[:, k], w1_in[:, k], g_all[:, ds(e, 1), k].broadcast_to([P, hidden]),
                                               ALU.mult).then_inc(scaled, 1)
                        pool.wait_ge(scaled, 2 * (e + 1) + 1)
                    copy(pool, w1s[b][0][:], w1_in[:], one).then_inc(split, 1)
                    copy(pool, w2s[b][0][:], w2_in[:], one).then_inc(split, 1)
                    pool.wait_ge(split, 4 * e + 3)
                    pool.tensor_tensor(w1s[b][1][:], w1_in[:], w1s[b][0][:], ALU.subtract).then_inc(split, 1)
                    pool.tensor_tensor(w2s[b][1][:], w2_in[:], w2s[b][0][:], ALU.subtract).then_inc(split, 1)

                prepare(0, 0)
                prepare(0, 1)
                with pool.Fori(1, E // 2) as i:
                    prepare(i, 0)
                    prepare(i, 1)

            @block.tensor
            def _(pe):
                if norm:
                    pe.wait_ge(small_in, 48 + 1)

                def bias_products(e):
                    pe.wait_ge(w_in, 32 * (e + 1) + 1)
                    pe.wait_ge(bias_ready, e + 1)
                    for m in range(MT):
                        for k in range(CT):
                            mm = pe.matmul(bias_ps[:, m:m + 1], w1_in[:, k, m * P:(m + 1) * P],
                                           b_all[:, ds(e, 1), k], start=k == 0, stop=k == CT - 1)
                    mm.then_inc(bias_made, 1)

                if norm:
                    bias_products(0)

                def hidden_products(b, e, j, s):
                    c = e * NCH + 2 * j + s
                    chunk = ds((2 * j + s) * CH, CH)
                    for m in range(MT):
                        pe.wait_ge(h_ready, 2 * MT * (e * (NCH // 2) + j) + 1) if s * MT + m < HR else \
                            pe.wait_ge(h_ready, c * MT + m + 2 - HR)
                        for k in range(CT):
                            mm = split_matmul(pe, h_ps[:, m % HR, 0:CH] if MT >= HR else h_ps[:, s * MT + m, 0:CH],
                                              w1s[b][0][:, k, m * P:(m + 1) * P], w1s[b][1][:, k, m * P:(m + 1) * P],
                                              xh[:, k, chunk], xl[:, k, chunk], k == 0, k == CT - 1)
                        mm.then_inc(h_made, 1)

                def output_products(b, e, j, s):
                    c = e * NCH + 2 * j + s
                    pe.wait_ge(h_split, (c + 1) * MT + 1)
                    for t in range(SUB):
                        pe.wait_ge(y_taken, c * SUB + 1)
                        tok = slice(t * P, (t + 1) * P)
                        for m in range(MT):
                            pe.matmul(y_ps[:, t, 0:C], hh[:, s, m, tok], w2s[b][0][:, m, :], start=m == 0, stop=False)
                            pe.matmul(y_ps[:, t, 0:C], hl[:, s, m, tok], w2s[b][0][:, m, :], start=False, stop=False)
                            mm = pe.matmul(y_ps[:, t, 0:C], hh[:, s, m, tok], w2s[b][1][:, m, :],
                                           start=False, stop=m == MT - 1)
                        mm.then_inc(y_made[s], 1)

                def part_of_chunks(b, e, j0, j1):
                    hidden_products(b, e, j0, 0)
                    with pe.Fori(j0, j1 - 1) as j:
                        hidden_products(b, e, j, 1)
                        output_products(b, e, j, 0)
                        hidden_products(b, e, j + 1, 0)
                        output_products(b, e, j, 1)
                    hidden_products(b, e, j1 - 1, 1)
                    output_products(b, e, j1 - 1, 0)
                    output_products(b, e, j1 - 1, 1)

                def expert_steps(i, next_too):
                    for b in range(2):
                        e = 2 * i + b
                        pe.wait_ge(split, 4 * (e + 1) + 1)
                        part_of_chunks(b, e, 0, FIRST)
                        if b == 0 or next_too:
                            if norm:
                                bias_products(e + 1)
                        if FIRST < NCH // 2:
                            part_of_chunks(b, e, FIRST, NCH // 2)

                with pe.Fori(0, E // 2 - 1) as i:
                    expert_steps(i, True)
                expert_steps(E // 2 - 1, False)

            @block.scalar
            def _(act):
                act.wait_ge(small_in, (48 if norm else 16) + 1)
                with act.Fori(0, E // 2) as i:
                    for b in range(2):
                        e = 2 * i + b
                        act.wait_ge(bias_ready, e + 2)
                        with act.Fori(0, NCH // 2) as j:
                            for s in range(2):
                                c = e * NCH + 2 * j + s
                                for m in range(MT):
                                    act.wait_ge(h_made, c * MT + m + 2)
                                    act.wait_ge(h_split, c * MT + m - 1 + 1) if (s or m >= 2) else \
                                        act.wait_ge(h_split, 2 * MT * (e * (NCH // 2) + j) + 1)
                                    bank = h_ps[:, m % HR, 0:CH] if MT >= HR else h_ps[:, s * MT + m, 0:CH]
                                    act.activation(h32[:, m % 2], bank, ACT.Gelu,
                                                   bias=bias1[:, b, m:m + 1]).then_inc(h_ready, 1)
                                    if m == 0:
                                        act.wait_ge(y_made[s], SUB * (e * (NCH // 2) + j) + 1)
                                    act.wait_ge(h_ready, c * MT + m + 2)
                                    act.activation(hh[:, s, m], h32[:, m % 2], ACT.Copy).then_inc(h_hi, 1)

            @block.vector
            def _(dve):
                dve.memset(acc[:], 0.0).then_inc(zeroed, 1)
                dve.wait_ge(zeroed, 1 + 1)
                dve.wait_ge(small_in, (48 if norm else 16) + 1)

                def bias(e, half):
                    b1_one = b1_all[:, ds(e, 1), :].rearrange("p e m -> p (e m)")
                    if norm:
                        dve.wait_ge(bias_made, e + 2)
                        dve.tensor_tensor(bias1[:, half], bias_ps[:, 0:MT], b1_one, ALU.add).then_inc(bias_ready, 1)
                    else:
                        dve.tensor_copy(bias1[:, half], b1_one).then_inc(bias_ready, 1)

                def split_hidden(e, j, s):
                    c = e * NCH + 2 * j + s
                    dve.wait_ge(y_made[s], SUB * (e * (NCH // 2) + j) + 1)
                    for m in range(MT):
                        dve.wait_ge(h_hi, c * MT + m + 2)
                        dve.tensor_tensor(hl[:, s, m], h32[:, m % 2], hh[:, s, m], ALU.subtract).then_inc(h_split, 1)

                def add_output(e, j, s):
                    for t in range(SUB):
                        dve.wait_ge(y_made[s], SUB * (e * (NCH // 2) + j) + t + 2)
                        tile = ds((2 * j + s) * SUB + t, 1)
                        weight = comb[:, tile, ds(e, 1)].rearrange("p t e -> p (t e)")
                        mine = acc[:, tile, :].rearrange("p t c -> p (t c)")
                        dve.scalar_tensor_tensor(out=mine, in0=y_ps[:, t, 0:C], scalar=weight, in1=mine,
                                                 op0=ALU.mult, op1=ALU.add).then_inc(y_taken, 1)

                def part_of_chunks(e, j0, j1):
                    split_hidden(e, j0, 0)
                    with dve.Fori(j0, j1 - 1) as j:
                        split_hidden(e, j, 1)
                        add_output(e, j, 0)
                        split_hidden(e, j + 1, 0)
                        add_output(e, j, 1)
                    split_hidden(e, j1 - 1, 1)
                    add_output(e, j1 - 1, 0)
                    add_output(e, j1 - 1, 1)

                def expert_steps(i, next_too):
                    for b in range(2):
                        e = 2 * i + b
                        part_of_chunks(e, 0, FIRST)
                        if b == 0 or next_too:
                            bias(e + 1, 1 - b)
                        if FIRST < NCH // 2:
                            part_of_chunks(e, FIRST, NCH // 2)

                bias(0, 0)
                with dve.Fori(0, E // 2 - 1) as i:
                    expert_steps(i, True)
                expert_steps(E // 2 - 1, False)
        core.end_phase()
        add_tokens(core, x_cm, acc, ident, comb, b2)
        core.end_phase()


def add_tokens(core, x_cm, acc, ident, comb, b2):
    nc = core.nc
    with ExitStack() as ctx:
        stage = core.sb(ctx, "stage", [P, 2, SUB, C])
        weights = core.sb(ctx, "weights", [P, 2, SUB, P])
        turned_weights = core.sb(ctx, "turned_weights", [P, 2, CH])
        b2_rows = core.sb(ctx, "b2_rows", [P, C])
        t_ps = core.ps(ctx, "t_ps", [P, 2, CT, 512])
        w_ps = core.ps(ctx, "w_ps", [P, 2, 512])
        cleared, b2_in, weighed, w_turned, w_ready = (
            core.sem(n) for n in ("cleared", "b2_in", "weighed", "w_turned", "w_ready"))
        staged, turned, added = core.sem("staged"), core.sem("turned"), core.sem("added")
        block = ctx.enter_context(core.block())

        @block.sync
        def _(sp):
            sp.wait_ge(cleared, 2 + 1)
            sp.dma_start(b2_rows[0:E, :], b2).then_inc(b2_in, 16)

        @block.scalar
        def _(act):
            with act.Fori(0, NCH // 2) as i:
                for b in range(2):
                    act.wait_ge(turned, 2 * i + 1)
                    act.activation(stage[:, b], acc[:, ds((2 * i + b) * SUB, SUB), :], ACT.Copy).then_inc(staged, 1)
                for b in range(2):
                    act.wait_ge(w_turned, 2 * i + b + 2)
                    act.wait_ge(turned, 2 * i + 1)
                    act.activation(turned_weights[:, b], w_ps[:, b, 0:CH], ACT.Copy).then_inc(w_ready, 1)

        @block.gpsimd
        def _(pool):
            pool.memset(weights[:], 0.0).then_inc(cleared, 1)
            pool.memset(b2_rows[:], 0.0).then_inc(cleared, 1)

        @block.tensor
        def _(pe):
            pe.wait_ge(b2_in, 16 + 1)
            with pe.Fori(0, NCH // 2) as i:
                for b in range(2):
                    pe.wait_ge(weighed, 2 * i + b + 2)
                    pe.wait_ge(w_ready, 2 * i + 1)
                    for t in range(SUB):
                        mm = pe.transpose(w_ps[:, b, t * P:(t + 1) * P], weights[:, b, t], ident[:])
                    mm.then_inc(w_turned, 1)
                for b in range(2):
                    pe.wait_ge(staged, 2 * i + b + 2)
                    pe.wait_ge(w_ready, 2 * i + b + 2)
                    pe.wait_ge(added, 2 * i + 1)
                    for k in range(CT):
                        pe.matmul(t_ps[:, b, k, 0:CH], b2_rows[:, k * P:(k + 1) * P], turned_weights[:, b],
                                  start=True, stop=False)
                        for t in range(SUB):
                            mm = pe.matmul(t_ps[:, b, k, t * P:(t + 1) * P], stage[:, b, t, k * P:(k + 1) * P], ident[:],
                                           start=False, stop=t == SUB - 1)
                    mm.then_inc(turned, 1)

        @block.vector
        def _(dve):
            dve.wait_ge(cleared, 2 + 1)
            with dve.Fori(0, NCH // 2) as i:
                for b in range(2):
                    dve.wait_ge(w_turned, 2 * i + 1)
                    dve.tensor_copy(weights[:, b, :, 0:E], comb[:, ds((2 * i + b) * SUB, SUB), :]).then_inc(weighed, 1)
                for b in range(2):
                    dve.wait_ge(turned, 2 * i + b + 2)
                    x = x_cm[:, :, ds((2 * i + b) * CH, CH)]
                    dve.tensor_tensor(x, t_ps[:, b, :, 0:CH], x, ALU.add).then_inc(added, 1)


def metaformer(nc, ins, out):
    with ExitStack() as keep:
        core = Core(nc, keep)
        qk_dram = nc.dram_tensor("qk_scratch", [2, 2 * C, T], F16, kind="Internal").ap()
        v_dram = nc.dram_tensor("v_scratch", [T, C], F32, kind="Internal").ap()
        o_dram = nc.dram_tensor("o_scratch", [3, C, T], F32, kind="Internal").ap()
        x_cm = core.sb(keep, "x_cm", [P, CT, T])
        ones = core.sb(keep, "ones", [P, P])
        ones32 = core.sb(keep, "ones32", [P, HD])
        ident = core.sb(keep, "ident", [P, P])
        iota = core.sb(keep, "iota", [P, E])
        eps5, eps6 = core.sb(keep, "eps5", [P, 1]), core.sb(keep, "eps6", [P, 1])
        small = {}
        for name, shape in (("b_proj", [P, CT]), ("b_out", [P, CT]), ("b_tap", [P, CT]), ("w_tap", [P, CT, 9]),
                            ("br", [P, E])):
            small[name] = core.sb(keep, name, shape)

        wqk1 = [core.sb(keep, "wqk1", [P, 4 * CT * P], F16) for _ in range(2)]
        wv1 = [core.sb(keep, "wv1", [P, CT, C], F16) for _ in range(2)]
        wr0, wr1 = ([core.sb(keep, "wr", [P, CT, E], F16) for _ in range(2)] for _ in range(2))
        w_proj = core.sb(keep, "w_proj", [P, CT, C])
        var_rows = core.sb(keep, "var_rows", [P, NCH, 32])
        row_spread = core.sb(keep, "row_spread", [32, NCH, P])
        norm_const = ones, var_rows, row_spread

        loaded, const_set, ident_zero = core.sem("loaded"), core.sem("const_set"), core.sem("ident_zero")
        with core.block() as block:
            @block.sync
            def _(sp):
                for b in range(B):
                    for k in range(CT):
                        sp.dma_start(x_cm[:, k, b * N:(b + 1) * N], ins["x"][b, k * P:(k + 1) * P, :]).then_inc(loaded, 16)
                for name, src in (("b_proj", "L0_conv_b_proj"), ("b_out", "L1_conv_bout"), ("b_tap", "L0_conv_b_lepe")):
                    sp.dma_start(small[name][:], ins[src]).then_inc(loaded, 16)
                sp.dma_start(small["w_tap"][:], ins["L0_conv_w_lepe"]).then_inc(loaded, 16)
                sp.dma_start(small["br"][:], ins["L0_ffn_br"].broadcast_to([P, E])).then_inc(loaded, 16)
                sp.dma_start(w_proj[:], ins["w_proj"]).then_inc(loaded, 16)
                sp.dma_start(var_rows[:], ins["var_rows"]).then_inc(loaded, 16)
                sp.dma_start(row_spread[:], ins["row_spread"]).then_inc(loaded, 16)
                sp.wait_ge(loaded, 16 * 12 + 1)

            @block.gpsimd
            def _(pool):
                pool.memset(ones[:], 1.0 / C).then_inc(const_set, 1)
                pool.memset(ones32[:], 1.0).then_inc(const_set, 1)
                pool.memset(eps5[:], 1e-5).then_inc(const_set, 1)
                pool.memset(eps6[:], 1e-6).then_inc(const_set, 1)
                pool.memset(ident[:], 0.0).then_inc(ident_zero, 1)
                pool.wait_ge(ident_zero, 1 + 1)
                pool.affine_select(out=ident[:], in_=ident[:], compare_op=ALU.not_equal, fill=1.0, base=0,
                                   pattern=[[-1, P]], channel_multiplier=1).then_inc(const_set, 1)
                pool.iota(iota[:], pattern=[[1, E]], base=0, channel_multiplier=0,
                          allow_small_or_imprecise_dtypes=True).then_inc(const_set, 1)

        core.end_phase()

        with ExitStack() as ctx:
            v_cm = core.sb(ctx, "v_cm", [P, CT, T])
            with ExitStack() as proj:
                xh, xl = core.sb(proj, "xh", [P, CT, T], F16), core.sb(proj, "xl", [P, CT, T], F16)
                wqk = [core.sb(proj, "wqk", [P, 4 * CT * P], F16) for _ in range(2)]
                wv = [core.sb(proj, "wv", [P, CT, C], F16) for _ in range(2)]
                split_weights(core, [(ins["w_qk0"], wqk[0][:], wqk[1][:]), (ins["w_v0"], wv[0][:], wv[1][:]),
                                     (ins["w_qk1"], wqk1[0][:], wqk1[1][:]), (ins["w_v1"], wv1[0][:], wv1[1][:]),
                                     (ins["w_r0"], wr0[0][:], wr0[1][:]), (ins["w_r1"], wr1[0][:], wr1[1][:])])
                core.end_phase()
                layer_norm(core, x_cm, xh, xl, norm_const, eps6)
                core.end_phase()
                project(core, xh, xl, wqk, wv, qk_dram, v_dram, v_cm, sigmoid=False)
                core.end_phase()
            out_cm = core.sb(ctx, "out_cm", [P, CT * T])
            softmax_attention(core, qk_dram, v_dram, v_cm, small["w_tap"], small["b_tap"], out_cm, ident,
                              ins["den_ones"], ins["den_spread"])
            core.end_phase()
            project_out(core, x_cm, w_proj, small["b_proj"], CT, o_cm=out_cm[:].rearrange("p (k t) -> p k t", k=CT))
            core.end_phase()

        with ExitStack() as ctx:
            comb = core.sb(ctx, "comb", [P, TT, E])
            xh, xl = core.sb(ctx, "xh", [P, CT, T], F16), core.sb(ctx, "xl", [P, CT, T], F16)
            with ExitStack() as inner:
                t32 = core.sb(inner, "t32", [P, CT, T])
                layer_norm(core, x_cm, xh, xl, norm_const, eps5, whole=t32)
                core.end_phase()
                route(core, xh, xl, wr0, small["br"][:], comb, iota)
                core.end_phase()
                layer_norm(core, t32, xh, xl, norm_const, eps5)
                core.end_phase()
            experts(core, x_cm, xh, xl, comb, ins["L0_ffn_W1"], ins["L0_ffn_b1"], ins["L0_ffn_W2"], ins["L0_ffn_b2"],
                    1024, ident, ones32[:, 0:1], ins["L0_ffn_ln_g"], ins["L0_ffn_ln_b"])

        with ExitStack() as ctx:
            rden = core.sb(ctx, "rden", [P, T])
            with ExitStack() as windows:
                masks = core.sb(windows, "masks", [P, len(window_slots()), CH], F16)
                with ExitStack() as tokens:
                    k_area = core.sb(tokens, "k_area", [P, CT, T])
                    k_tok = [half.rearrange("p (t c) -> p t c", c=C) for half in
                             (k_area[:].bitcast(F16).rearrange("p k t -> p (k t)")[:, n * TT * C:(n + 1) * TT * C] for n in range(2))]
                    with ExitStack() as proj:
                        xh, xl = core.sb(proj, "xh", [P, CT, T], F16), core.sb(proj, "xl", [P, CT, T], F16)
                        layer_norm(core, x_cm, xh, xl, norm_const, eps6, whole=k_area)
                        core.end_phase()
                        project(core, xh, xl, wqk1, wv1, qk_dram, v_dram, None, sigmoid=True, k_tok=k_tok)
                        core.end_phase()
                    window_norms(core, qk_dram, k_tok, masks, ins["masks"], ins["head_sum"], rden)
                    core.end_phase()
                window_attention(core, qk_dram, v_dram, masks, o_dram)
                core.end_phase()
            w_out = core.sb(ctx, "w_out", [P, 3 * CT, C])
            spread = core.sb(ctx, "spread", [P, 3 * CT, P])
            project_out(core, x_cm, w_out, small["b_out"], 3 * CT, o_dram=o_dram.rearrange("w c t -> (w c) t"),
                        rden=rden, spread=spread, fetch=((w_out, ins["w_out"]), (spread, ins["head_spread"])))
            core.end_phase()

        with ExitStack() as ctx:
            comb = core.sb(ctx, "comb", [P, TT, E])
            xh, xl = core.sb(ctx, "xh", [P, CT, T], F16), core.sb(ctx, "xl", [P, CT, T], F16)
            with ExitStack() as inner:
                layer_norm(core, x_cm, xh, xl, norm_const, eps5, add_back=True)
                core.end_phase()
                route(core, xh, xl, wr1, None, comb, iota)
                core.end_phase()
            experts(core, x_cm, xh, xl, comb, ins["L1_ffn_w1"], ins["L1_ffn_b1"], ins["L1_ffn_w2"], ins["L1_ffn_b2"],
                    256, ident, ones32[:, 0:1])

        stored = core.sem("stored")
        with core.block() as block:
            @block.sync
            def _(sp):
                for b in range(B):
                    for k in range(CT):
                        sp.dma_start(out[b, k * P:(k + 1) * P, :], x_cm[:, k, b * N:(b + 1) * N]).then_inc(stored, 16)
                sp.wait_ge(stored, 64 + 1)


def window_masks(np):
    tiles = []
    for w in WINDOWS:
        for delta, sub in window_parts(w):
            key = sub * P + np.arange(P)
            query = np.arange(CH)
            dy = (key // HW)[:, None] + 8 * delta - (query // HW)[None, :]
            dx = (key % HW)[:, None] - (query % HW)[None, :]
            seen = (dy >= -(w // 2)) & (dy < w // 2) & (dx >= -(w // 2)) & (dx < w // 2)
            tiles.append(seen.astype(np.float16))
    return np.ascontiguousarray(np.stack(tiles, 1))


def kernel(**inputs):
    import numpy as np
    import concourse.bacc as bacc
    from concourse.bass_utils import run_bass_kernel_spmd as run

    a = {k: np.asarray(v) for k, v in inputs.items()}

    def tiled(w):
        return np.ascontiguousarray(w.reshape(-1, P, w.shape[1]).transpose(1, 0, 2))

    def by_channel(v):
        return np.ascontiguousarray(np.moveaxis(v.reshape(*v.shape[:-1], -1, P), -1, 0))

    def by_tile(q, k):
        both = np.concatenate([q, k], 1).reshape(CT, P, 4, P)
        return np.ascontiguousarray(both.transpose(1, 2, 0, 3).reshape(P, 4 * CT * P))

    head_sum = np.zeros((P, 3 * CT, 3 * HEADS), np.float32)
    for k in range(3 * CT):
        for p in range(P):
            head_sum[p, k, (k * P + p) // HD] = 1.0
    head_spread = np.zeros((P, 3 * CT, P), np.float32)
    head_spread[:3 * HEADS] = head_sum.transpose(2, 1, 0)
    var_rows, row_spread = np.zeros((P, NCH, 32), np.float32), np.zeros((32, NCH, P), np.float32)
    for c in range(NCH):
        var_rows[:, c, c] = 1.0 / C
        row_spread[c, c] = 1.0
    den_ones = np.zeros((P, QC, HD), np.float32)
    den_spread = np.zeros((P, QC, P), np.float32)
    for qc in range(QC):
        den_ones[:, qc, qc] = 1.0
        den_ones[:, :, QC:] = 1.0
        for b in range(2):
            for h in range(2):
                den_spread[64 * (1 - b) + h * HD + qc, qc, 64 * b + h * HD:64 * b + (h + 1) * HD] = 1.0
    qkv = a["L0_conv_w_qkv"].reshape(HEADS, 3, HD, C)
    q0, k0, v0 = (qkv[:, i].reshape(C, C).T for i in range(3))
    arrays = {
        "x": a["x"].reshape(B, C, N),
        "w_qk0": by_tile(q0, k0), "w_v0": tiled(v0),
        "w_proj": tiled(a["L0_conv_w_proj"].T), "L0_conv_b_proj": by_channel(a["L0_conv_b_proj"]),
        "L0_conv_w_lepe": tiled(a["L0_conv_w_lepe"].reshape(C, 9)), "L0_conv_b_lepe": by_channel(a["L0_conv_b_lepe"]),
        "w_r0": tiled(a["L0_ffn_Wr"]), "L0_ffn_br": a["L0_ffn_br"].reshape(1, E),
        "w_qk1": by_tile(a["L1_conv_Wq"].T, a["L1_conv_Wk"].T), "w_v1": tiled(a["L1_conv_Wv"].T),
        "w_out": tiled(a["L1_conv_Wout"].T), "L1_conv_bout": by_channel(a["L1_conv_bout"]),
        "w_r1": tiled(a["L1_ffn_router_w"].T),
        "var_rows": var_rows, "row_spread": row_spread, "den_ones": den_ones, "den_spread": den_spread,
        "masks": window_masks(np), "head_sum": head_sum, "head_spread": head_spread,
    }
    for name in ("L0_ffn_ln_g", "L0_ffn_ln_b", "L0_ffn_W1", "L0_ffn_b1", "L0_ffn_W2", "L0_ffn_b2",
                 "L1_ffn_w1", "L1_ffn_b1", "L1_ffn_w2", "L1_ffn_b2"):
        arrays[name] = by_channel(a[name]) if name.endswith(("ln_g", "ln_b", "b1")) else a[name]
    arrays = {k: np.ascontiguousarray(v) for k, v in arrays.items()}

    nc = bacc.Bacc("TRN2", target_bir_lowering=False, num_devices=1)
    ins = {k: nc.dram_tensor(f"in_{k}", v.shape, mybir.dt.from_np(v.dtype), kind="ExternalInput").ap()
           for k, v in arrays.items()}
    out = nc.dram_tensor("out", [B, C, N], F32, kind="ExternalOutput").ap()
    metaformer(nc, ins, out)
    r = run(nc, [{f"in_{k}": v for k, v in arrays.items()}], core_ids=[0])
    return r.results[0]["out"].reshape(B, C, HW, HW)
```
